# Optimizing a Trainium2 kernel written in Bass

```python
import numpy as np
import jax
import jax.numpy as jnp

def _softmax(x, axis=-1):
    return jax.nn.softmax(x, axis=axis)

def _gelu(x):
    return jax.nn.gelu(x, approximate=True)

def _silu(x):
    return jax.nn.silu(x)

def _sigmoid(x):
    return jax.nn.sigmoid(x)

def _layernorm(x, axis=-1, eps=1e-05):
    m = jnp.mean(x, axis=axis, keepdims=True)
    v = jnp.var(x, axis=axis, keepdims=True)
    return (x - m) / jnp.sqrt(v + eps)

def _scatter_add(tgt, idx, src, axis=0):
    return tgt.at[idx].add(src)

def _segment_sum(src, seg, n):
    return jax.ops.segment_sum(src, seg, n)
kernel_name = 'mk_cond_seq_d4_seqx_r8_1eba85'

def setup_inputs(seed: int=0):
    np.random.seed(seed)
    _w = jnp.asarray

    def _rec_inputs():
        import jax
        import jax.numpy as jnp
        _rk = jax.random.key(seed)
        x = 1.648e-05 + 1 * jax.random.normal(jax.random.fold_in(_rk, 1), (4, 256, 144), jnp.float32)
        _lenS = 256 - jax.random.randint(jax.random.fold_in(_rk, 7), (4,), 0, max(1, 256 // 4) + 1, jnp.int32)
        _lenS2 = 256 - jax.random.randint(jax.random.fold_in(_rk, 8), (4,), 0, max(1, 256 // 4) + 1, jnp.int32)
        cond_1152 = 0.00914911 + 1.00357 * jax.random.normal(jax.random.fold_in(_rk, 11), (4, 144), jnp.float32)
        return (x, cond_1152)
    x, cond_1152 = _rec_inputs()

    def _L0_cond_setup():
        import jax, jax.numpy as jnp
        import numpy as np
        B, L, C = (8, 128, 144)
        H = 16
        D = C // H
        FF = int(C * 4.0)
        EPS = 1e-06

        def _layernorm(x):
            mu = jnp.mean(x, axis=-1, keepdims=True)
            var = jnp.mean(jnp.square(x - mu), axis=-1, keepdims=True)
            return (x - mu) * jax.lax.rsqrt(var + EPS)

        def _modulate(x, shift, scale):
            return x * (1.0 + scale) + shift

        def _attention(h, W_qkv, b_qkv, W_proj, b_proj):
            b, l, c = h.shape
            qkv = h @ W_qkv + b_qkv
            qkv = qkv.reshape(b, l, 3, H, D)
            q, k, v = (qkv[:, :, 0], qkv[:, :, 1], qkv[:, :, 2])
            scale = D ** (-0.5)
            scores = jnp.einsum('blhd,bmhd->bhlm', q * scale, k)
            attn = jax.nn.softmax(scores, axis=-1)
            o = jnp.einsum('bhlm,bmhd->blhd', attn, v).reshape(b, l, c)
            return o @ W_proj + b_proj
        key = jax.random.key(seed)
        ks = jax.random.split(key, 12)
        s = 0.02
        return {'x': jax.random.normal(ks[0], (B, L, C), jnp.float32), 'c': jax.random.normal(ks[1], (B, 1, C), jnp.float32), 'W_qkv': jax.random.normal(ks[2], (C, 3 * C), jnp.float32) * s, 'b_qkv': jnp.zeros((3 * C,), jnp.float32), 'W_proj': jax.random.normal(ks[3], (C, C), jnp.float32) * s, 'b_proj': jnp.zeros((C,), jnp.float32), 'W_fc1': jax.random.normal(ks[4], (C, FF), jnp.float32) * s, 'b_fc1': jnp.zeros((FF,), jnp.float32), 'W_fc2': jax.random.normal(ks[5], (FF, C), jnp.float32) * s, 'b_fc2': jnp.zeros((C,), jnp.float32), 'W_ada': jax.random.normal(ks[6], (C, 6 * C), jnp.float32) * s, 'b_ada': jnp.zeros((6 * C,), jnp.float32)}
    _L0_cond_all = _L0_cond_setup()
    _L0_cond_in = {k: v for k, v in _L0_cond_all.items() if k in ('W_qkv', 'b_qkv', 'W_proj', 'b_proj', 'W_fc1', 'b_fc1', 'W_fc2', 'b_fc2', 'W_ada', 'b_ada')}
    del _L0_cond_all

    def _L1_cond_setup():
        import jax, jax.numpy as jnp
        import numpy as np
        NUM_HEADS = 16
        NUM_EXPERTS = 4
        TOP_K = 2
        LN_EPS = 1e-06

        def _ln(h):
            mu = jnp.mean(h, axis=-1, keepdims=True)
            var = jnp.var(h, axis=-1, keepdims=True)
            return (h - mu) * jax.lax.rsqrt(var + LN_EPS)

        def _modulate(h, shift, scale):
            return h * (1.0 + scale[:, None, :]) + shift[:, None, :]
        key = jax.random.key(seed)
        ks = jax.random.split(key, 12)
        B, N, C = (8, 128, 144)
        H = 4 * C
        E = NUM_EXPERTS
        s = 0.02
        return {'x': jax.random.normal(ks[0], (B, N, C), jnp.float32), 'c': jax.random.normal(ks[1], (B, C), jnp.float32), 'w_adaln': jax.random.normal(ks[2], (C, 6 * C), jnp.float32) * s, 'b_adaln': jnp.zeros((6 * C,), jnp.float32), 'w_qkv': jax.random.normal(ks[3], (C, 3 * C), jnp.float32) * s, 'b_qkv': jnp.zeros((3 * C,), jnp.float32), 'w_proj': jax.random.normal(ks[4], (C, C), jnp.float32) * s, 'b_proj': jnp.zeros((C,), jnp.float32), 'w_gate': jax.random.normal(ks[5], (C, E), jnp.float32) * s, 'w1': jax.random.normal(ks[6], (E, C, H), jnp.float32) * s, 'b1': jnp.zeros((E, H), jnp.float32), 'w2': jax.random.normal(ks[7], (E, H, C), jnp.float32) * s, 'b2': jnp.zeros((E, C), jnp.float32)}
    _L1_cond_all = _L1_cond_setup()
    _L1_cond_in = {k: v for k, v in _L1_cond_all.items() if k in ('w_adaln', 'b_adaln', 'w_qkv', 'b_qkv', 'w_proj', 'b_proj', 'w_gate', 'w1', 'b1', 'w2', 'b2')}
    del _L1_cond_all

    def _L2_cond_setup():
        import jax, jax.numpy as jnp
        import numpy as np
        H = 144
        NH = 16
        HD = H // NH
        MLP = int(H * 4.0)
        EPS = 1e-06

        def _ln(z, scale=None):
            m = jnp.mean(z, axis=-1, keepdims=True)
            v = jnp.mean(jnp.square(z - m), axis=-1, keepdims=True)
            y = (z - m) * jax.lax.rsqrt(v + EPS)
            if scale is not None:
                y = y * scale
            return y
        key = jax.random.key(seed)
        ks = jax.random.split(key, 16)
        B, N = (16, 128)
        x = jax.random.normal(ks[0], (B, N, H), dtype=jnp.float32)
        c = jax.random.normal(ks[1], (B, H), dtype=jnp.float32)

        def xav(k, fan_in, fan_out):
            lim = np.sqrt(6.0 / (fan_in + fan_out))
            return jax.random.uniform(k, (fan_in, fan_out), jnp.float32, -lim, lim)
        w_mod = 0.02 * jax.random.normal(ks[2], (H, 6 * H), dtype=jnp.float32)
        b_mod = 0.02 * jax.random.normal(ks[3], (6 * H,), dtype=jnp.float32)
        w_qkv = xav(ks[4], H, 3 * H)
        b_qkv = jnp.zeros((3 * H,), jnp.float32)
        g_q = jnp.ones((HD,), jnp.float32)
        g_k = jnp.ones((HD,), jnp.float32)
        w_proj = xav(ks[5], H, H)
        b_proj = jnp.zeros((H,), jnp.float32)
        w1 = xav(ks[6], H, MLP)
        b1 = jnp.zeros((MLP,), jnp.float32)
        w2 = xav(ks[7], MLP, H)
        b2 = jnp.zeros((H,), jnp.float32)
        return dict(x=x, c=c, w_mod=w_mod, b_mod=b_mod, w_qkv=w_qkv, b_qkv=b_qkv, g_q=g_q, g_k=g_k, w_proj=w_proj, b_proj=b_proj, w1=w1, b1=b1, w2=w2, b2=b2)
    _L2_cond_all = _L2_cond_setup()
    _L2_cond_in = {k: v for k, v in _L2_cond_all.items() if k in ('w_mod', 'b_mod', 'w_qkv', 'b_qkv', 'g_q', 'g_k', 'w_proj', 'b_proj', 'w1', 'b1', 'w2', 'b2')}
    del _L2_cond_all

    def _L3_cond_setup():
        import jax, jax.numpy as jnp
        import numpy as np
        from jax.scipy.linalg import expm
        N, D, COND_DIM = (144, 64, 144)
        B, T = (16, 128)

        def _rotation(cond, W, b):
            v = jax.nn.silu(cond) @ W.T + b
            iu, ju = jnp.triu_indices(D, k=1)
            A = jnp.zeros((cond.shape[0], D, D), dtype=v.dtype)
            A = A.at[:, iu, ju].set(v).at[:, ju, iu].set(-v)
            return expm(A)
        key = jax.random.key(seed)
        k1, k2, k3, k4, k5 = jax.random.split(key, 5)
        x = jax.random.normal(k1, (B, T, N), dtype=jnp.float32)
        cond = jax.random.normal(k2, (B, COND_DIM), dtype=jnp.float32)
        P = jax.random.normal(k3, (N, D), dtype=jnp.float32)
        n_skew = D * (D - 1) // 2
        bound = 1.0 / np.sqrt(COND_DIM)
        W = jax.random.uniform(k4, (n_skew, COND_DIM), minval=-bound, maxval=bound, dtype=jnp.float32)
        b = jax.random.uniform(k5, (n_skew,), minval=-bound, maxval=bound, dtype=jnp.float32)
        return {'x': x, 'cond': cond, 'P': P, 'W': W, 'b': b}
    _L3_cond_all = _L3_cond_setup()
    _L3_cond_in = {k: v for k, v in _L3_cond_all.items() if k in ('P', 'W', 'b')}
    del _L3_cond_all
    return {'x': x, 'cond_1152': cond_1152, 'L0_cond_W_qkv': _L0_cond_in['W_qkv'], 'L0_cond_b_qkv': _L0_cond_in['b_qkv'], 'L0_cond_W_proj': _L0_cond_in['W_proj'], 'L0_cond_b_proj': _L0_cond_in['b_proj'], 'L0_cond_W_fc1': _L0_cond_in['W_fc1'], 'L0_cond_b_fc1': _L0_cond_in['b_fc1'], 'L0_cond_W_fc2': _L0_cond_in['W_fc2'], 'L0_cond_b_fc2': _L0_cond_in['b_fc2'], 'L0_cond_W_ada': _L0_cond_in['W_ada'], 'L0_cond_b_ada': _L0_cond_in['b_ada'], 'L1_cond_w_adaln': _L1_cond_in['w_adaln'], 'L1_cond_b_adaln': _L1_cond_in['b_adaln'], 'L1_cond_w_qkv': _L1_cond_in['w_qkv'], 'L1_cond_b_qkv': _L1_cond_in['b_qkv'], 'L1_cond_w_proj': _L1_cond_in['w_proj'], 'L1_cond_b_proj': _L1_cond_in['b_proj'], 'L1_cond_w_gate': _L1_cond_in['w_gate'], 'L1_cond_w1': _L1_cond_in['w1'], 'L1_cond_b1': _L1_cond_in['b1'], 'L1_cond_w2': _L1_cond_in['w2'], 'L1_cond_b2': _L1_cond_in['b2'], 'L2_cond_w_mod': _L2_cond_in['w_mod'], 'L2_cond_b_mod': _L2_cond_in['b_mod'], 'L2_cond_w_qkv': _L2_cond_in['w_qkv'], 'L2_cond_b_qkv': _L2_cond_in['b_qkv'], 'L2_cond_g_q': _L2_cond_in['g_q'], 'L2_cond_g_k': _L2_cond_in['g_k'], 'L2_cond_w_proj': _L2_cond_in['w_proj'], 'L2_cond_b_proj': _L2_cond_in['b_proj'], 'L2_cond_w1': _L2_cond_in['w1'], 'L2_cond_b1': _L2_cond_in['b1'], 'L2_cond_w2': _L2_cond_in['w2'], 'L2_cond_b2': _L2_cond_in['b2'], 'L3_cond_P': _L3_cond_in['P'], 'L3_cond_W': _L3_cond_in['W'], 'L3_cond_b': _L3_cond_in['b']}

def reference(x, cond_1152, L0_cond_W_qkv, L0_cond_b_qkv, L0_cond_W_proj, L0_cond_b_proj, L0_cond_W_fc1, L0_cond_b_fc1, L0_cond_W_fc2, L0_cond_b_fc2, L0_cond_W_ada, L0_cond_b_ada, L1_cond_w_adaln, L1_cond_b_adaln, L1_cond_w_qkv, L1_cond_b_qkv, L1_cond_w_proj, L1_cond_b_proj, L1_cond_w_gate, L1_cond_w1, L1_cond_b1, L1_cond_w2, L1_cond_b2, L2_cond_w_mod, L2_cond_b_mod, L2_cond_w_qkv, L2_cond_b_qkv, L2_cond_g_q, L2_cond_g_k, L2_cond_w_proj, L2_cond_b_proj, L2_cond_w1, L2_cond_b1, L2_cond_w2, L2_cond_b2, L3_cond_P, L3_cond_W, L3_cond_b):
    import jax
    import jax.numpy as jnp

    def _L0_cond_ref(x, c, W_qkv, b_qkv, W_proj, b_proj, W_fc1, b_fc1, W_fc2, b_fc2, W_ada, b_ada):
        import jax, jax.numpy as jnp
        import numpy as np
        B, L, C = (8, 128, 144)
        H = 16
        D = C // H
        FF = int(C * 4.0)
        EPS = 1e-06

        def _layernorm(x):
            mu = jnp.mean(x, axis=-1, keepdims=True)
            var = jnp.mean(jnp.square(x - mu), axis=-1, keepdims=True)
            return (x - mu) * jax.lax.rsqrt(var + EPS)

        def _modulate(x, shift, scale):
            return x * (1.0 + scale) + shift

        def _attention(h, W_qkv, b_qkv, W_proj, b_proj):
            b, l, c = h.shape
            qkv = h @ W_qkv + b_qkv
            qkv = qkv.reshape(b, l, 3, H, D)
            q, k, v = (qkv[:, :, 0], qkv[:, :, 1], qkv[:, :, 2])
            scale = D ** (-0.5)
            scores = jnp.einsum('blhd,bmhd->bhlm', q * scale, k)
            attn = jax.nn.softmax(scores, axis=-1)
            o = jnp.einsum('bhlm,bmhd->blhd', attn, v).reshape(b, l, c)
            return o @ W_proj + b_proj
        ada = jax.nn.silu(c) @ W_ada + b_ada
        shift_msa, scale_msa, gate_msa, shift_mlp, scale_mlp, gate_mlp = jnp.split(ada, 6, axis=-1)
        h = _modulate(_layernorm(x), shift_msa, scale_msa)
        x = x + gate_msa * _attention(h, W_qkv, b_qkv, W_proj, b_proj)
        h = _modulate(_layernorm(x), shift_mlp, scale_mlp)
        mlp = jax.nn.gelu(h @ W_fc1 + b_fc1, approximate=True) @ W_fc2 + b_fc2
        x = x + gate_mlp * mlp
        return x

    def _L1_cond_ref(x, c, w_adaln, b_adaln, w_qkv, b_qkv, w_proj, b_proj, w_gate, w1, b1, w2, b2):
        import jax, jax.numpy as jnp
        import numpy as np
        NUM_HEADS = 16
        NUM_EXPERTS = 4
        TOP_K = 2
        LN_EPS = 1e-06

        def _ln(h):
            mu = jnp.mean(h, axis=-1, keepdims=True)
            var = jnp.var(h, axis=-1, keepdims=True)
            return (h - mu) * jax.lax.rsqrt(var + LN_EPS)

        def _modulate(h, shift, scale):
            return h * (1.0 + scale[:, None, :]) + shift[:, None, :]
        B, N, C = x.shape
        nh = NUM_HEADS
        hd = C // nh
        mod = jax.nn.silu(c) @ w_adaln + b_adaln
        sh_msa, sc_msa, g_msa, sh_mlp, sc_mlp, g_mlp = jnp.split(mod, 6, axis=-1)
        h = _modulate(_ln(x), sh_msa, sc_msa)
        qkv = (h @ w_qkv + b_qkv).reshape(B, N, 3, nh, hd).transpose(2, 0, 3, 1, 4)
        q, k, v = (qkv[0], qkv[1], qkv[2])
        attn = jax.nn.softmax(jnp.einsum('bhqd,bhkd->bhqk', q, k) * hd ** (-0.5), axis=-1)
        o = jnp.einsum('bhqk,bhkd->bhqd', attn, v).transpose(0, 2, 1, 3).reshape(B, N, C)
        o = o @ w_proj + b_proj
        x = x + g_msa[:, None, :] * o
        xn = _modulate(_ln(x), sh_mlp, sc_mlp)
        xf = xn.reshape(-1, C)
        gate_logits = xf @ w_gate
        topk_logits, topk_idx = jax.lax.top_k(gate_logits, TOP_K)
        gates = jax.nn.softmax(topk_logits, axis=-1)
        cw = jnp.sum(jax.nn.one_hot(topk_idx, NUM_EXPERTS, dtype=xf.dtype) * gates[..., None], axis=1)
        hmid = jax.nn.gelu(jnp.einsum('tc,ech->eth', xf, w1) + b1[:, None, :], approximate=True)
        eo = jnp.einsum('eth,ehc->etc', hmid, w2) + b2[:, None, :]
        moe = jnp.einsum('te,etc->tc', cw, eo).reshape(B, N, C)
        return x + g_mlp[:, None, :] * moe

    def _L2_cond_ref(x, c, w_mod, b_mod, w_qkv, b_qkv, g_q, g_k, w_proj, b_proj, w1, b1, w2, b2):
        import jax, jax.numpy as jnp
        import numpy as np
        H = 144
        NH = 16
        HD = H // NH
        MLP = int(H * 4.0)
        EPS = 1e-06

        def _ln(z, scale=None):
            m = jnp.mean(z, axis=-1, keepdims=True)
            v = jnp.mean(jnp.square(z - m), axis=-1, keepdims=True)
            y = (z - m) * jax.lax.rsqrt(v + EPS)
            if scale is not None:
                y = y * scale
            return y
        B, N, _ = x.shape
        mod = jax.nn.swish(c) @ w_mod + b_mod
        sh_msa, sc_msa, g_msa, sh_mlp, sc_mlp, g_mlp = jnp.split(mod, 6, axis=1)
        xn = _ln(x) * (1 + sc_msa[:, None, :]) + sh_msa[:, None, :]
        qkv = xn @ w_qkv + b_qkv
        qkv = qkv.reshape(B, N, 3, NH, HD).transpose(2, 0, 3, 1, 4)
        q, k, v = (qkv[0], qkv[1], qkv[2])
        q = _ln(q, g_q)
        k = _ln(k, g_k)
        attn = jax.nn.softmax(jnp.einsum('bhqd,bhkd->bhqk', q, k) * HD ** (-0.5), axis=-1)
        o = jnp.einsum('bhqk,bhkd->bhqd', attn, v)
        o = o.transpose(0, 2, 1, 3).reshape(B, N, H) @ w_proj + b_proj
        x = x + g_msa[:, None, :] * o
        xn2 = _ln(x) * (1 + sc_mlp[:, None, :]) + sh_mlp[:, None, :]
        h = jax.nn.gelu(xn2 @ w1 + b1, approximate=True)
        x = x + g_mlp[:, None, :] * (h @ w2 + b2)
        return x

    def _L3_cond_ref(x, cond, P, W, b):
        import jax, jax.numpy as jnp
        import numpy as np
        from jax.scipy.linalg import expm
        N, D, COND_DIM = (144, 64, 144)
        B, T = (16, 128)

        def _rotation(cond, W, b):
            v = jax.nn.silu(cond) @ W.T + b
            iu, ju = jnp.triu_indices(D, k=1)
            A = jnp.zeros((cond.shape[0], D, D), dtype=v.dtype)
            A = A.at[:, iu, ju].set(v).at[:, ju, iu].set(-v)
            return expm(A)
        U, _ = jnp.linalg.qr(P)
        R = _rotation(cond, W, b)
        z = jnp.einsum('btn,nd->btd', x, U)
        z_rot = jnp.einsum('btd,bde->bte', z, R)
        x_rot = x + jnp.einsum('btd,nd->btn', z_rot - z, U)
        return x_rot
    x = _L0_cond_ref(x, cond_1152[:, None, :], L0_cond_W_qkv, L0_cond_b_qkv, L0_cond_W_proj, L0_cond_b_proj, L0_cond_W_fc1, L0_cond_b_fc1, L0_cond_W_fc2, L0_cond_b_fc2, L0_cond_W_ada, L0_cond_b_ada)
    x = _L1_cond_ref(x, cond_1152, L1_cond_w_adaln, L1_cond_b_adaln, L1_cond_w_qkv, L1_cond_b_qkv, L1_cond_w_proj, L1_cond_b_proj, L1_cond_w_gate, L1_cond_w1, L1_cond_b1, L1_cond_w2, L1_cond_b2)
    x = _L2_cond_ref(x, cond_1152, L2_cond_w_mod, L2_cond_b_mod, L2_cond_w_qkv, L2_cond_b_qkv, L2_cond_g_q, L2_cond_g_k, L2_cond_w_proj, L2_cond_b_proj, L2_cond_w1, L2_cond_b1, L2_cond_w2, L2_cond_b2)
    x = _L3_cond_ref(x, cond_1152, L3_cond_P, L3_cond_W, L3_cond_b)
    return x

_drawn_inputs = setup_inputs


def setup_inputs(seed=0):
    import zlib

    import numpy as np

    out = dict(_drawn_inputs(seed))
    spreads = {'L0_cond_b_qkv': (0.0, 0.8),
     'L0_cond_b_proj': (0.0, 0.498),
     'L0_cond_b_fc1': (0.0, 0.8),
     'L0_cond_b_fc2': (0.0, 0.461),
     'L0_cond_b_ada': (0.0, 0.493),
     'L1_cond_b_adaln': (0.0, 0.556),
     'L1_cond_b_qkv': (0.0, 0.8),
     'L1_cond_b_proj': (0.0, 0.449),
     'L1_cond_b1': (0.0, 0.8),
     'L1_cond_b2': (0.0, 0.645),
     'L2_cond_b_qkv': (0.0, 2.0),
     'L2_cond_g_q': (1.0, 0.6),
     'L2_cond_g_k': (1.0, 0.6),
     'L2_cond_b_proj': (0.0, 2.0),
     'L2_cond_b1': (0.0, 2.0),
     'L2_cond_b2': (0.0, 2.0)}
    factors = {'L0_cond_W_qkv': 8.0,
     'L0_cond_W_proj': 8.0,
     'L0_cond_W_fc1': 5.186,
     'L0_cond_W_fc2': 4.82,
     'L1_cond_w_adaln': 3.035,
     'L1_cond_w_qkv': 8.0,
     'L1_cond_w_proj': 8.0,
     'L1_cond_w_gate': 5.509,
     'L1_cond_w1': 7.353,
     'L1_cond_w2': 6.855,
     'L2_cond_b_mod': 5.205,
     'L2_cond_w_qkv': 3.092,
     'L2_cond_w1': 2.924}
    for name, (base, spread) in spreads.items():
        noise = np.random.default_rng([zlib.crc32(name.encode()), seed]).standard_normal(out[name].shape)
        drawn = base * np.exp(spread * noise) if base else spread * noise
        out[name] = jnp.asarray(drawn.astype(out[name].dtype))
    for name, factor in factors.items():
        out[name] = (out[name] * factor).astype(out[name].dtype)
    return out
```

```python
import concourse.bass as bass
from concourse import mybir
from contextlib import ExitStack


def cond_sequence_kernel(nc, t, out):
    F32 = mybir.dt.float32
    BF16 = mybir.dt.bfloat16
    U32 = mybir.dt.uint32
    ALU = mybir.AluOpType
    ACT = mybir.ActivationFunctionType
    AX = mybir.AxisListType

    B, T, C = 4, 256, 144
    P = 128
    NT = T // P
    CR = C - P
    H, HD = 16, 9
    FF = 4 * C
    FC = FF // P
    FR = FF - FC * P
    NL, NU = 3, 12
    NE = 4
    EXPERTS = [1, NE, 1]
    EPS = 1e-6
    SCALE = float(HD) ** -0.5
    DR = 64
    NSK = DR * (DR - 1) // 2
    SLOTS = 6
    KS_ROWS = SLOTS * HD
    CH = [96, 96, 72]
    NCH = [2 * C // c for c in CH]
    QKJ = [[(0, 2), (2, 3)], [(0, 2), (2, 3)], [(0, 2), (2, 4)]]
    TAYLOR = 10
    SQUARINGS = 16

    def hidden_chunks(L):
        E = EXPERTS[L]
        groups = []
        for e in range(E):
            groups += [[(e, c, P) for c in range(FC)], [(e, FC, FR)]]
        return groups

    def experts_before(u):
        return sum(EXPERTS[k // B] for k in range(u))

    ND, NA = 3, 2
    d_order = [("ada", L) for L in range(NL)] + [("gate", L, b) for L in range(NL) for b in range(B)]

    def prep_jobs(u):
        L = u // B
        jobs = [("t1", u)] + [("qk", u, j) for j in range(2)]
        if L == 2:
            jobs += [("var", u), ("rs", u, 0), ("rs", u, 1)]
        return jobs + [("v", u)]

    def mlp_jobs(u):
        L = u // B
        return [("t3", u)] + ([("gl", u)] if L == 1 else []) + [("fc2", u, e) for e in range(EXPERTS[L])]

    d_order += prep_jobs(0) + [("s", 0, h) for h in range(H)] + [("nm", 0)] + prep_jobs(1)
    for u in range(NU):
        if u + 1 < NU:
            d_order += [("s", u + 1, h) for h in range(H)]
        d_order += [("t2", u)]
        if u + 1 < NU:
            d_order += [("nm", u + 1)]
        d_order += [("proj", u)]
        if u + 2 < NU:
            d_order += prep_jobs(u + 2)
        d_order += mlp_jobs(u)
    d_order += [("wt", k) for k in range(8)] + [("vv", k) for k in range(4)] + [("ut",), ("fro",)]
    d_order += [("tay", k) for k in range(TAYLOR - 1)] + [("ft",)] + [("sq", k) for k in range(SQUARINGS)]
    d_order += [("pt",)] + [("qr", j) for j in range(DR)] + [("vqt",), ("vvt",)]
    d_order += [(s, k) for k in range(5) for s in ("nn", "tn")] + [("kk",), ("uu",)]
    d_order += [("gm", k) for k in range(2)] + [("m", b) for b in range(B)]
    d_order += [job for b in range(B) for job in (("t4", b), ("y", b))]
    LN_ORDER = [(1, 0), (1, 1)]
    for u in range(NU):
        LN_ORDER += ([(1, u + 2)] if u + 2 < NU else []) + [(2, u)]
    CONSTS = 14 + SQUARINGS
    W_IN = [16 * (6 + 6 * EXPERTS[L] + (0, 2, 16)[L]) for L in range(NL)]
    d_no = {name: n for n, name in enumerate(d_order)}

    a_order = []
    for u in range(NU):
        a_order += [("e", u, g) for g in range(H // 2)]
        a_order += [("g", u, k) for k in range(len(hidden_chunks(u // B)))]
    a_no = {name: n for n, name in enumerate(a_order)}

    ctx = ExitStack()
    with ctx:
        def sb(name, shape, dt=F32):
            return ctx.enter_context(nc.sbuf_tensor(name, shape, dt))

        def sem(name):
            return ctx.enter_context(nc.semaphore(name))

        x = sb("x", [P, B, NT, C])
        xh = sb("xh", [P, NT, C])
        stats = sb("stats", [P, NT, 6])
        mv = sb("mv", [P, NT, 2])
        ve = sb("ve", [P, NT])
        rstd = sb("rstd", [P, NT])
        mhalf = sb("mhalf", [P, 1])
        phalf = sb("phalf", [P, 1])
        hT = sb("hT", [P, T])
        hTr = sb("hTr", [CR + 1, T])
        h2T = sb("h2T", [P, T])
        h2Tr = sb("h2Tr", [CR + 1, T])
        oT = sb("oT", [P, T])
        oTr = sb("oTr", [CR + 1, T])
        on = sb("on", [P, NT, C])
        rden = sb("rden", [P, NT * H])
        parts = sb("parts", [96, 3, 4, T], BF16)
        r1 = sb("r1", [96, 4, T])
        qsq = sb("qsq", [72, 4, T])
        qn = r1[0:72]
        qve = sb("qve", [P, T])
        qrs = sb("qrs", [P, T])
        pick = sb("pick", [72, 32])
        spread = sb("spread", [P, 4, 8, HD])
        QS = [sb(f"QS{i}", [KS_ROWS + 1, H, T], BF16) for i in range(2)]
        KS = [sb(f"KS{i}", [KS_ROWS + 1, H, T], BF16) for i in range(2)]
        V = [sb(f"V{i}", [P, NT, H, HD + 1]) for i in range(2)]
        nm = [sb(f"nm{i}", [P, NT, H], BF16) for i in range(2)]
        nmT = sb("nmT", [H, T], BF16)
        NPT = 3
        PT = sb("PT", [P, NPT, 4, T])
        G = sb("G", [P, 2, FC + 1, T])
        tmp = sb("tmp", [P, NT, C])
        acc = sb("acc", [P, NT, C])
        lraw = sb("lraw", [P, NT, NE])
        lg = sb("lg", [P, NT, NE])
        lgm = sb("lgm", [P, NT])
        lge = sb("lge", [P, NT, NE])
        cmpt = sb("cmpt", [P, NT, NE, NE])
        rank = sb("rank", [P, NT, NE])
        cwt = sb("cwt", [P, NT, NE])
        den = sb("den", [P, NT])
        cw = sb("cw", [P, NT, NE])
        cT = sb("cT", [P, B])
        cTr = sb("cTr", [CR, B])
        sT = sb("sT", [P, B])
        sTr = sb("sTr", [CR + 1, B])
        ee = sb("ee", [P, B])
        eer = sb("eer", [CR, B])
        sTb = PT[:, 0, 0:2, :].rearrange("p k t -> p (k t)").rearrange("p (b q) -> p b q", b=B)
        sTrb = PT[0:CR + 1, 1, 0:2, :].rearrange("p k t -> p (k t)").rearrange("p (b q) -> p b q", b=B)
        mod = sb("mod", [P, NL, 6, B])
        modr = sb("modr", [CR, NL, 6, B])
        gates = sb("gates", [P, NL, B, 2, C])
        ident = sb("ident", [P, P])
        identb = sb("identb", [P, P], BF16)
        Wada = sb("Wada", [P, NL, 6 * C])
        Wadar = sb("Wadar", [CR + 1, NL, 6 * C])
        Wqkv = sb("Wqkv", [P, NL, 3 * C])
        Wqkvr = sb("Wqkvr", [CR + 1, NL, 3 * C])
        gm = sb("gm", [P, 2 * H])
        gmr = sb("gmr", [CR + 1, 2 * H])
        Wp = sb("Wp", [P, NL, C])
        Wpr = sb("Wpr", [CR + 1, NL, C])
        W1 = [sb(f"W1_{L}", [P, EXPERTS[L], FF]) for L in range(NL)]
        W1r = [sb(f"W1r_{L}", [CR + 1, EXPERTS[L], FF]) for L in range(NL)]
        W2 = [sb(f"W2_{L}", [P, EXPERTS[L], FC + 1, C]) for L in range(NL)]
        Wg = sb("Wg", [P, NE])
        Wgr = sb("Wgr", [CR, NE])
        gq = sb("gq", [72, 2])
        Wl = W1[1][0:126, :, :].rearrange("p e f -> p (e f)").rearrange("p (t c) -> p t c", t=16)
        WT = Wada[:, :, :].rearrange("p l n -> p (l n)")[:, 0:NSK]
        WTr = Wadar[:, :, :].rearrange("p l n -> p (l n)")[:, 0:NSK]
        vs = sb("vs", [B, NSK])
        Up = sb("Up", [DR, B, DR])
        Ask = sb("Ask", [DR, B, DR])
        fr = sb("fr", [DR, B])
        frb = sb("frb", [DR, B])
        thr = sb("thr", [DR, SQUARINGS])
        need = sb("need", [DR, B, SQUARINGS])
        needu = sb("needu", [DR, SQUARINGS, 2, B], U32)
        fac = sb("fac", [DR, B, SQUARINGS])
        X = sb("X", [DR, B, DR])
        E0 = sb("E0", [DR, B, DR])
        Asq = E0
        Z = sb("Z", [DR, 2 * B, DR])
        ones = sb("ones", [DR, DR])
        Pt = sb("Pt", [DR, C])
        Pn = sb("Pn", [P, DR])
        Pnr = sb("Pnr", [CR, DR])
        Vq = sb("Vq", [DR, C])
        vb = sb("vb", [DR, C])
        junk = sb("junk", [DR, C])
        junk2 = sb("junk2", [DR, C])
        qsc = sb("qsc", [DR, 8])
        Nn = sb("Nn", [DR, 2, DR])
        Tn = sb("Tn", [DR, DR])
        VqT = sb("VqT", [P, DR])
        VqTr = sb("VqTr", [CR, DR])
        Kq = sb("Kq", [DR, C])
        Ut = sb("Ut", [DR, C])
        FmI = sb("FmI", [DR, B, DR])
        Gm = sb("Gm", [DR, B, C])
        M = Wqkv[:, :, :].rearrange("p l n -> p (l n)")[:, 0:B * C].rearrange("p (b c) -> p b c", b=B)
        Mr = Wqkvr[0:CR, :, :].rearrange("p l n -> p (l n)")[:, 0:B * C].rearrange("p (b c) -> p b c", b=B)
        xT, xTr = hT, hTr[0:CR]
        y = G[:, :, :, :].rearrange("p e c t -> p (e c t)")[:, 0:B * NT * C].rearrange("p (b n c) -> p b n c", b=B, n=NT)

        scr = nc.dram_tensor("parts_scratch", (2, 3, 2 * C, T), BF16).ap()
        nmscr = nc.dram_tensor("maxima_scratch", (2, H, T), BF16).ap()
        vscr = nc.dram_tensor("skew_scratch", (B, NSK), F32).ap()

        A_ring = [ctx.enter_context(nc.psum_tensor(f"A{i}", [P, 4, T], F32)) for i in range(NA)]
        D_ring = [ctx.enter_context(nc.psum_tensor(f"D{i}", [P, 512], F32)) for i in range(ND)]
        O = ctx.enter_context(nc.psum_tensor("O", [P, NT, H, 16], F32))

        d_full = [sem(f"d_full{i}") for i in range(ND)]
        d_free = [sem(f"d_free{i}") for i in range(ND)]
        a_full = [sem(f"a_full{i}") for i in range(NA)]
        a_free = [sem(f"a_free{i}") for i in range(NA)]
        consts = sem("consts")
        nm_out = [sem(f"nm_out{i}") for i in range(2)]
        mixed = sem("mixed")
        F_done = sem("F_done")
        var_done = sem("var_done")
        rstd_done = sem("rstd_done")
        qrs_done = sem("qrs_done")
        norm_done = sem("norm_done")
        vn_done = sem("vn_done")
        vg_done = sem("vg_done")
        x_in = sem("x_in")
        c_in = sem("c_in")
        w_in = [sem(f"w_in{L}") for L in range(NL)]
        ada_in = sem("ada_in")
        l3_in = sem("l3_in")
        pt_in = sem("pt_in")
        silu_done = sem("silu_done")
        centred = sem("centred")
        xh_ready = sem("xh_ready")
        p1_done = sem("p1_done")
        p2_done = sem("p2_done")
        r1_done = sem("r1_done")
        p3_done = sem("p3_done")
        sq_done = sem("sq_done")
        parts_out = [sem(f"parts_out{i}") for i in range(2)]
        stk_in = [sem(f"stk_in{i}") for i in range(2)]
        nm_in = [sem(f"nm_in{i}") for i in range(2)]
        on_done = sem("on_done")
        x_new = sem("x_new")
        lgm_done = sem("lgm_done")
        lge_done = sem("lge_done")
        dchain = sem("dchain")
        achain = sem("achain")
        pchain = sem("pchain")
        tri_done = sem("tri_done")
        pv_step = sem("pv_step")
        v_out = sem("v_out")
        up_zero = sem("up_zero")
        up_in = sem("up_in")
        X_done = sem("X_done")
        fr_done = sem("fr_done")
        E_done = sem("E_done")
        sig_done = sem("sig_done")
        qr_done = sem("qr_done")
        N_done = sem("N_done")
        y_out = sem("y_out")

        def slot(name):
            if name in a_no:
                return a_no[name] % NA, a_no[name] // NA, a_full, a_free
            return d_no[name] % ND, d_no[name] // ND, d_full, d_free

        def D(name):
            return D_ring[d_no[name] % ND]

        def A(name):
            return A_ring[a_no[name] % NA]

        def written(eng, name):
            i, turn, full, _ = slot(name)
            eng.wait_ge(full[i], turn + 1)

        def used(eng, name):
            i, turn, _, free = slot(name)
            eng.wait_ge(free[i], turn + 1)

        def release(ins, name):
            i, _, _, free = slot(name)
            return ins.then_inc(free[i], 1)

        def hidden_jobs(u):
            return [("g", u, k) for k in range(len(hidden_chunks(u // B)))]

        def fc2_job(n):
            for u in range(NU):
                if n < EXPERTS[u // B]:
                    return ("fc2", u, n)
                n -= EXPERTS[u // B]

        def remainder(eng, u, j):
            if u // B == 2:
                eng.wait_ge(r1_done, 2 * (u - 2 * B) + j + 1)
            else:
                used(eng, ("qk", u, j))

        def norm_job(n):
            kind, u = LN_ORDER[n]
            return ("t1" if kind == 1 else "t3", u)

        block = ctx.enter_context(nc.Block())

        @block.sync
        def _(sp):
            sp.dma_start(cT[:, :], t["cond"][:, 0:P].rearrange("b c -> c b"), allow_slow_non_contiguous=True).then_inc(c_in, 16)
            sp.dma_start(cTr[:, :], t["cond"][:, P:C].rearrange("b c -> c b"), allow_slow_non_contiguous=True).then_inc(c_in, 16)
            for b in range(B):
                sp.dma_start(x[:, b, :, :], t["x"][b].rearrange("(n p) c -> p n c", p=P)).then_inc(x_in, 16)
            for L in range(NL):
                sp.dma_start(Wada[:, L, :], t["ada"][L][0:P, :]).then_inc(ada_in, 16)
                sp.dma_start(Wadar[0:CR, L, :], t["ada"][L][P:C, :]).then_inc(ada_in, 16)
                sp.dma_start(Wadar[CR:CR + 1, L, :], t["b_ada"][L].unsqueeze(0)).then_inc(ada_in, 16)

            def load(L, dst, src):
                sp.dma_start(dst, src).then_inc(w_in[L], 16)

            for L in range(NL):
                load(L, Wqkv[:, L, :], t["qkv"][L][0:P, :])
                load(L, Wqkvr[0:CR, L, :], t["qkv"][L][P:C, :])
                load(L, Wqkvr[CR:CR + 1, L, :], t["b_qkv"][L].unsqueeze(0))
                load(L, Wp[:, L, :], t["proj"][L][0:P, :])
                load(L, Wpr[0:CR, L, :], t["proj"][L][P:C, :])
                load(L, Wpr[CR:CR + 1, L, :], t["b_proj"][L].unsqueeze(0))
                if L == 1:
                    load(L, Wg[:, :], t["w_gate"][0:P, :])
                    load(L, Wgr[:, :], t["w_gate"][P:C, :])
                if L == 2:
                    for s, g in enumerate(("g_q", "g_k")):
                        for k in range(8):
                            load(L, gq[HD * k:HD * k + HD, s:s + 1], t[g].unsqueeze(1))
                for e in range(EXPERTS[L]):
                    load(L, W1[L][:, e, :], t["w1"][L][e][0:P, :])
                    load(L, W1r[L][0:CR, e, :], t["w1"][L][e][P:C, :])
                    load(L, W1r[L][CR:CR + 1, e, :], t["b1"][L][e].unsqueeze(0))
                    load(L, W2[L][:, e, 0:FC, :], t["w2"][L][e][0:FC * P, :].rearrange("(c p) n -> p c n", p=P))
                    load(L, W2[L][0:FR, e, FC, :], t["w2"][L][e][FC * P:FF, :])
                    load(L, W2[L][FR:FR + 1, e, FC, :], t["b2"][L][e].unsqueeze(0))

            def prep(u):
                L, i = u // B, u % 2
                sp.wait_ge(p1_done, 2 * u + 2)
                sp.wait_ge(p2_done, 2 * u + 2)
                sp.wait_ge(p3_done, 2 * u + 2)
                if u >= 2:
                    sp.wait_ge(stk_in[i], 16 * 2 * SLOTS * (u // 2))
                for p in range(3):
                    sp.dma_start(scr[i, p].rearrange("(k r) t -> r k t", r=CH[L]),
                                 parts[0:CH[L], p, 0:NCH[L], :]).then_inc(parts_out[i], 16)
                sp.wait_ge(parts_out[i], 16 * 3 * (u // 2 + 1))
                if u >= 2:
                    written(sp, ("e", u - 2, H // 2 - 1))
                for s, (dst, first) in enumerate(((QS[i], True), (KS[i], False))):
                    src = scr[i, :, s * C:(s + 1) * C, :].rearrange("p (h r) t -> p r h t", r=HD)
                    for slot in range(SLOTS):
                        part = ((0, 0, 1, 1, 2, 0), (0, 1, 0, 1, 0, 2))[s][slot]
                        sp.dma_start(dst[HD * slot:HD * slot + HD, :, :], src[part]).then_inc(stk_in[i], 16)

            def maxima(u):
                i = u % 2
                used(sp, ("nm", u))
                if u >= 2:
                    written(sp, ("e", u - 2, H // 2 - 1))
                sp.dma_start(nmscr[i], nmT[:, :]).then_inc(nm_out[i], 16)
                sp.wait_ge(nm_out[i], 16 * (u // 2 + 1))
                sp.dma_start(QS[i][KS_ROWS:KS_ROWS + 1, :, :], nmscr[i].unsqueeze(0)).then_inc(nm_in[i], 16)

            sp.wait_ge(consts, CONSTS)
            prep(0)
            maxima(0)
            prep(1)
            for u in range(NU):
                if u + 1 < NU:
                    maxima(u + 1)
                if u + 2 < NU:
                    prep(u + 2)
            written(sp, ("fc2", 2 * B - 1, NE - 1))
            written(sp, ("gate", NL - 1, B - 1))
            sp.dma_start(Wl, t["rot_w"].rearrange("(p t) c -> p t c", t=16)).then_inc(l3_in, 16)
            sp.dma_start(WTr[CR:CR + 1, :], t["rot_b"].unsqueeze(0)).then_inc(l3_in, 16)
            sp.dma_start(Pn[:, :], t["rot_p"][0:P, :]).then_inc(pt_in, 16)
            sp.dma_start(Pnr[:, :], t["rot_p"][P:C, :]).then_inc(pt_in, 16)
            used(sp, ("vv", 3))
            sp.dma_start(vscr, vs[:, :]).then_inc(v_out, 16)
            sp.wait_ge(v_out, 16)
            sp.wait_ge(up_zero, 1)
            at = 0
            for r in range(DR - 1):
                n = DR - 1 - r
                sp.dma_start(Up[r:r + 1, :, r + 1:DR], vscr[:, at:at + n].unsqueeze(0),
                             allow_slow_non_contiguous=True).then_inc(up_in, 16)
                at += n
            for b in range(B):
                used(sp, ("y", b))
                sp.dma_start(out[b].rearrange("(n p) c -> p n c", p=P), y[:, b, :, :]).then_inc(y_out, 16)
            sp.wait_ge(y_out, 16 * B)

        @block.gpsimd
        def _(pool):
            count = [0]

            def link(ins):
                count[0] += 1
                ins.then_inc(pchain, 1)
                pool.wait_ge(pchain, count[0])

            link(nc.gpsimd.memset(ident[:, :], 0.0))
            link(nc.gpsimd.affine_select(out=ident[:, :], in_=ident[:, :], compare_op=ALU.not_equal, fill=1.0,
                                         base=0, pattern=[[-1, P]], channel_multiplier=1))
            nc.gpsimd.tensor_copy(identb[:, :], ident[:, :]).then_inc(consts, 1)
            link(nc.gpsimd.memset(pick[:, :], 1.0 / HD))
            link(nc.gpsimd.affine_select(out=pick[:, :], in_=pick[:, :], compare_op=ALU.is_ge, fill=0.0,
                                         base=0, pattern=[[-HD, 32]], channel_multiplier=1))
            nc.gpsimd.affine_select(out=pick[:, :], in_=pick[:, :], compare_op=ALU.is_ge, fill=0.0,
                                    base=HD - 1, pattern=[[HD, 32]], channel_multiplier=-1).then_inc(consts, 1)
            link(nc.gpsimd.memset(spread[:, :, :, :], 0.0))
            link(nc.gpsimd.affine_select(out=spread[:, :, :, :], in_=spread[:, :, :, :], compare_op=ALU.not_equal,
                                         fill=1.0, base=0, pattern=[[-32, 4], [-1, 8], [0, HD]],
                                         channel_multiplier=1))
            nc.gpsimd.memset(mhalf[:, :], -0.5).then_inc(consts, 1)
            nc.gpsimd.memset(phalf[:, :], 0.5).then_inc(consts, 1)
            for tile in (hTr, h2Tr, oTr):
                nc.gpsimd.memset(tile[:, :], 1.0).then_inc(consts, 1)
            nc.gpsimd.memset(sTr[:, :], 1.0).then_inc(consts, 1)
            for i in range(2):
                nc.gpsimd.memset(V[i][:, :, :, :], 1.0).then_inc(consts, 1)
            nc.gpsimd.memset(ones[:, :], 1.0).then_inc(consts, 1)
            for k in range(SQUARINGS):
                nc.gpsimd.memset(thr[:, k:k + 1], 2.0 * 4.0 ** k).then_inc(consts, 1)
            nc.gpsimd.memset(Up[:, :, :], 0.0).then_inc(up_zero, 1)
            nc.gpsimd.memset(Vq[:, :], 0.0).then_inc(up_zero, 1)

            def deviation(n):
                pool.wait_ge(var_done, n + 1)
                if n >= 1:
                    pool.wait_ge(xh_ready, NT * n)
                nc.gpsimd.tensor_tensor(rstd[:, :], ve[:, :], mhalf[:, :].to_broadcast([P, NT]),
                                        ALU.pow).then_inc(rstd_done, 1)

            def prep(u):
                L = u // B
                deviation(LN_ORDER.index((1, u)))
                if L == 2:
                    used(pool, ("var", u))
                    if u > 2 * B:
                        written(pool, ("rs", u - 1, 1))
                    nc.gpsimd.tensor_tensor(qrs[:, :], qve[:, :], mhalf[:, :].to_broadcast([P, T]),
                                            ALU.pow).then_inc(qrs_done, 1)
                for j, (a, b) in enumerate(QKJ[L]):
                    pool.wait_ge(p2_done, 2 * u + j + 1)
                    remainder(pool, u, j)
                    nc.gpsimd.tensor_tensor(parts[0:CH[L], 2, a:b, :], r1[0:CH[L], a:b, :],
                                            parts[0:CH[L], 1, a:b, :], ALU.subtract).then_inc(p3_done, 1)

            def residual(n):
                u, b = n // 2, (n // 2) % B
                if n % 2 == 0:
                    used(pool, ("proj", u))
                elif u // B == 1:
                    pool.wait_ge(mixed, b + 1)
                else:
                    used(pool, ("fc2", u, 0))
                nc.gpsimd.tensor_tensor(x[:, b, :, :], x[:, b, :, :], tmp[:, :, :], ALU.add).then_inc(x_new, 1)

            prep(0)
            prep(1)
            for u in range(NU):
                residual(2 * u)
                if u + 2 < NU:
                    prep(u + 2)
                deviation(LN_ORDER.index((2, u)))
                residual(2 * u + 1)
            for j in range(DR):
                pool.wait_ge(sig_done, j + 1)
                if j >= 1:
                    pool.wait_ge(qr_done, j)
                nc.gpsimd.tensor_tensor(qsc[:, 1:2], qsc[:, 0:1], phalf[0:DR, :], ALU.pow).then_inc(norm_done, 1)
            pool.wait_ge(vn_done, 1)
            nc.gpsimd.tensor_tensor(qsc[:, 6:7], qsc[:, 7:8], mhalf[0:DR, :], ALU.pow).then_inc(vg_done, 1)
            for s, sign in ((0, 1), (1, -1)):
                used(pool, ("vvt",))
                nc.gpsimd.affine_select(out=Nn[:, s, :], in_=Nn[:, s, :], compare_op=ALU.is_gt, fill=0.0, base=0,
                                        pattern=[[sign, DR]], channel_multiplier=-sign).then_inc(tri_done, 1)

        @block.scalar
        def _(act):
            act.wait_ge(c_in, 32)
            nc.scalar.activation(ee[:, :], cT[:, :], ACT.Exp, scale=-1.0).then_inc(achain, 1)
            nc.scalar.activation(eer[:, :], cTr[:, :], ACT.Exp, scale=-1.0).then_inc(achain, 1)

            def prep(u):
                L, i, b = u // B, u % 2, u % B
                written(act, ("t1", u))
                if u >= 1:
                    written(act, ("v", u - 1))
                nc.scalar.activation(hT[:, :], D(("t1", u))[:, 0:T], ACT.Identity,
                                     scale=mod[:, L, 1, b:b + 1], bias=mod[:, L, 0, b:b + 1])
                release(nc.scalar.activation(hTr[0:CR, :], D(("t1", u))[0:CR, T:2 * T], ACT.Identity,
                                               scale=modr[:, L, 1, b:b + 1], bias=modr[:, L, 0, b:b + 1]),
                          ("t1", u))
                c = CH[L]
                if L < 2:
                    if u >= 1:
                        act.wait_ge(parts_out[(u - 1) % 2], 16 * 3 * ((u - 1) // 2 + 1))
                    for j, (lo, hi) in enumerate(QKJ[L]):
                        name = ("qk", u, j)
                        written(act, name)
                        nc.scalar.copy(parts[0:c, 0, lo:hi, :],
                                       D(name)[0:c, 0:(hi - lo) * T].rearrange("p (k t) -> p k t", t=T)).then_inc(p1_done, 1)
                else:
                    for j, (lo, hi) in enumerate(QKJ[L]):
                        name = ("qk", u, j)
                        written(act, name)
                        if u > 2 * B:
                            written(act, ("var", u - 1))
                        src = D(name)[0:c, :].rearrange("p (k t) -> p k t", t=T)
                        nc.scalar.activation(qsq[:, lo:hi, :], src, ACT.Square).then_inc(sq_done, 1)
                        act.wait_ge(p3_done, 2 * u)
                        release(nc.scalar.activation(qn[:, lo:hi, :], src, ACT.Copy, scale=gq[:, j:j + 1]), name)
                    act.wait_ge(parts_out[(u - 1) % 2], 16 * 3 * ((u - 1) // 2 + 1))
                    for j, (lo, hi) in enumerate(QKJ[L]):
                        used(act, ("rs", u, j))
                        nc.scalar.copy(parts[0:c, 0, lo:hi, :], qn[:, lo:hi, :]).then_inc(p1_done, 1)
                name = ("v", u)
                written(act, name)
                if u >= 2:
                    act.wait_ge(pv_step, 8 * (u - 1))
                release(nc.scalar.copy(V[i][:, :, :, 0:HD],
                                         D(name)[:, 0:NT * C].rearrange("p (n h r) -> p n h r", n=NT, h=H)),
                          name)

            def maxima(u):
                name = ("nm", u)
                written(act, name)
                if u >= 1:
                    act.wait_ge(nm_out[(u - 1) % 2], 16 * ((u - 1) // 2 + 1))
                release(nc.scalar.copy(nmT[:, :], D(name)[:, :].bitcast(BF16)[0:H, 0:T]), name)

            used(act, ("ada", NL - 1))
            act.wait_ge(consts, CONSTS)
            prep(0)
            maxima(0)
            prep(1)
            written(act, ("gate", NL - 1, B - 1))
            for u in range(NU):
                L, b = u // B, u % B
                for g in range(H // 2):
                    name = ("e", u, g)
                    n = 8 * u + g
                    written(act, name)
                    if n >= NPT:
                        act.wait_ge(pv_step, n - NPT + 1)
                    release(nc.scalar.activation(PT[:, n % NPT, :, :], A(name)[:, :, :], ACT.Exp, scale=SCALE), name)
                name = ("t2", u)
                written(act, name)
                if u >= 1:
                    written(act, ("proj", u - 1))
                nc.scalar.copy(oT[:, :], D(name)[:, 0:T])
                release(nc.scalar.copy(oTr[0:CR, :], D(name)[0:CR, T:2 * T]), name)
                if u + 1 < NU:
                    maxima(u + 1)
                if u + 2 < NU:
                    prep(u + 2)
                name = ("t3", u)
                written(act, name)
                if u >= 1:
                    written(act, hidden_jobs(u - 1)[-1])
                nc.scalar.activation(h2T[:, :], D(name)[:, 0:T], ACT.Identity,
                                     scale=mod[:, L, 4, b:b + 1], bias=mod[:, L, 3, b:b + 1])
                release(nc.scalar.activation(h2Tr[0:CR, :], D(name)[0:CR, T:2 * T], ACT.Identity,
                                               scale=modr[:, L, 4, b:b + 1], bias=modr[:, L, 3, b:b + 1]),
                          name)
                if L == 1:
                    act.wait_ge(lgm_done, b + 1)
                    nc.scalar.activation(lge[:, :, :], lg[:, :, :], ACT.Exp).then_inc(lge_done, 1)
                for k, group in enumerate(hidden_chunks(L)):
                    name = ("g", u, k)
                    e0, c0, rows = group[0]
                    n = len(group)
                    at = experts_before(u) + e0
                    written(act, name)
                    if at >= 2 and c0 == 0:
                        written(act, fc2_job(at - 2))
                    release(nc.scalar.activation(G[0:rows, at % 2, c0:c0 + n, :], A(name)[0:rows, 0:n, :],
                                                 ACT.Gelu_apprx_tanh), name)
            for j in range(DR):
                name = ("qr", j)
                used(act, name)
                if j >= 1:
                    act.wait_ge(qr_done, j)
                nc.scalar.activation(junk[:, j:C], vb[:, j:C], ACT.Square,
                                     accum_out=qsc[:, 0:1]).then_inc(sig_done, 1)

        @block.vector
        def _(dve):
            count = [0]

            def link(ins):
                count[0] += 1
                ins.then_inc(dchain, 1)
                dve.wait_ge(dchain, count[0])

            for i in range(2):
                nc.vector.memset(KS[i][32:KS_ROWS + 1, :, :].bitcast(U32), 0x3F803F80).then_inc(consts, 1)
            nc.vector.memset(G[FR:FR + 1, :, FC, :], 1.0).then_inc(consts, 1)
            dve.wait_ge(achain, 2)
            dve.wait_ge(consts, CONSTS)
            link(nc.vector.tensor_scalar(ee[:, :], ee[:, :], 1.0, None, ALU.add))
            link(nc.vector.tensor_scalar(eer[:, :], eer[:, :], 1.0, None, ALU.add))
            link(nc.vector.reciprocal(ee[:, :], ee[:, :]))
            link(nc.vector.reciprocal(eer[:, :], eer[:, :]))
            link(nc.vector.tensor_tensor(sT[:, :], cT[:, :], ee[:, :], ALU.mult))
            link(nc.vector.tensor_tensor(sTr[0:CR, :], cTr[:, :], eer[:, :], ALU.mult))
            nc.vector.tensor_copy(sTb[:, :, :], sT[:, :].unsqueeze(2).to_broadcast([P, B, P])).then_inc(silu_done, 1)
            nc.vector.tensor_copy(sTrb[:, :, :],
                                  sTr[:, :].unsqueeze(2).to_broadcast([CR + 1, B, P])).then_inc(silu_done, 1)
            for L in range(NL):
                name = ("ada", L)
                written(dve, name)
                src = D(name)[:, 0:6 * B].rearrange("p (s b) -> p s b", b=B)
                srcr = D(name)[0:CR, 6 * B:12 * B].rearrange("p (s b) -> p s b", b=B)
                nc.vector.tensor_copy(mod[:, L, 0:4:3, :], src[:, 0:4:3, :])
                nc.vector.tensor_copy(modr[:, L, 0:4:3, :], srcr[:, 0:4:3, :])
                nc.vector.tensor_scalar(mod[:, L, 1:5:3, :], src[:, 1:5:3, :], 1.0, None, ALU.add)
                release(nc.vector.tensor_scalar(modr[:, L, 1:5:3, :], srcr[:, 1:5:3, :], 1.0, None, ALU.add),
                          name)
            for L in range(NL):
                for b in range(B):
                    name = ("gate", L, b)
                    written(dve, name)
                    release(nc.vector.tensor_copy(gates[:, L, b, :, :],
                                                    D(name)[:, 0:2 * C].rearrange("p (s c) -> p s c", s=2)),
                              name)
            dve.wait_ge(w_in[2], W_IN[2])
            for w, m in ((Wqkv, gm), (Wqkvr, gmr)):
                wv = w[:, 2, 0:2 * C].rearrange("p (h r) -> p h r", r=HD)
                link(nc.vector.tensor_reduce(m[:, :], wv, AX.X, ALU.add))
                link(nc.vector.tensor_scalar(m[:, :], m[:, :], 1.0 / HD, None, ALU.mult))
                nc.vector.tensor_tensor(wv, wv, m[:, :].unsqueeze(2).to_broadcast([w.shape[0], 2 * H, HD]),
                                        ALU.subtract).then_inc(centred, 1)

            def layer_norm(n, b):
                for k in range(NT):
                    nc.vector.bn_stats(stats[:, k, :], x[:, b, k, :]).then_inc(dchain, 1)
                count[0] += NT
                dve.wait_ge(dchain, count[0])
                for k in range(NT):
                    nc.vector.bn_aggr(mv[:, k, :], stats[:, k, :]).then_inc(dchain, 1)
                count[0] += NT
                dve.wait_ge(dchain, count[0])
                nc.vector.tensor_scalar(ve[:, :], mv[:, :, 1], EPS, None, ALU.add).then_inc(var_done, 1)
                dve.wait_ge(rstd_done, n + 1)
                if n >= 1:
                    written(dve, norm_job(n - 1))
                for k in range(NT):
                    nc.vector.tensor_scalar(xh[:, k, :], x[:, b, k, :], mv[:, k, 0:1], rstd[:, k:k + 1],
                                            ALU.subtract, ALU.mult).then_inc(xh_ready, 1)

            def ln_no(kind, u):
                return LN_ORDER.index((kind, u))

            def prep(u):
                L, b = u // B, u % B
                if u < B:
                    dve.wait_ge(x_in, 16 * B)
                else:
                    dve.wait_ge(x_new, 2 * (u - B) + 2)
                layer_norm(ln_no(1, u), b)
                c = CH[L]
                if L == 2:
                    name = ("var", u)
                    written(dve, name)
                    if u > 2 * B:
                        dve.wait_ge(qrs_done, u - 2 * B)
                    release(nc.vector.tensor_scalar(qve[:, :], D(name)[:, 0:T], EPS, None, ALU.add), name)
                    for j, (lo, hi) in enumerate(QKJ[L]):
                        name = ("rs", u, j)
                        written(dve, name)
                        used(dve, ("qk", u, j))
                        release(nc.vector.tensor_tensor(
                            qn[:, lo:hi, :], qn[:, lo:hi, :], D(name)[0:c, :].rearrange("p (k t) -> p k t", t=T),
                            ALU.mult), name)
                for j, (lo, hi) in enumerate(QKJ[L]):
                    dve.wait_ge(p1_done, 2 * u + j + 1)
                    if u >= 1:
                        dve.wait_ge(p3_done, 2 * u)
                    if L < 2:
                        name = ("qk", u, j)
                        ins = nc.vector.tensor_tensor(
                            r1[0:c, lo:hi, :], D(name)[0:c, 0:(hi - lo) * T].rearrange("p (k t) -> p k t", t=T),
                            parts[0:c, 0, lo:hi, :], ALU.subtract)
                        release(ins, name)
                    else:
                        used(dve, ("rs", u, j))
                        nc.vector.tensor_tensor(r1[0:c, lo:hi, :], qn[0:c, lo:hi, :], parts[0:c, 0, lo:hi, :],
                                                ALU.subtract).then_inc(r1_done, 1)
                    remainder(dve, u, j)
                    if u >= 1:
                        dve.wait_ge(parts_out[(u - 1) % 2], 16 * 3 * ((u - 1) // 2 + 1))
                    nc.vector.tensor_copy(parts[0:c, 1, lo:hi, :], r1[0:c, lo:hi, :]).then_inc(p2_done, 1)

            def maxima(u, h):
                name = ("s", u, h)
                written(dve, name)
                if u >= 2 and h == 0:
                    written(dve, ("nm", u - 2))
                release(nc.vector.tensor_reduce(nm[u % 2][:, :, h], D(name)[:, :].rearrange("p (n k) -> p n k", n=NT),
                                                  AX.X, ALU.max, negate=True), name)

            def gated(n, src, gate):
                if n >= 1:
                    dve.wait_ge(x_new, n)
                return nc.vector.tensor_tensor(tmp[:, :, :], src,
                                               gate.unsqueeze(1).to_broadcast([P, NT, C]), ALU.mult)

            prep(0)
            for h in range(H):
                if h == 0:
                    pass
                maxima(0, h)
            prep(1)
            for u in range(NU):
                L, b = u // B, u % B
                if u + 1 < NU:
                    for h in range(H):
                        maxima(u + 1, h)
                dve.wait_ge(pv_step, 8 * (u + 1))
                link(nc.vector.reciprocal(rden[:, :], O[:, :, :, HD].rearrange("p n h -> p (n h)")))
                if u >= 1:
                    written(dve, ("t2", u - 1))
                nc.vector.tensor_tensor(
                    on[:, :, :].rearrange("p n (h r) -> p n h r", r=HD), O[:, :, :, 0:HD],
                    rden[:, :].rearrange("p (n h) -> p n h", n=NT).unsqueeze(3).to_broadcast([P, NT, H, HD]),
                    ALU.mult).then_inc(on_done, 1)
                name = ("proj", u)
                written(dve, name)
                release(gated(2 * u, D(name)[:, 0:NT * C].rearrange("p (n c) -> p n c", n=NT),
                              gates[:, L, b, 0, :]), name)
                if u + 2 < NU:
                    prep(u + 2)
                dve.wait_ge(x_new, 2 * u + 1)
                layer_norm(ln_no(2, u), b)
                if L == 1:
                    name = ("gl", u)
                    written(dve, name)
                    if b >= 1:
                        dve.wait_ge(lge_done, b)
                    gl = D(name)[:, 0:NT * NE].rearrange("p (n e) -> p n e", n=NT)
                    release(nc.vector.tensor_copy(lraw[:, :, :], gl), name)
                    used(dve, name)
                    link(nc.vector.tensor_reduce(lgm[:, :], lraw[:, :, :], AX.X, ALU.max))
                    nc.vector.tensor_tensor(lg[:, :, :], lraw[:, :, :],
                                            lgm[:, :].unsqueeze(2).to_broadcast([P, NT, NE]),
                                            ALU.subtract).then_inc(lgm_done, 1)
                    dve.wait_ge(lgm_done, b + 1)
                    link(nc.vector.memset(cmpt[:, :, :, :], 0.0))
                    n_cmp = 0
                    for f in range(NE):
                        for lo, hi, op in ((0, f, ALU.is_gt), (f + 1, NE, ALU.is_ge)):
                            if hi > lo:
                                nc.vector.tensor_tensor(
                                    cmpt[:, :, lo:hi, f], lraw[:, :, f:f + 1].to_broadcast([P, NT, hi - lo]),
                                    lraw[:, :, lo:hi], op).then_inc(dchain, 1)
                                n_cmp += 1
                    count[0] += n_cmp
                    dve.wait_ge(dchain, count[0])
                    link(nc.vector.tensor_reduce(rank[:, :, :], cmpt[:, :, :, :], AX.X, ALU.add))
                    dve.wait_ge(lge_done, b + 1)
                    link(nc.vector.scalar_tensor_tensor(cwt[:, :, :], rank[:, :, :], 1.5, lge[:, :, :],
                                                        ALU.is_lt, ALU.mult))
                    link(nc.vector.tensor_reduce(den[:, :], cwt[:, :, :], AX.X, ALU.add))
                    link(nc.vector.reciprocal(den[:, :], den[:, :]))
                    link(nc.vector.tensor_tensor(cw[:, :, :], cwt[:, :, :],
                                                 den[:, :].unsqueeze(2).to_broadcast([P, NT, NE]), ALU.mult))
                    for e in range(NE):
                        name = ("fc2", u, e)
                        written(dve, name)
                        for k in range(NT):
                            src = D(name)[:, k * C:(k + 1) * C]
                            if e == 0:
                                ins = nc.vector.tensor_scalar(acc[:, k, :], src, cw[:, k, e:e + 1], None, ALU.mult)
                            else:
                                ins = nc.vector.scalar_tensor_tensor(acc[:, k, :], src, cw[:, k, e:e + 1],
                                                                     acc[:, k, :], ALU.mult, ALU.add)
                        release(ins, name)
                        used(dve, name)
                    gated(2 * u + 1, acc[:, :, :], gates[:, L, b, 1, :]).then_inc(mixed, 1)
                else:
                    name = ("fc2", u, 0)
                    written(dve, name)
                    release(gated(2 * u + 1, D(name)[:, 0:NT * C].rearrange("p (n c) -> p n c", n=NT),
                                  gates[:, L, b, 1, :]), name)

            WTv = WT[:, :].rearrange("c (p t) -> c t p", t=16)
            WTrv = WTr[0:CR, :].rearrange("c (p t) -> c t p", t=16)
            for k in range(8):
                name = ("wt", k)
                written(dve, name)
                q = k // 2
                if k % 2 == 0:
                    ins = nc.vector.tensor_copy(WTv[:, 4 * q:4 * q + 4, :],
                                                D(name)[:, 0:504].rearrange("c (t p) -> c t p", t=4))
                else:
                    ins = nc.vector.tensor_copy(WTrv[:, 4 * q:4 * q + 4, :],
                                                D(name)[0:CR, 0:504].rearrange("c (t p) -> c t p", t=4))
                release(ins, name)
            for k in range(4):
                name = ("vv", k)
                written(dve, name)
                release(nc.vector.tensor_copy(vs[:, 504 * k:504 * k + 504], D(name)[0:B, 0:504]),
                          name)
            idb = ident[0:DR, 0:DR].unsqueeze(1).to_broadcast([DR, B, DR])
            written(dve, ("ut",))
            release(nc.vector.tensor_tensor(Ask[:, :, :], Up[:, :, :],
                                              D(("ut",))[0:DR, 0:256].rearrange("p (b j) -> p b j", b=B), ALU.subtract),
                      ("ut",))
            used(dve, ("ut",))
            link(nc.vector.tensor_tensor(Asq[:, :, :], Ask[:, :, :], Ask[:, :, :], ALU.mult))
            nc.vector.tensor_reduce(fr[:, :], Asq[:, :, :], AX.X, ALU.add).then_inc(fr_done, 1)
            written(dve, ("fro",))
            release(nc.vector.tensor_copy(frb[:, :], D(("fro",))[0:DR, 0:B]), ("fro",))
            used(dve, ("fro",))
            link(nc.vector.tensor_tensor(need[:, :, :], frb[:, :].unsqueeze(2).to_broadcast([DR, B, SQUARINGS]),
                                         thr[:, :].unsqueeze(1).to_broadcast([DR, B, SQUARINGS]), ALU.is_gt))
            for s in range(2):
                link(nc.vector.tensor_copy(needu[:, :, s, :], need[:, :, :].rearrange("p b k -> p k b")))
            link(nc.vector.tensor_scalar(fac[:, :, :], need[:, :, :], -0.5, 1.0, ALU.mult, ALU.add))
            n = SQUARINGS // 2
            while n >= 1:
                link(nc.vector.tensor_tensor(fac[:, :, 0:n], fac[:, :, 0:n], fac[:, :, n:2 * n], ALU.mult))
                n //= 2
            nc.vector.tensor_tensor(X[:, :, :], Ask[:, :, :], fac[:, :, 0:1].to_broadcast([DR, B, DR]),
                                    ALU.mult).then_inc(X_done, 1)
            dve.wait_ge(X_done, 1)
            nc.vector.scalar_tensor_tensor(E0[:, :, :], X[:, :, :], 1.0 / TAYLOR, idb, ALU.mult,
                                           ALU.add).then_inc(E_done, 1)
            for k in range(TAYLOR - 1):
                name = ("tay", k)
                dst = Z[:, 0:B, :] if k == TAYLOR - 2 else E0[:, :, :]
                written(dve, name)
                release(nc.vector.scalar_tensor_tensor(
                    dst, D(name)[0:DR, 0:B * DR].rearrange("p (b j) -> p b j", b=B), -1.0 / (TAYLOR - 1 - k), idb,
                    ALU.mult, ALU.add), name)
            name = ("ft",)
            written(dve, name)
            release(nc.vector.tensor_copy(Z[:, B:2 * B, :],
                                            D(name)[0:DR, 0:B * DR].rearrange("p (b j) -> p b j", b=B)),
                      name)
            for k in range(SQUARINGS):
                name = ("sq", k)
                written(dve, name)
                release(nc.vector.copy_predicated(
                    Z[:, :, :], needu[:, k, :, :].rearrange("p s b -> p (s b)").unsqueeze(2).to_broadcast([DR, 2 * B, DR]),
                    D(name)[0:DR, :].rearrange("p (b j) -> p b j", j=DR)), name)
            used(dve, ("sq", SQUARINGS - 1))
            nc.vector.tensor_tensor(FmI[:, :, :], Z[:, B:2 * B, :], idb, ALU.subtract).then_inc(F_done, 1)
            dve.wait_ge(pt_in, 32)
            name = ("pt",)
            written(dve, name)
            release(nc.vector.tensor_copy(Pt[:, :], D(name)[0:DR, 0:C]), name)
            for j in range(DR):
                name = ("qr", j)
                row = D(name)[0:DR, :]
                norm, sa, g, sg, head, w = (qsc[:, k:k + 1] for k in range(1, 7))
                written(dve, name)
                release(nc.vector.tensor_copy(vb[:, j:C], row[:, j:C]), name)
                used(dve, name)
                alpha = vb[:, j:j + 1]
                link(nc.vector.tensor_scalar(sg, alpha, 0.0, 2.0, ALU.is_ge, ALU.mult))
                dve.wait_ge(norm_done, j + 1)
                link(nc.vector.scalar_tensor_tensor(sa, sg, 1.0, norm, ALU.subtract, ALU.mult))
                link(nc.vector.tensor_tensor(alpha, alpha, sa, ALU.add))
                link(nc.vector.scalar_tensor_tensor(g, sa, -1.0, alpha, ALU.mult, ALU.mult))
                link(nc.vector.tensor_scalar(g, g, -1e-37, None, ALU.min))
                link(nc.vector.reciprocal(g, g))
                nc.vector.scalar_tensor_tensor(Vq[:, j:C], vb[:, j:C], ident[0:DR, j:j + 1], Vq[:, j:C],
                                               ALU.mult, ALU.add).then_inc(dchain, 1)
                nc.vector.tensor_tensor_reduce(out=junk2[:, j:C], in0=Pt[:, j:C], in1=vb[:, j:C], scale=g,
                                               scalar=0.0, op0=ALU.mult, op1=ALU.add, accum_out=w).then_inc(dchain, 1)
                count[0] += 2
                dve.wait_ge(dchain, count[0])
                nc.vector.scalar_tensor_tensor(Pt[:, j:C], vb[:, j:C], w, Pt[:, j:C], ALU.mult,
                                               ALU.add).then_inc(qr_done, 1)
                dve.wait_ge(qr_done, j + 1)
            link(nc.vector.tensor_tensor_reduce(out=junk2[:, :], in0=Vq[:, :], in1=Vq[:, :], scale=0.5, scalar=1e-37,
                                                op0=ALU.mult, op1=ALU.add, accum_out=qsc[:, 3:4]))
            nc.vector.tensor_copy(qsc[:, 7:8], qsc[:, 3:4]).then_inc(vn_done, 1)
            dve.wait_ge(vg_done, 1)
            nc.vector.tensor_scalar(Vq[:, :], Vq[:, :], qsc[:, 6:7], None, ALU.mult).then_inc(qr_done, 1)
            name = ("vqt",)
            written(dve, name)
            nc.vector.tensor_copy(VqT[:, :], D(name)[:, 0:DR])
            release(nc.vector.tensor_copy(VqTr[:, :], D(name)[0:CR, DR:2 * DR]), name)
            name = ("vvt",)
            written(dve, name)
            nc.vector.tensor_copy(Nn[:, 0, :], D(name)[0:DR, 0:DR])
            release(nc.vector.tensor_copy(Nn[:, 1, :], D(name)[0:DR, 0:DR]), name)
            dve.wait_ge(tri_done, 2)
            nc.vector.tensor_tensor(Tn[:, :], ident[0:DR, 0:DR], Nn[:, 0, :], ALU.subtract).then_inc(N_done, 1)
            for k in range(5):
                name = ("nn", k)
                written(dve, name)
                dve.wait_ge(N_done, 1)
                release(nc.vector.tensor_copy(Nn[:, :, :], D(name)[0:DR, 0:2 * DR].rearrange("p (s j) -> p s j", s=2)),
                          name)
                name = ("tn", k)
                written(dve, name)
                release(nc.vector.tensor_tensor(Tn[:, :], Tn[:, :], D(name)[0:DR, 0:DR], ALU.add), name)
            written(dve, ("kk",))
            release(nc.vector.tensor_copy(Kq[:, :], D(("kk",))[0:DR, 0:C]), ("kk",))
            written(dve, ("uu",))
            link(nc.vector.tensor_scalar(Ut[:, DR:C], D(("uu",))[0:DR, DR:C], -1.0, None, ALU.mult))
            release(nc.vector.tensor_tensor(Ut[:, 0:DR], ident[0:DR, 0:DR], D(("uu",))[0:DR, 0:DR], ALU.subtract),
                      ("uu",))
            for k in range(2):
                written(dve, ("gm", k))
                release(nc.vector.tensor_copy(Gm[:, 2 * k:2 * k + 2, :],
                                                D(("gm", k))[0:DR, 0:2 * C].rearrange("p (b c) -> p b c", b=2)),
                          ("gm", k))
            for b in range(B):
                written(dve, ("m", b))
                nc.vector.tensor_copy(M[:, b, :], D(("m", b))[:, 0:C])
                release(nc.vector.tensor_copy(Mr[:, b, :], D(("m", b))[0:CR, C:2 * C]), ("m", b))
            for b in range(B):
                name = ("t4", b)
                written(dve, name)
                if b >= 1:
                    written(dve, ("y", b - 1))
                nc.vector.tensor_copy(xT[:, :], D(name)[:, 0:T])
                release(nc.vector.tensor_copy(xTr[:, :], D(name)[0:CR, T:2 * T]), name)
                name = ("y", b)
                written(dve, name)
                dve.wait_ge(x_new, 2 * NU)
                release(nc.vector.tensor_tensor(y[:, b, :, :], D(name)[:, 0:NT * C].rearrange("p (n c) -> p n c", n=NT),
                                                  x[:, b, :, :], ALU.add), name)

        @block.tensor
        def _(pe):
            mm = nc.tensor.matmul
            issued = {"d": 0, "a": 0}

            def d_take(name):
                n = d_no[name]
                assert n == issued["d"], (name, n, issued["d"], d_order[issued["d"]])
                issued["d"] += 1
                if n >= ND:
                    pe.wait_ge(d_free[n % ND], n // ND)
                return D_ring[n % ND]

            def d_give(ins, name):
                return ins.then_inc(d_full[d_no[name] % ND], 1)

            def a_take(name):
                n = a_no[name]
                assert n == issued["a"]
                issued["a"] += 1
                if n >= NA:
                    pe.wait_ge(a_free[n % NA], n // NA)
                return A_ring[n % NA]

            def a_give(ins, name):
                return ins.then_inc(a_full[a_no[name] % NA], 1)

            pe.wait_ge(consts, CONSTS)
            pe.wait_ge(ada_in, 16 * 9)
            pe.wait_ge(silu_done, 2)
            for L in range(NL):
                name = ("ada", L)
                d = d_take(name)
                for s in (0, 1, 3, 4):
                    for lo, rows, col in ((0, P, 0), (P, CR, 6 * B)):
                        o = d[0:rows, col + s * B:col + (s + 1) * B]
                        mm(o, Wada[:, L, s * C + lo:s * C + lo + rows], sT[:, :], start=True, stop=False)
                        last = mm(o, Wadar[:, L, s * C + lo:s * C + lo + rows], sTr[:, :], start=False, stop=True)
                d_give(last, name)
            for L in range(NL):
                for b in range(B):
                    name = ("gate", L, b)
                    d = d_take(name)
                    for k, s in enumerate((2, 5)):
                        o = d[:, k * C:(k + 1) * C]
                        mm(o, sTb[:, b, :], Wada[:, L, s * C:(s + 1) * C], start=True, stop=False)
                        last = mm(o, sTrb[:, b, :], Wadar[:, L, s * C:(s + 1) * C], start=False, stop=True)
                    d_give(last, name)

            def transposed(name, src, ready, value):
                d = d_take(name)
                pe.wait_ge(ready, value)
                for k in range(NT):
                    nc.tensor.transpose(d[:, k * P:(k + 1) * P], src[:, k, 0:P], ident[:, :])
                    last = nc.tensor.transpose(d[0:CR, T + k * P:T + (k + 1) * P], src[:, k, P:C], ident[:, :])
                d_give(last, name)

            def prep(u):
                L, i = u // B, u % 2
                transposed(("t1", u), xh, xh_ready, NT * (LN_ORDER.index((1, u)) + 1))
                if u % B == 0:
                    pe.wait_ge(w_in[L], W_IN[L])
                if u == 2 * B:
                    pe.wait_ge(centred, 2)
                used(pe, ("t1", u))
                c = CH[L]
                for j, (lo, hi) in enumerate(QKJ[L]):
                    name = ("qk", u, j)
                    d = d_take(name)
                    for k in range(lo, hi):
                        o = d[0:c, (k - lo) * T:(k - lo + 1) * T]
                        mm(o, Wqkv[:, L, k * c:(k + 1) * c], hT[:, :], start=True, stop=False)
                        last = mm(o, Wqkvr[:, L, k * c:(k + 1) * c], hTr[:, :], start=False, stop=True)
                    d_give(last, name)
                if L == 2:
                    name = ("var", u)
                    d = d_take(name)
                    for k in range(4):
                        pe.wait_ge(sq_done, 2 * (u - 2 * B) + k // 2 + 1)
                        last = mm(d[32 * k:32 * k + 32, 0:T], pick[:, :], qsq[:, k, :], start=True, stop=True)
                    d_give(last, name)
                    for j, (lo, hi) in enumerate(QKJ[L]):
                        name = ("rs", u, j)
                        d = d_take(name)
                        pe.wait_ge(qrs_done, u - 2 * B + 1)
                        for k in range(lo, hi):
                            last = mm(d[0:c, (k - lo) * T:(k - lo + 1) * T],
                                      spread[:, k, :, :].rearrange("p k r -> p (k r)"), qrs[:, :],
                                      start=True, stop=True)
                        d_give(last, name)
                name = ("v", u)
                d = d_take(name)
                for k in range(NT):
                    o = d[:, k * C:(k + 1) * C]
                    mm(o, hT[:, k * P:(k + 1) * P], Wqkv[:, L, 2 * C:3 * C], start=True, stop=False)
                    last = mm(o, hTr[:, k * P:(k + 1) * P], Wqkvr[:, L, 2 * C:3 * C], start=False, stop=True)
                d_give(last, name)

            def scores(u, h):
                i = u % 2
                if h == 0:
                    pe.wait_ge(stk_in[i], 16 * 2 * SLOTS * (u // 2 + 1))
                name = ("s", u, h)
                d = d_take(name)
                for k in range(NT):
                    last = mm(d[:, k * T:(k + 1) * T], QS[i][0:KS_ROWS, h, k * P:(k + 1) * P],
                              KS[i][0:KS_ROWS, h, :], start=True, stop=True)
                d_give(last, name)

            def maxima(u):
                name = ("nm", u)
                d = d_take(name)
                used(pe, ("s", u, H - 1))
                db = d[:, :].bitcast(BF16)
                for k in range(NT):
                    last = nc.tensor.transpose(db[0:H, k * P:(k + 1) * P], nm[u % 2][:, k, :], identb[:, :])
                d_give(last, name)

            def weights(u, g):
                i = u % 2
                if g == 0:
                    pe.wait_ge(nm_in[i], 16 * (u // 2 + 1))
                name = ("e", u, g)
                a = a_take(name)
                for hh in range(2):
                    for k in range(NT):
                        last = mm(a[:, 2 * hh + k, :], KS[i][:, 2 * g + hh, k * P:(k + 1) * P],
                                  QS[i][:, 2 * g + hh, :], start=True, stop=True)
                a_give(last, name)

            def values(u, g):
                n = 8 * u + g
                used(pe, ("e", u, g))
                if g == 0:
                    used(pe, ("v", u))
                    if u >= 1:
                        pe.wait_ge(on_done, u)
                for hh in range(2):
                    for q in range(NT):
                        for k in range(NT):
                            last = mm(O[:, q, 2 * g + hh, 0:HD + 1], PT[:, n % NPT, 2 * hh + k, q * P:(q + 1) * P],
                                      V[u % 2][:, k, 2 * g + hh, :], start=k == 0, stop=k == NT - 1)
                last.then_inc(pv_step, 1)

            prep(0)
            for h in range(H):
                scores(0, h)
            maxima(0)
            prep(1)
            for u in range(NU):
                L = u // B
                for g in range(H // 2):
                    weights(u, g)
                    if u + 1 < NU:
                        scores(u + 1, 2 * g)
                        scores(u + 1, 2 * g + 1)
                    if g >= 1:
                        values(u, g - 1)
                values(u, H // 2 - 1)
                transposed(("t2", u), on, on_done, u + 1)
                if u + 1 < NU:
                    maxima(u + 1)
                name = ("proj", u)
                d = d_take(name)
                used(pe, ("t2", u))
                for k in range(NT):
                    o = d[:, k * C:(k + 1) * C]
                    mm(o, oT[:, k * P:(k + 1) * P], Wp[:, L, :], start=True, stop=False)
                    last = mm(o, oTr[:, k * P:(k + 1) * P], Wpr[:, L, :], start=False, stop=True)
                d_give(last, name)
                if u + 2 < NU:
                    prep(u + 2)
                transposed(("t3", u), xh, xh_ready, NT * (LN_ORDER.index((2, u)) + 1))
                used(pe, ("t3", u))
                if L == 1:
                    name = ("gl", u)
                    d = d_take(name)
                    for k in range(NT):
                        o = d[:, k * NE:(k + 1) * NE]
                        mm(o, h2T[:, k * P:(k + 1) * P], Wg[:, :], start=True, stop=False)
                        last = mm(o, h2Tr[0:CR, k * P:(k + 1) * P], Wgr[:, :], start=False, stop=True)
                    d_give(last, name)
                groups = hidden_chunks(L)

                def fc1(e):
                    for k in (2 * e, 2 * e + 1):
                        name = ("g", u, k)
                        a = a_take(name)
                        for j, (e, c, rows) in enumerate(groups[k]):
                            mm(a[0:rows, j, :], W1[L][:, e, c * P:c * P + rows], h2T[:, :], start=True, stop=False)
                            last = mm(a[0:rows, j, :], W1r[L][:, e, c * P:c * P + rows], h2Tr[:, :],
                                      start=False, stop=True)
                        a_give(last, name)

                fc1(0)
                for e in range(EXPERTS[L]):
                    if e + 1 < EXPERTS[L]:
                        fc1(e + 1)
                    at = experts_before(u) + e
                    name = ("fc2", u, e)
                    d = d_take(name)
                    used(pe, ("g", u, 2 * e + 1))
                    for k in range(NT):
                        o = d[:, k * C:(k + 1) * C]
                        for c in range(FC + 1):
                            rows = P if c < FC else FR + 1
                            last = mm(o, G[0:rows, at % 2, c, k * P:(k + 1) * P], W2[L][0:rows, e, c, :],
                                      start=c == 0, stop=c == FC)
                    d_give(last, name)

            pe.wait_ge(l3_in, 32)
            for k in range(8):
                name = ("wt", k)
                d = d_take(name)
                q = k // 2
                for j in range(4):
                    if k % 2 == 0:
                        last = nc.tensor.transpose(d[:, 126 * j:126 * j + 126], Wl[:, 4 * q + j, 0:P],
                                                   ident[0:126, 0:126])
                    else:
                        last = nc.tensor.transpose(d[0:CR, 126 * j:126 * j + 126], Wl[:, 4 * q + j, P:C],
                                                   ident[0:126, 0:126])
                d_give(last, name)
            used(pe, ("wt", 7))
            for k in range(4):
                name = ("vv", k)
                d = d_take(name)
                mm(d[0:B, 0:504], sT[:, :], WT[:, 504 * k:504 * k + 504], start=True, stop=False)
                d_give(mm(d[0:B, 0:504], sTr[:, :], WTr[:, 504 * k:504 * k + 504], start=False, stop=True), name)
            name = ("ut",)
            d = d_take(name)
            pe.wait_ge(up_in, 16 * (DR - 1))
            for b in range(B):
                last = nc.tensor.transpose(d[0:DR, b * DR:(b + 1) * DR], Up[:, b, :], ident[0:DR, 0:DR])
            d_give(last, name)
            name = ("fro",)
            d = d_take(name)
            pe.wait_ge(fr_done, 1)
            d_give(mm(d[0:DR, 0:B], ones[:, :], fr[:, :], start=True, stop=True), name)
            for k in range(TAYLOR - 1):
                name = ("tay", k)
                d = d_take(name)
                if k == 0:
                    pe.wait_ge(E_done, 1)
                else:
                    used(pe, ("tay", k - 1))
                for b in range(B):
                    last = mm(d[0:DR, b * DR:(b + 1) * DR], X[:, b, :], E0[:, b, :], start=True, stop=True)
                d_give(last, name)
            name = ("ft",)
            d = d_take(name)
            used(pe, ("tay", TAYLOR - 2))
            for b in range(B):
                last = nc.tensor.transpose(d[0:DR, b * DR:(b + 1) * DR], Z[:, b, :], ident[0:DR, 0:DR])
            d_give(last, name)
            for k in range(SQUARINGS):
                name = ("sq", k)
                d = d_take(name)
                used(pe, ("sq", k - 1) if k else ("ft",))
                for b in range(2 * B):
                    last = mm(d[0:DR, b * DR:(b + 1) * DR], Z[:, (b + B) % (2 * B), :], Z[:, b, :],
                              start=True, stop=True)
                d_give(last, name)
            name = ("pt",)
            d = d_take(name)
            pe.wait_ge(pt_in, 32)
            nc.tensor.transpose(d[0:DR, 0:P], Pn[:, :], ident[:, :])
            d_give(nc.tensor.transpose(d[0:DR, P:C], Pnr[:, :], ident[0:CR, 0:CR]), name)
            used(pe, ("pt",))
            for j in range(DR):
                name = ("qr", j)
                d = d_take(name)
                if j >= 1:
                    pe.wait_ge(qr_done, j)
                d_give(mm(d[0:DR, j:C], ident[0:DR, j:j + 1].to_broadcast([DR, DR]), Pt[:, j:C],
                          start=True, stop=True), name)
            pe.wait_ge(qr_done, DR + 1)
            name = ("vqt",)
            d = d_take(name)
            nc.tensor.transpose(d[:, 0:DR], Vq[:, 0:P], ident[0:DR, 0:DR])
            d_give(nc.tensor.transpose(d[0:CR, DR:2 * DR], Vq[:, P:C], ident[0:DR, 0:DR]), name)
            name = ("vvt",)
            d = d_take(name)
            used(pe, ("vqt",))
            mm(d[0:DR, 0:DR], VqT[:, :], VqT[:, :], start=True, stop=False)
            d_give(mm(d[0:DR, 0:DR], VqTr[:, :], VqTr[:, :], start=False, stop=True), name)
            pe.wait_ge(tri_done, 2)
            for k in range(5):
                name = ("nn", k)
                d = d_take(name)
                if k:
                    used(pe, ("nn", k - 1))
                mm(d[0:DR, 0:DR], Nn[:, 1, :], Nn[:, 0, :], start=True, stop=True)
                d_give(mm(d[0:DR, DR:2 * DR], Nn[:, 0, :], Nn[:, 1, :], start=True, stop=True), name)
                name = ("tn", k)
                d = d_take(name)
                used(pe, ("nn", k))
                if k:
                    used(pe, ("tn", k - 1))
                else:
                    pe.wait_ge(N_done, 1)
                d_give(mm(d[0:DR, 0:DR], Nn[:, 1, :], Tn[:, :], start=True, stop=True), name)
            name = ("kk",)
            d = d_take(name)
            used(pe, ("tn", 4))
            d_give(mm(d[0:DR, 0:C], Tn[:, :], Vq[:, :], start=True, stop=True), name)
            name = ("uu",)
            d = d_take(name)
            used(pe, ("kk",))
            d_give(mm(d[0:DR, 0:C], Vq[:, 0:DR], Kq[:, :], start=True, stop=True), name)
            used(pe, ("uu",))
            pe.wait_ge(F_done, 1)
            for k in range(2):
                name = ("gm", k)
                d = d_take(name)
                for j in range(2):
                    last = mm(d[0:DR, j * C:(j + 1) * C], FmI[:, 2 * k + j, :], Ut[:, :], start=True, stop=True)
                d_give(last, name)
            for b in range(B):
                name = ("m", b)
                d = d_take(name)
                used(pe, ("gm", b // 2))
                mm(d[:, 0:C], Ut[:, 0:P], Gm[:, b, :], start=True, stop=True)
                d_give(mm(d[0:CR, C:2 * C], Ut[:, P:C], Gm[:, b, :], start=True, stop=True), name)
            for b in range(B):
                transposed(("t4", b), x[:, b, :, :], x_new, 2 * NU)
                name = ("y", b)
                d = d_take(name)
                used(pe, ("t4", b))
                used(pe, ("m", b))
                for k in range(NT):
                    o = d[:, k * C:(k + 1) * C]
                    mm(o, xT[:, k * P:(k + 1) * P], M[:, b, :], start=True, stop=False)
                    last = mm(o, xTr[:, k * P:(k + 1) * P], Mr[:, b, :], start=False, stop=True)
                d_give(last, name)


def build(nc, aps, out):
    t = {"x": aps["x"], "cond": aps["cond_1152"]}
    t["ada"] = [aps["L0_cond_W_ada"], aps["L1_cond_w_adaln"], aps["L2_cond_w_mod"]]
    t["b_ada"] = [aps["L0_cond_b_ada"], aps["L1_cond_b_adaln"], aps["L2_cond_b_mod"]]
    t["qkv"] = [aps["L0_cond_W_qkv"], aps["L1_cond_w_qkv"], aps["L2_cond_w_qkv"]]
    t["b_qkv"] = [aps[f"L{L}_cond_b_qkv"] for L in range(3)]
    t["proj"] = [aps["L0_cond_W_proj"], aps["L1_cond_w_proj"], aps["L2_cond_w_proj"]]
    t["b_proj"] = [aps[f"L{L}_cond_b_proj"] for L in range(3)]
    t["w1"] = [[aps["L0_cond_W_fc1"]], [aps["L1_cond_w1"][e] for e in range(4)], [aps["L2_cond_w1"]]]
    t["b1"] = [[aps["L0_cond_b_fc1"]], [aps["L1_cond_b1"][e] for e in range(4)], [aps["L2_cond_b1"]]]
    t["w2"] = [[aps["L0_cond_W_fc2"]], [aps["L1_cond_w2"][e] for e in range(4)], [aps["L2_cond_w2"]]]
    t["b2"] = [[aps["L0_cond_b_fc2"]], [aps["L1_cond_b2"][e] for e in range(4)], [aps["L2_cond_b2"]]]
    t["w_gate"] = aps["L1_cond_w_gate"]
    t["g_q"], t["g_k"] = aps["L2_cond_g_q"], aps["L2_cond_g_k"]
    t["rot_p"], t["rot_w"], t["rot_b"] = aps["L3_cond_P"], aps["L3_cond_W"], aps["L3_cond_b"]
    cond_sequence_kernel(nc, t, out)


def kernel(**inputs):
    import numpy as _np
    import concourse.bacc as _bacc
    from concourse import mybir as _mybir
    from concourse.bass_utils import run_bass_kernel_spmd as _run

    nc = _bacc.Bacc("TRN2", target_bir_lowering=False, num_devices=1)
    arrays, aps = {}, {}
    for name, value in inputs.items():
        a = _np.ascontiguousarray(value)
        arrays[f"in_{name}_dram"] = a
        aps[name] = nc.dram_tensor(f"in_{name}_dram", a.shape, _mybir.dt.from_np(a.dtype), kind="ExternalInput").ap()
    out = nc.dram_tensor("out_0_dram", (4, 256, 144), _mybir.dt.float32, kind="ExternalOutput").ap()
    build(nc, aps, out)
    r = _run(nc, [arrays], core_ids=[0])
    return r.results[0]["out_0_dram"]
```

```python
import concourse.bass as bass
from concourse import mybir
from contextlib import ExitStack


def cond_sequence_kernel(nc, t, out):
    F32 = mybir.dt.float32
    BF16 = mybir.dt.bfloat16
    U32 = mybir.dt.uint32
    ALU = mybir.AluOpType
    ACT = mybir.ActivationFunctionType
    AX = mybir.AxisListType

    B, T, C = 4, 256, 144
    P = 128
    NT = T // P
    CR = C - P
    H, HD = 16, 9
    FF = 4 * C
    FC = FF // P
    FR = FF - FC * P
    NL, NU = 3, 12
    NE = 4
    EXPERTS = [1, NE, 1]
    EPS = 1e-6
    SCALE = float(HD) ** -0.5
    DR = 64
    NSK = DR * (DR - 1) // 2
    SLOTS = 6
    KS_ROWS = SLOTS * HD
    CH = [96, 96, 72]
    NCH = [2 * C // c for c in CH]
    QKJ = [[(0, 2), (2, 3)], [(0, 2), (2, 3)], [(0, 2), (2, 4)]]
    TAYLOR = 10
    SQUARINGS = 16

    def hidden_chunks(L):
        E = EXPERTS[L]
        groups = []
        for e in range(E):
            groups += [[(e, c, P) for c in range(FC)], [(e, FC, FR)]]
        return groups

    def experts_before(u):
        return sum(EXPERTS[k // B] for k in range(u))

    HG = H // 4
    DIVIDE_AT = {3: 0, 5: 1, 7: 2}

    ND, NA = 3, 2
    d_order = [("ada", L) for L in range(NL)] + [("gate", L, b) for L in range(NL) for b in range(B)]

    def prep_jobs(u):
        L = u // B
        jobs = [("t1", u)] + [("qk", u, j) for j in range(2)]
        if L == 2:
            jobs += [("var", u), ("rs", u, 0), ("rs", u, 1)]
        return jobs + [("v", u)]

    def mlp_jobs(u):
        L = u // B
        return [("t3", u)] + ([("gl", u)] if L == 1 else []) + [("fc2", u, e) for e in range(EXPERTS[L])]

    V_JOBS = [("wt", k) for k in range(8)] + [("vv", k) for k in range(4)] + [("pt",)]
    EXP_JOBS = ([("ut",), ("fro",)] + [("tay", k) for k in range(TAYLOR - 1)] + [("ft",)]
                + [("sq", k) for k in range(SQUARINGS)])
    T_JOBS = ([("vqt",), ("vvt",)] + [(s, k) for k in range(5) for s in ("nn", "tn")] + [("kk",), ("uu",)])
    U_JOBS = [[("gm", 0), ("gm", 1)], [("m", 0), ("m", 1)], [("m", 2), ("m", 3)]]

    def rotation_jobs(u, g):
        at = H // 2 * u + g
        if at < DR:
            return [("qr", at)]
        at -= DR
        if at < len(EXP_JOBS):
            return [EXP_JOBS[at]] + T_JOBS[at:at + 1]
        at -= len(EXP_JOBS)
        return U_JOBS[at] if at < len(U_JOBS) else []

    def y_jobs(b):
        return [("t4", b), ("y", b)]

    d_order += prep_jobs(0)
    for h in range(H):
        d_order += [("s", 0, h)] + V_JOBS[h:h + 1]
    d_order += [("nm", 0)] + prep_jobs(1)
    for u in range(NU):
        for g in range(H // 2):
            if u + 1 < NU:
                d_order += [("s", u + 1, 2 * g), ("s", u + 1, 2 * g + 1)]
            d_order += rotation_jobs(u, g)
        if u + 1 < NU:
            d_order += [("nm", u + 1)]
        d_order += [("proj", u)]
        if u + 2 < NU:
            d_order += prep_jobs(u + 2)
        if u == NU - 1:
            d_order += [job for b in range(B - 1) for job in y_jobs(b)]
        d_order += mlp_jobs(u)
    d_order += y_jobs(B - 1)
    LN_ORDER = [(1, 0), (1, 1)]
    for u in range(NU):
        LN_ORDER += ([(1, u + 2)] if u + 2 < NU else []) + [(2, u)]
    CONSTS = 15 + SQUARINGS
    W_IN = [16 * (8 + 6 * EXPERTS[L] + (0, 2, 16)[L]) for L in range(NL)]
    d_no = {name: n for n, name in enumerate(d_order)}

    a_order = []
    for u in range(NU):
        a_order += [("e", u, g) for g in range(H // 2)]
        a_order += [("g", u, k) for k in range(len(hidden_chunks(u // B)))]
    a_no = {name: n for n, name in enumerate(a_order)}

    ctx = ExitStack()
    with ctx:
        def sb(name, shape, dt=F32):
            return ctx.enter_context(nc.sbuf_tensor(name, shape, dt))

        def sem(name):
            return ctx.enter_context(nc.semaphore(name))

        x = sb("x", [P, B, NT, C])
        xh = sb("xh", [P, NT, C])
        stats = sb("stats", [P, NT, 6])
        mv = sb("mv", [P, NT, 2])
        ve = sb("ve", [P, NT])
        rstd = sb("rstd", [P, NT])
        mhalf = sb("mhalf", [P, 1])
        phalf = sb("phalf", [P, 1])
        mone = sb("mone", [DR, 1])
        hT = sb("hT", [P, T])
        hTr = sb("hTr", [CR + 1, T])
        h2T = sb("h2T", [P, T])
        h2Tr = sb("h2Tr", [CR + 1, T])
        oT = sb("oT", [P, HG, T])
        ob = sb("ob", [P, T])
        rden = sb("rden", [P, T // 32])
        qt = ob
        parts = sb("parts", [96, 3, 4, T], BF16)
        r1 = sb("r1", [96, 4, T])
        qn = r1[0:72]
        qve = sb("qve", [P, T])
        qrs = sb("qrs", [P, T])
        pick = sb("pick", [72, 32])
        spread = sb("spread", [P, 4, 8, HD])
        QS = [sb(f"QS{i}", [KS_ROWS + 1, H, T], BF16) for i in range(2)]
        KS = [sb(f"KS{i}", [KS_ROWS + 1, H, T], BF16) for i in range(2)]
        V = [sb(f"V{i}", [P, NT, H, HD + 1]) for i in range(2)]
        nm = [sb(f"nm{i}", [P, NT, H], BF16) for i in range(2)]
        nmT = sb("nmT", [H, T], BF16)
        NPT = 4
        PT = sb("PT", [P, NPT, 4, T])
        G = sb("G", [P, 2, FC + 1, T])
        tmp = sb("tmp", [P, NT, C])
        acc = sb("acc", [P, NT, C])
        lraw = sb("lraw", [P, NT, NE])
        lg = sb("lg", [P, NT, NE])
        lgm = sb("lgm", [P, NT])
        lge = sb("lge", [P, NT, NE])
        cmpt = sb("cmpt", [P, NT, NE, NE])
        rank = sb("rank", [P, NT, NE])
        cwt = sb("cwt", [P, NT, NE])
        den = sb("den", [P, NT])
        cw = sb("cw", [P, NT, NE])
        cT = sb("cT", [P, B])
        cTr = sb("cTr", [CR, B])
        sT = sb("sT", [P, B])
        sTr = sb("sTr", [CR + 1, B])
        ee = sb("ee", [P, B])
        eer = sb("eer", [CR, B])
        sTb = PT[:, 0, 0:2, :].rearrange("p k t -> p (k t)").rearrange("p (b q) -> p b q", b=B)
        sTrb = PT[0:CR + 1, 1, 0:2, :].rearrange("p k t -> p (k t)").rearrange("p (b q) -> p b q", b=B)
        mod = sb("mod", [P, NL, 6, B])
        modr = sb("modr", [CR, NL, 6, B])
        gates = sb("gates", [P, NL, B, 2, C])
        ident = sb("ident", [P, P])
        identb = sb("identb", [P, P], BF16)
        Wada = sb("Wada", [P, NL, 6 * C])
        Wadar = sb("Wadar", [CR + 1, NL, 6 * C])
        Wqkv = sb("Wqkv", [P, NL, 3 * C])
        Wqkvr = sb("Wqkvr", [CR + 1, NL, 3 * C])
        gm = sb("gm", [P, 2 * H])
        gmr = sb("gmr", [CR + 1, 2 * H])
        Wp = sb("Wp", [P, NL, HG, C])
        W1 = [sb(f"W1_{L}", [P, EXPERTS[L], FF]) for L in range(NL)]
        W1r = [sb(f"W1r_{L}", [CR + 1, EXPERTS[L], FF]) for L in range(NL)]
        W2 = [sb(f"W2_{L}", [P, EXPERTS[L], FC + 1, C]) for L in range(NL)]
        Wg = sb("Wg", [P, NE])
        Wgr = sb("Wgr", [CR, NE])
        gq = sb("gq", [72, 2])
        old = Wada[:, :, :].rearrange("p l n -> p (l n)")
        qsq = old[0:72, 0:4 * T].rearrange("p (k t) -> p k t", t=T)
        old_at = [4 * T]

        def reuse(rows, *shape):
            n = 1
            for k in shape:
                n *= k
            part = old[0:rows, old_at[0]:old_at[0] + n]
            old_at[0] += n
            assert old_at[0] <= NL * 6 * C
            return part if len(shape) == 1 else part.rearrange("p (b n) -> p b n", b=shape[0])

        Wl = W1[1][0:126, :, :].rearrange("p e f -> p (e f)").rearrange("p (t c) -> p t c", t=16)
        WT = W2[1][:, :, :, :].rearrange("p e c n -> p (e c n)")[:, 0:NSK]
        WTr = W1r[1][:, :, :].rearrange("p e f -> p (e f)")[:, 0:NSK]
        vs = G[0:B, :, :, :].rearrange("p e c t -> p (e c t)")[:, 0:NSK]
        Up = sb("Up", [DR, B, DR])
        Ask = sb("Ask", [DR, B, DR])
        fr = sb("fr", [DR, B])
        frb = sb("frb", [DR, B])
        thr = sb("thr", [DR, SQUARINGS])
        need = sb("need", [DR, B, SQUARINGS])
        needu = sb("needu", [DR, SQUARINGS, 2, B], U32)
        fac = sb("fac", [DR, B, SQUARINGS])
        X = sb("X", [DR, B, DR])
        E0 = sb("E0", [DR, B, DR])
        Asq = E0
        Z = sb("Z", [DR, 2 * B, DR])
        ones = sb("ones", [DR, DR])
        Pt = sb("Pt", [DR, C])
        Pn = sb("Pn", [P, DR])
        Pnr = sb("Pnr", [CR, DR])
        Vq = sb("Vq", [DR, C])
        vb = sb("vb", [DR, C])
        heads = sb("heads", [DR, DR])
        below = sb("below", [DR, DR])
        junk = reuse(DR, C)
        junk2 = reuse(DR, C)
        qsc = sb("qsc", [DR, 10])
        Nn = reuse(DR, 2, DR)
        Tn = reuse(DR, DR)
        VqT = reuse(P, DR)
        VqTr = reuse(CR, DR)
        Kq = reuse(DR, C)
        Ut = reuse(DR, C)
        FmI = sb("FmI", [DR, B, DR])
        Gm = sb("Gm", [DR, B, C])
        M = Wqkv[:, :, :].rearrange("p l n -> p (l n)")[:, 0:B * C].rearrange("p (b c) -> p b c", b=B)
        Mr = Wqkvr[0:CR, :, :].rearrange("p l n -> p (l n)")[:, 0:B * C].rearrange("p (b c) -> p b c", b=B)
        xT, xTr = hT, hTr[0:CR]

        scr = nc.dram_tensor("parts_scratch", (2, 3, 2 * C, T), BF16).ap()
        nmscr = nc.dram_tensor("maxima_scratch", (2, H, T), BF16).ap()
        vscr = nc.dram_tensor("skew_scratch", (B, NSK), F32).ap()

        A_ring = [ctx.enter_context(nc.psum_tensor(f"A{i}", [P, 4, T], F32)) for i in range(NA)]
        D_ring = [ctx.enter_context(nc.psum_tensor(f"D{i}", [P, 512], F32)) for i in range(ND)]
        O = ctx.enter_context(nc.psum_tensor("O", [P, T], F32))

        d_full = [sem(f"d_full{i}") for i in range(ND)]
        d_free = [sem(f"d_free{i}") for i in range(ND)]
        a_full = [sem(f"a_full{i}") for i in range(NA)]
        a_free = [sem(f"a_free{i}") for i in range(NA)]
        consts = sem("consts")
        nm_out = [sem(f"nm_out{i}") for i in range(2)]
        mixed = sem("mixed")
        F_done = sem("F_done")
        var_done = sem("var_done")
        rstd_done = sem("rstd_done")
        qsd_done = sem("qsd_done")
        qrs_done = sem("qrs_done")
        norm_done = sem("norm_done")
        vn_done = sem("vn_done")
        vg_done = sem("vg_done")
        x_in = sem("x_in")
        c_in = sem("c_in")
        w_in = [sem(f"w_in{L}") for L in range(NL)]
        ada_in = sem("ada_in")
        l3_in = sem("l3_in")
        pt_in = sem("pt_in")
        silu_done = sem("silu_done")
        centred = sem("centred")
        xh_ready = sem("xh_ready")
        p1_done = sem("p1_done")
        p2_done = sem("p2_done")
        r1_done = sem("r1_done")
        p3_done = sem("p3_done")
        sq_done = sem("sq_done")
        parts_out = [sem(f"parts_out{i}") for i in range(2)]
        stk_in = [sem(f"stk_in{i}") for i in range(2)]
        nm_in = [sem(f"nm_in{i}") for i in range(2)]
        o_read = sem("o_read")
        oT_done = sem("oT_done")
        wp_zero = sem("wp_zero")
        x_new = sem("x_new")
        lgm_done = sem("lgm_done")
        lge_done = sem("lge_done")
        dchain = sem("dchain")
        achain = sem("achain")
        pchain = sem("pchain")
        tri_done = sem("tri_done")
        pv_step = sem("pv_step")
        v_out = sem("v_out")
        up_zero = sem("up_zero")
        up_in = sem("up_in")
        X_done = sem("X_done")
        fr_done = sem("fr_done")
        E_done = sem("E_done")
        sig_done = sem("sig_done")
        dot_done = sem("dot_done")
        w_done = sem("w_done")
        v_cut = sem("v_cut")
        qr_done = sem("qr_done")
        N_done = sem("N_done")
        y_out = sem("y_out")

        def slot(name):
            if name in a_no:
                return a_no[name] % NA, a_no[name] // NA, a_full, a_free
            return d_no[name] % ND, d_no[name] // ND, d_full, d_free

        def D(name):
            return D_ring[d_no[name] % ND]

        def A(name):
            return A_ring[a_no[name] % NA]

        def written(eng, name):
            i, turn, full, _ = slot(name)
            eng.wait_ge(full[i], turn + 1)

        def used(eng, name):
            i, turn, _, free = slot(name)
            eng.wait_ge(free[i], turn + 1)

        def release(ins, name):
            i, _, _, free = slot(name)
            return ins.then_inc(free[i], 1)

        def hidden_jobs(u):
            return [("g", u, k) for k in range(len(hidden_chunks(u // B)))]

        def fc2_job(n):
            for u in range(NU):
                if n < EXPERTS[u // B]:
                    return ("fc2", u, n)
                n -= EXPERTS[u // B]

        def remainder(eng, u, j):
            if u // B == 2:
                eng.wait_ge(r1_done, 2 * (u - 2 * B) + j + 1)
            else:
                used(eng, ("qk", u, j))

        def norm_job(n):
            kind, u = LN_ORDER[n]
            return ("t1" if kind == 1 else "t3", u)

        block = ctx.enter_context(nc.Block())

        @block.sync
        def _(sp):
            sp.dma_start(cT[:, :], t["cond"][:, 0:P].rearrange("b c -> c b"), allow_slow_non_contiguous=True).then_inc(c_in, 16)
            sp.dma_start(cTr[:, :], t["cond"][:, P:C].rearrange("b c -> c b"), allow_slow_non_contiguous=True).then_inc(c_in, 16)
            for b in range(B):
                sp.dma_start(x[:, b, :, :], t["x"][b].rearrange("(n p) c -> p n c", p=P)).then_inc(x_in, 16)
            for L in range(NL):
                sp.dma_start(Wada[:, L, :], t["ada"][L][0:P, :]).then_inc(ada_in, 16)
                sp.dma_start(Wadar[0:CR, L, :], t["ada"][L][P:C, :]).then_inc(ada_in, 16)
                sp.dma_start(Wadar[CR:CR + 1, L, :], t["b_ada"][L].unsqueeze(0)).then_inc(ada_in, 16)

            def load(L, dst, src):
                sp.dma_start(dst, src).then_inc(w_in[L], 16)

            def load_block(L):
                load(L, Wqkv[:, L, :], t["qkv"][L][0:P, :])
                load(L, Wqkvr[0:CR, L, :], t["qkv"][L][P:C, :])
                load(L, Wqkvr[CR:CR + 1, L, :], t["b_qkv"][L].unsqueeze(0))
                if L == 0:
                    sp.wait_ge(wp_zero, 1)
                for j in range(4):
                    load(L, Wp[32 * j:32 * j + HD, L, :, :],
                         t["proj"][L].rearrange("(q j r) n -> j r q n", q=HG, j=4)[j])
                load(L, Wp[HD:HD + 1, L, 0, :], t["b_proj"][L].unsqueeze(0))
                if L == 1:
                    load(L, Wg[:, :], t["w_gate"][0:P, :])
                    load(L, Wgr[:, :], t["w_gate"][P:C, :])
                if L == 2:
                    for s, g in enumerate(("g_q", "g_k")):
                        for k in range(8):
                            load(L, gq[HD * k:HD * k + HD, s:s + 1], t[g].unsqueeze(1))
                for e in range(EXPERTS[L]):
                    load(L, W1[L][:, e, :], t["w1"][L][e][0:P, :])
                    load(L, W1r[L][0:CR, e, :], t["w1"][L][e][P:C, :])
                    load(L, W1r[L][CR:CR + 1, e, :], t["b1"][L][e].unsqueeze(0))
                    load(L, W2[L][:, e, 0:FC, :], t["w2"][L][e][0:FC * P, :].rearrange("(c p) n -> p c n", p=P))
                    load(L, W2[L][0:FR, e, FC, :], t["w2"][L][e][FC * P:FF, :])
                    load(L, W2[L][FR:FR + 1, e, FC, :], t["b2"][L][e].unsqueeze(0))

            load_block(0)
            sp.dma_start(Wl, t["rot_w"].rearrange("(p t) c -> p t c", t=16)).then_inc(l3_in, 16)
            sp.dma_start(WTr[CR:CR + 1, :], t["rot_b"].unsqueeze(0)).then_inc(l3_in, 16)
            sp.dma_start(Pn[:, :], t["rot_p"][0:P, :]).then_inc(pt_in, 16)
            sp.dma_start(Pnr[:, :], t["rot_p"][P:C, :]).then_inc(pt_in, 16)

            def prep(u):
                L, i = u // B, u % 2
                sp.wait_ge(p1_done, 2 * u + 2)
                sp.wait_ge(p2_done, 2 * u + 2)
                sp.wait_ge(p3_done, 2 * u + 2)
                if u >= 2:
                    sp.wait_ge(stk_in[i], 16 * 2 * SLOTS * (u // 2))
                for p in range(3):
                    sp.dma_start(scr[i, p].rearrange("(k r) t -> r k t", r=CH[L]),
                                 parts[0:CH[L], p, 0:NCH[L], :]).then_inc(parts_out[i], 16)
                sp.wait_ge(parts_out[i], 16 * 3 * (u // 2 + 1))
                if u >= 2:
                    written(sp, ("e", u - 2, H // 2 - 1))
                for s, (dst, first) in enumerate(((QS[i], True), (KS[i], False))):
                    src = scr[i, :, s * C:(s + 1) * C, :].rearrange("p (h r) t -> p r h t", r=HD)
                    for slot in range(SLOTS):
                        part = ((0, 0, 1, 1, 2, 0), (0, 1, 0, 1, 0, 2))[s][slot]
                        sp.dma_start(dst[HD * slot:HD * slot + HD, :, :], src[part]).then_inc(stk_in[i], 16)

            def maxima(u):
                i = u % 2
                used(sp, ("nm", u))
                if u >= 2:
                    written(sp, ("e", u - 2, H // 2 - 1))
                sp.dma_start(nmscr[i], nmT[:, :]).then_inc(nm_out[i], 16)
                sp.wait_ge(nm_out[i], 16 * (u // 2 + 1))
                sp.dma_start(QS[i][KS_ROWS:KS_ROWS + 1, :, :], nmscr[i].unsqueeze(0)).then_inc(nm_in[i], 16)

            sp.wait_ge(consts, CONSTS)
            prep(0)
            maxima(0)
            prep(1)
            used(sp, ("vv", 3))
            sp.dma_start(vscr, vs[:, :]).then_inc(v_out, 16)
            load_block(1)
            load_block(2)
            sp.wait_ge(v_out, 16)
            sp.wait_ge(up_zero, 1)

            def skew_row(r):
                first = r * (2 * DR - 1 - r) // 2
                sp.dma_start(Up[r:r + 1, :, r + 1:DR], vscr[:, first:first + DR - 1 - r].unsqueeze(0),
                             allow_slow_non_contiguous=True).then_inc(up_in, 16)

            for u in range(NU):
                if u + 1 < NU:
                    maxima(u + 1)
                if u + 2 < NU:
                    prep(u + 2)
                for r in range(9 * u, min(9 * u + 9, DR - 1)):
                    skew_row(r)
            for b in range(B):
                used(sp, ("y", b))
                sp.dma_start(out[b].rearrange("(n p) c -> p n c", p=P), x[:, b, :, :]).then_inc(y_out, 16)
            sp.wait_ge(y_out, 16 * B)

        @block.gpsimd
        def _(pool):
            count = [0]

            def link(ins):
                count[0] += 1
                ins.then_inc(pchain, 1)
                pool.wait_ge(pchain, count[0])

            nc.gpsimd.memset(Wp[:, :, :, :], 0.0).then_inc(wp_zero, 1)

            link(nc.gpsimd.memset(ident[:, :], 0.0))
            link(nc.gpsimd.affine_select(out=ident[:, :], in_=ident[:, :], compare_op=ALU.not_equal, fill=1.0,
                                         base=0, pattern=[[-1, P]], channel_multiplier=1))
            nc.gpsimd.tensor_copy(identb[:, :], ident[:, :]).then_inc(consts, 1)
            link(nc.gpsimd.memset(pick[:, :], 1.0 / HD))
            link(nc.gpsimd.affine_select(out=pick[:, :], in_=pick[:, :], compare_op=ALU.is_ge, fill=0.0,
                                         base=0, pattern=[[-HD, 32]], channel_multiplier=1))
            nc.gpsimd.affine_select(out=pick[:, :], in_=pick[:, :], compare_op=ALU.is_ge, fill=0.0,
                                    base=HD - 1, pattern=[[HD, 32]], channel_multiplier=-1).then_inc(consts, 1)
            link(nc.gpsimd.memset(spread[:, :, :, :], 0.0))
            link(nc.gpsimd.affine_select(out=spread[:, :, :, :], in_=spread[:, :, :, :], compare_op=ALU.not_equal,
                                         fill=1.0, base=0, pattern=[[-32, 4], [-1, 8], [0, HD]],
                                         channel_multiplier=1))
            nc.gpsimd.memset(mhalf[:, :], -0.5).then_inc(consts, 1)
            nc.gpsimd.memset(phalf[:, :], 0.5).then_inc(consts, 1)
            nc.gpsimd.memset(mone[:, :], -1.0).then_inc(consts, 1)
            for tile in (hTr, h2Tr):
                nc.gpsimd.memset(tile[:, :], 1.0).then_inc(consts, 1)
            nc.gpsimd.memset(sTr[:, :], 1.0).then_inc(consts, 1)
            for i in range(2):
                nc.gpsimd.memset(V[i][:, :, :, :], 1.0).then_inc(consts, 1)
            nc.gpsimd.memset(ones[:, :], 1.0).then_inc(consts, 1)
            for k in range(SQUARINGS):
                nc.gpsimd.memset(thr[:, k:k + 1], 2.0 * 4.0 ** k).then_inc(consts, 1)
            nc.gpsimd.memset(Up[:, :, :], 0.0).then_inc(up_zero, 1)
            link(nc.gpsimd.memset(below[:, :], -1.0))
            link(nc.gpsimd.affine_select(out=below[:, :], in_=below[:, :], compare_op=ALU.is_gt, fill=0.0, base=0,
                                         pattern=[[-1, DR]], channel_multiplier=1))

            def deviation(n):
                pool.wait_ge(var_done, n + 1)
                if n >= 1:
                    pool.wait_ge(xh_ready, NT * n)
                nc.gpsimd.tensor_tensor(rstd[:, :], ve[:, :], mhalf[:, :].to_broadcast([P, NT]),
                                        ALU.pow).then_inc(rstd_done, 1)

            def prep(u):
                L = u // B
                deviation(LN_ORDER.index((1, u)))
                for j, (a, b) in enumerate(QKJ[L]):
                    pool.wait_ge(p2_done, 2 * u + j + 1)
                    remainder(pool, u, j)
                    nc.gpsimd.tensor_tensor(parts[0:CH[L], 2, a:b, :], r1[0:CH[L], a:b, :],
                                            parts[0:CH[L], 1, a:b, :], ALU.subtract).then_inc(p3_done, 1)

            def residual(n):
                u, b = n // 2, (n // 2) % B
                if n % 2 == 0:
                    used(pool, ("proj", u))
                elif u // B == 1:
                    pool.wait_ge(mixed, b + 1)
                else:
                    used(pool, ("fc2", u, 0))
                nc.gpsimd.tensor_tensor(x[:, b, :, :], x[:, b, :, :], tmp[:, :, :], ALU.add).then_inc(x_new, 1)

            def reflector(j):
                norm, sa, g, sg, dot, w = (qsc[:, k:k + 1] for k in range(1, 7))
                alpha, head = vb[:, j:j + 1], heads[:, j:j + 1]
                pool.wait_ge(sig_done, j + 1)
                link(nc.gpsimd.tensor_scalar(sg, alpha, 0.0, 2.0, ALU.is_ge, ALU.mult))
                link(nc.gpsimd.tensor_tensor(norm, qsc[:, 0:1], phalf[0:DR, :], ALU.pow))
                link(nc.gpsimd.tensor_scalar(sg, sg, -1.0, None, ALU.add))
                link(nc.gpsimd.tensor_tensor(sa, sg, norm, ALU.mult))
                link(nc.gpsimd.tensor_tensor(head, alpha, sa, ALU.add))
                link(nc.gpsimd.tensor_tensor(g, sa, head, ALU.mult))
                link(nc.gpsimd.tensor_scalar(g, g, 1e-37, None, ALU.max))
                link(nc.gpsimd.tensor_tensor(g, g, mone[:, :], ALU.pow))
                link(nc.gpsimd.tensor_tensor(g, below[:, j:j + 1], g, ALU.mult))
                link(nc.gpsimd.tensor_tensor(w, Pt[:, j:j + 1], sa, ALU.mult))
                pool.wait_ge(dot_done, j + 1)
                link(nc.gpsimd.tensor_tensor(w, w, dot, ALU.add))
                nc.gpsimd.tensor_tensor(w, w, g, ALU.mult).then_inc(w_done, 1)

            def rotation(name):
                if name[0] == "qr":
                    reflector(name[1])
                elif name == ("vqt",):
                    pool.wait_ge(qr_done, DR)
                    link(nc.gpsimd.affine_select(out=Vq[:, :], in_=Pt[:, :], compare_op=ALU.is_gt, fill=0.0, base=0,
                                                 pattern=[[1, C]], channel_multiplier=-1))
                    nc.gpsimd.affine_select(out=heads[:, :], in_=heads[:, :], compare_op=ALU.is_equal, fill=0.0, base=0,
                                            pattern=[[1, DR]], channel_multiplier=-1).then_inc(v_cut, 1)
                    pool.wait_ge(vn_done, 1)
                    nc.gpsimd.tensor_tensor(qsc[:, 6:7], qsc[:, 7:8], mhalf[0:DR, :], ALU.pow).then_inc(vg_done, 1)
                elif name == ("vvt",):
                    for s, sign in ((0, 1), (1, -1)):
                        used(pool, ("vvt",))
                        nc.gpsimd.affine_select(out=Nn[:, s, :], in_=Nn[:, s, :], compare_op=ALU.is_gt, fill=0.0,
                                                base=0, pattern=[[sign, DR]],
                                                channel_multiplier=-sign).then_inc(tri_done, 1)

            prep(0)
            prep(1)
            for u in range(NU):
                for g in range(H // 2):
                    for name in rotation_jobs(u, g):
                        rotation(name)
                residual(2 * u)
                if u + 2 < NU:
                    prep(u + 2)
                deviation(LN_ORDER.index((2, u)))
                residual(2 * u + 1)

        @block.scalar
        def _(act):
            act.wait_ge(c_in, 32)
            nc.scalar.activation(ee[:, :], cT[:, :], ACT.Exp, scale=-1.0).then_inc(achain, 1)
            nc.scalar.activation(eer[:, :], cTr[:, :], ACT.Exp, scale=-1.0).then_inc(achain, 1)

            def prep(u):
                L, i, b = u // B, u % 2, u % B
                written(act, ("t1", u))
                if u >= 1:
                    written(act, ("v", u - 1))
                nc.scalar.activation(hT[:, :], D(("t1", u))[:, 0:T], ACT.Identity,
                                     scale=mod[:, L, 1, b:b + 1], bias=mod[:, L, 0, b:b + 1])
                release(nc.scalar.activation(hTr[0:CR, :], D(("t1", u))[0:CR, T:2 * T], ACT.Identity,
                                               scale=modr[:, L, 1, b:b + 1], bias=modr[:, L, 0, b:b + 1]),
                          ("t1", u))
                c = CH[L]
                if L < 2:
                    if u >= 1:
                        act.wait_ge(parts_out[(u - 1) % 2], 16 * 3 * ((u - 1) // 2 + 1))
                    for j, (lo, hi) in enumerate(QKJ[L]):
                        name = ("qk", u, j)
                        written(act, name)
                        nc.scalar.copy(parts[0:c, 0, lo:hi, :],
                                       D(name)[0:c, 0:(hi - lo) * T].rearrange("p (k t) -> p k t", t=T)).then_inc(p1_done, 1)
                else:
                    for j, (lo, hi) in enumerate(QKJ[L]):
                        name = ("qk", u, j)
                        written(act, name)
                        if u > 2 * B:
                            written(act, ("var", u - 1))
                        src = D(name)[0:c, :].rearrange("p (k t) -> p k t", t=T)
                        nc.scalar.activation(qsq[:, lo:hi, :], src, ACT.Square).then_inc(sq_done, 1)
                        act.wait_ge(p3_done, 2 * u)
                        release(nc.scalar.activation(qn[:, lo:hi, :], src, ACT.Copy, scale=gq[:, j:j + 1]), name)
                    used(act, ("var", u))
                    if u > 2 * B:
                        written(act, ("rs", u - 1, 1))
                    nc.scalar.activation(qrs[:, :], qve[:, :], ACT.Sqrt).then_inc(qsd_done, 1)
                    act.wait_ge(parts_out[(u - 1) % 2], 16 * 3 * ((u - 1) // 2 + 1))
                    for j, (lo, hi) in enumerate(QKJ[L]):
                        used(act, ("rs", u, j))
                        nc.scalar.copy(parts[0:c, 0, lo:hi, :], qn[:, lo:hi, :]).then_inc(p1_done, 1)
                name = ("v", u)
                written(act, name)
                if u >= 2:
                    act.wait_ge(pv_step, HG * (u - 1))
                release(nc.scalar.copy(V[i][:, :, :, 0:HD],
                                         D(name)[:, 0:NT * C].rearrange("p (n h r) -> p n h r", n=NT, h=H)),
                          name)

            def maxima(u):
                name = ("nm", u)
                written(act, name)
                if u >= 1:
                    act.wait_ge(nm_out[(u - 1) % 2], 16 * ((u - 1) // 2 + 1))
                release(nc.scalar.copy(nmT[:, :], D(name)[:, :].bitcast(BF16)[0:H, 0:T]), name)

            def reflected_row(j):
                name = ("qr", j)
                written(act, name)
                if j >= 1:
                    act.wait_ge(qr_done, j)
                release(nc.scalar.copy(vb[:, j:C], D(name)[0:DR, j:C]), name)
                used(act, name)
                nc.scalar.activation(junk[:, j:C], vb[:, j:C], ACT.Square,
                                     accum_out=qsc[:, 0:1]).then_inc(sig_done, 1)

            used(act, ("ada", NL - 1))
            act.wait_ge(consts, CONSTS)
            prep(0)
            maxima(0)
            prep(1)
            written(act, ("gate", NL - 1, B - 1))
            for u in range(NU):
                L, b = u // B, u % B
                for g in range(H // 2):
                    name = ("e", u, g)
                    n = 8 * u + g
                    written(act, name)
                    if n >= NPT:
                        act.wait_ge(pv_step, (n - NPT) // 2 + 1)
                    release(nc.scalar.activation(PT[:, n % NPT, :, :], A(name)[:, :, :], ACT.Exp, scale=SCALE), name)
                    for name in rotation_jobs(u, g):
                        if name[0] == "qr":
                            reflected_row(name[1])
                if u + 1 < NU:
                    maxima(u + 1)
                if u + 2 < NU:
                    prep(u + 2)
                name = ("t3", u)
                written(act, name)
                if u >= 1:
                    written(act, hidden_jobs(u - 1)[-1])
                nc.scalar.activation(h2T[:, :], D(name)[:, 0:T], ACT.Identity,
                                     scale=mod[:, L, 4, b:b + 1], bias=mod[:, L, 3, b:b + 1])
                release(nc.scalar.activation(h2Tr[0:CR, :], D(name)[0:CR, T:2 * T], ACT.Identity,
                                               scale=modr[:, L, 4, b:b + 1], bias=modr[:, L, 3, b:b + 1]),
                          name)
                if L == 1:
                    act.wait_ge(lgm_done, b + 1)
                    nc.scalar.activation(lge[:, :, :], lg[:, :, :], ACT.Exp).then_inc(lge_done, 1)
                for k, group in enumerate(hidden_chunks(L)):
                    name = ("g", u, k)
                    e0, c0, rows = group[0]
                    n = len(group)
                    at = experts_before(u) + e0
                    written(act, name)
                    if at == 0 and k == 0:
                        act.wait_ge(v_out, 16)
                    if at >= 2 and c0 == 0:
                        written(act, fc2_job(at - 2))
                    release(nc.scalar.activation(G[0:rows, at % 2, c0:c0 + n, :], A(name)[0:rows, 0:n, :],
                                                 ACT.Gelu_apprx_tanh), name)
        @block.vector
        def _(dve):
            count = [0]

            def link(ins):
                count[0] += 1
                ins.then_inc(dchain, 1)
                dve.wait_ge(dchain, count[0])

            for i in range(2):
                nc.vector.memset(KS[i][32:KS_ROWS + 1, :, :].bitcast(U32), 0x3F803F80).then_inc(consts, 1)
            nc.vector.memset(G[FR:FR + 1, :, FC, :], 1.0).then_inc(consts, 1)
            nc.vector.memset(O[:, :], 1.0).then_inc(consts, 1)
            dve.wait_ge(achain, 2)
            dve.wait_ge(consts, CONSTS)
            link(nc.vector.tensor_scalar(ee[:, :], ee[:, :], 1.0, None, ALU.add))
            link(nc.vector.tensor_scalar(eer[:, :], eer[:, :], 1.0, None, ALU.add))
            link(nc.vector.reciprocal(ee[:, :], ee[:, :]))
            link(nc.vector.reciprocal(eer[:, :], eer[:, :]))
            link(nc.vector.tensor_tensor(sT[:, :], cT[:, :], ee[:, :], ALU.mult))
            link(nc.vector.tensor_tensor(sTr[0:CR, :], cTr[:, :], eer[:, :], ALU.mult))
            nc.vector.tensor_copy(sTb[:, :, :], sT[:, :].unsqueeze(2).to_broadcast([P, B, P])).then_inc(silu_done, 1)
            nc.vector.tensor_copy(sTrb[:, :, :],
                                  sTr[:, :].unsqueeze(2).to_broadcast([CR + 1, B, P])).then_inc(silu_done, 1)
            for L in range(NL):
                name = ("ada", L)
                written(dve, name)
                src = D(name)[:, 0:6 * B].rearrange("p (s b) -> p s b", b=B)
                srcr = D(name)[0:CR, 6 * B:12 * B].rearrange("p (s b) -> p s b", b=B)
                nc.vector.tensor_copy(mod[:, L, 0:4:3, :], src[:, 0:4:3, :])
                nc.vector.tensor_copy(modr[:, L, 0:4:3, :], srcr[:, 0:4:3, :])
                nc.vector.tensor_scalar(mod[:, L, 1:5:3, :], src[:, 1:5:3, :], 1.0, None, ALU.add)
                release(nc.vector.tensor_scalar(modr[:, L, 1:5:3, :], srcr[:, 1:5:3, :], 1.0, None, ALU.add),
                          name)
            for L in range(NL):
                for b in range(B):
                    name = ("gate", L, b)
                    written(dve, name)
                    release(nc.vector.tensor_copy(gates[:, L, b, :, :],
                                                    D(name)[:, 0:2 * C].rearrange("p (s c) -> p s c", s=2)),
                              name)
            def centre():
                dve.wait_ge(w_in[2], W_IN[2])
                for w, m in ((Wqkv, gm), (Wqkvr, gmr)):
                    wv = w[:, 2, 0:2 * C].rearrange("p (h r) -> p h r", r=HD)
                    link(nc.vector.tensor_reduce(m[:, :], wv, AX.X, ALU.add))
                    link(nc.vector.tensor_scalar(m[:, :], m[:, :], 1.0 / HD, None, ALU.mult))
                    nc.vector.tensor_tensor(wv, wv, m[:, :].unsqueeze(2).to_broadcast([w.shape[0], 2 * H, HD]),
                                            ALU.subtract).then_inc(centred, 1)

            def layer_norm(n, b):
                for k in range(NT):
                    nc.vector.bn_stats(stats[:, k, :], x[:, b, k, :]).then_inc(dchain, 1)
                count[0] += NT
                dve.wait_ge(dchain, count[0])
                for k in range(NT):
                    nc.vector.bn_aggr(mv[:, k, :], stats[:, k, :]).then_inc(dchain, 1)
                count[0] += NT
                dve.wait_ge(dchain, count[0])
                nc.vector.tensor_scalar(ve[:, :], mv[:, :, 1], EPS, None, ALU.add).then_inc(var_done, 1)
                dve.wait_ge(rstd_done, n + 1)
                if n >= 1:
                    written(dve, norm_job(n - 1))
                for k in range(NT):
                    nc.vector.tensor_scalar(xh[:, k, :], x[:, b, k, :], mv[:, k, 0:1], rstd[:, k:k + 1],
                                            ALU.subtract, ALU.mult).then_inc(xh_ready, 1)

            def ln_no(kind, u):
                return LN_ORDER.index((kind, u))

            def prep(u):
                L, b = u // B, u % B
                if u < B:
                    dve.wait_ge(x_in, 16 * B)
                else:
                    dve.wait_ge(x_new, 2 * (u - B) + 2)
                layer_norm(ln_no(1, u), b)
                if u == 2 * B:
                    centre()
                c = CH[L]
                if L == 2:
                    name = ("var", u)
                    written(dve, name)
                    if u > 2 * B:
                        dve.wait_ge(qrs_done, u - 2 * B)
                    release(nc.vector.tensor_scalar(qve[:, :], D(name)[:, 0:T], EPS, None, ALU.add), name)
                    dve.wait_ge(qsd_done, u - 2 * B + 1)
                    link(nc.vector.reciprocal(qrs[:, :], qrs[:, :]))
                    link(nc.vector.tensor_tensor(qt[:, :], qrs[:, :], qrs[:, :], ALU.mult))
                    link(nc.vector.scalar_tensor_tensor(qt[:, :], qt[:, :], -0.5, qve[:, :], ALU.mult, ALU.mult))
                    nc.vector.scalar_tensor_tensor(qrs[:, :], qt[:, :], 1.5, qrs[:, :], ALU.add,
                                                   ALU.mult).then_inc(qrs_done, 1)
                    for j, (lo, hi) in enumerate(QKJ[L]):
                        name = ("rs", u, j)
                        written(dve, name)
                        used(dve, ("qk", u, j))
                        release(nc.vector.tensor_tensor(
                            qn[:, lo:hi, :], qn[:, lo:hi, :], D(name)[0:c, :].rearrange("p (k t) -> p k t", t=T),
                            ALU.mult), name)
                for j, (lo, hi) in enumerate(QKJ[L]):
                    dve.wait_ge(p1_done, 2 * u + j + 1)
                    if u >= 1:
                        dve.wait_ge(p3_done, 2 * u)
                    if L < 2:
                        name = ("qk", u, j)
                        ins = nc.vector.tensor_tensor(
                            r1[0:c, lo:hi, :], D(name)[0:c, 0:(hi - lo) * T].rearrange("p (k t) -> p k t", t=T),
                            parts[0:c, 0, lo:hi, :], ALU.subtract)
                        release(ins, name)
                    else:
                        used(dve, ("rs", u, j))
                        nc.vector.tensor_tensor(r1[0:c, lo:hi, :], qn[0:c, lo:hi, :], parts[0:c, 0, lo:hi, :],
                                                ALU.subtract).then_inc(r1_done, 1)
                    remainder(dve, u, j)
                    if u >= 1:
                        dve.wait_ge(parts_out[(u - 1) % 2], 16 * 3 * ((u - 1) // 2 + 1))
                    nc.vector.tensor_copy(parts[0:c, 1, lo:hi, :], r1[0:c, lo:hi, :]).then_inc(p2_done, 1)

            def maxima(u, h):
                name = ("s", u, h)
                written(dve, name)
                if u >= 2 and h == 0:
                    written(dve, ("nm", u - 2))
                release(nc.vector.tensor_reduce(nm[u % 2][:, :, h], D(name)[:, :].rearrange("p (n k) -> p n k", n=NT),
                                                  AX.X, ALU.max, negate=True), name)

            def gated(n, src, gate):
                if n >= 1:
                    dve.wait_ge(x_new, n)
                return nc.vector.tensor_tensor(tmp[:, :, :], src,
                                               gate.unsqueeze(1).to_broadcast([P, NT, C]), ALU.mult)

            def divide(u, q):
                n = HG * u + q
                dve.wait_ge(pv_step, n + 1)
                nc.vector.transpose(ob[:, :], O[:, :]).then_inc(o_read, 1)
                dve.wait_ge(o_read, n + 1)
                blocks = ob[:, :].rearrange("p (k r) -> p k r", r=32)
                link(nc.vector.reciprocal(rden[:, :], blocks[:, :, HD]))
                link(nc.vector.tensor_tensor(blocks, blocks, rden[:, :].unsqueeze(2).to_broadcast([P, T // 32, 32]),
                                             ALU.mult))
                if u >= 1:
                    written(dve, ("proj", u - 1))
                nc.vector.transpose(oT[:, q, :], ob[:, :]).then_inc(oT_done, 1)
                dve.wait_ge(oT_done, n + 1)

            WTv = WT[:, :].rearrange("c (p t) -> c t p", t=16)
            WTrv = WTr[0:CR, :].rearrange("c (p t) -> c t p", t=16)
            idb = ident[0:DR, 0:DR].unsqueeze(1).to_broadcast([DR, B, DR])

            def skew_vectors(name):
                written(dve, name)
                if name[0] == "wt":
                    q = name[1] // 2
                    dst, rows = ((WTv, P), (WTrv, CR))[name[1] % 2]
                    ins = nc.vector.tensor_copy(dst[:, 4 * q:4 * q + 4, :],
                                                D(name)[0:rows, 0:504].rearrange("c (t p) -> c t p", t=4))
                elif name[0] == "vv":
                    q = name[1]
                    ins = nc.vector.tensor_copy(vs[:, 504 * q:504 * q + 504], D(name)[0:B, 0:504])
                else:
                    ins = nc.vector.tensor_copy(Pt[:, :], D(name)[0:DR, 0:C])
                release(ins, name)

            def update_rows(j):
                dve.wait_ge(w_done, j + 1)
                nc.vector.scalar_tensor_tensor(Pt[:, j + 1:C], vb[:, j + 1:C], qsc[:, 6:7], Pt[:, j + 1:C], ALU.mult,
                                               ALU.add).then_inc(qr_done, 1)

            def exponential(name):
                kind = name[0]
                d = D(name)[0:DR, :]
                if kind == "ut":
                    written(dve, name)
                    release(nc.vector.tensor_tensor(Ask[:, :, :], Up[:, :, :],
                                                    d[:, 0:256].rearrange("p (b j) -> p b j", b=B), ALU.subtract),
                            name)
                    used(dve, name)
                    link(nc.vector.tensor_tensor(Asq[:, :, :], Ask[:, :, :], Ask[:, :, :], ALU.mult))
                    nc.vector.tensor_reduce(fr[:, :], Asq[:, :, :], AX.X, ALU.add).then_inc(fr_done, 1)
                elif kind == "fro":
                    written(dve, name)
                    release(nc.vector.tensor_copy(frb[:, :], d[:, 0:B]), name)
                    used(dve, name)
                    link(nc.vector.tensor_tensor(need[:, :, :],
                                                 frb[:, :].unsqueeze(2).to_broadcast([DR, B, SQUARINGS]),
                                                 thr[:, :].unsqueeze(1).to_broadcast([DR, B, SQUARINGS]), ALU.is_gt))
                    for s in range(2):
                        link(nc.vector.tensor_copy(needu[:, :, s, :], need[:, :, :].rearrange("p b k -> p k b")))
                    link(nc.vector.tensor_scalar(fac[:, :, :], need[:, :, :], -0.5, 1.0, ALU.mult, ALU.add))
                    n = SQUARINGS // 2
                    while n >= 1:
                        link(nc.vector.tensor_tensor(fac[:, :, 0:n], fac[:, :, 0:n], fac[:, :, n:2 * n], ALU.mult))
                        n //= 2
                    nc.vector.tensor_tensor(X[:, :, :], Ask[:, :, :], fac[:, :, 0:1].to_broadcast([DR, B, DR]),
                                            ALU.mult).then_inc(X_done, 1)
                    dve.wait_ge(X_done, 1)
                    nc.vector.scalar_tensor_tensor(E0[:, :, :], X[:, :, :], 1.0 / TAYLOR, idb, ALU.mult,
                                                   ALU.add).then_inc(E_done, 1)
                elif kind == "tay":
                    k = name[1]
                    dst = Z[:, 0:B, :] if k == TAYLOR - 2 else E0[:, :, :]
                    written(dve, name)
                    release(nc.vector.scalar_tensor_tensor(
                        dst, d[:, 0:B * DR].rearrange("p (b j) -> p b j", b=B), -1.0 / (TAYLOR - 1 - k), idb,
                        ALU.mult, ALU.add), name)
                elif kind == "ft":
                    written(dve, name)
                    release(nc.vector.tensor_copy(Z[:, B:2 * B, :], d[:, 0:B * DR].rearrange("p (b j) -> p b j", b=B)),
                            name)
                elif kind == "sq":
                    k = name[1]
                    written(dve, name)
                    release(nc.vector.copy_predicated(
                        Z[:, :, :],
                        needu[:, k, :, :].rearrange("p s b -> p (s b)").unsqueeze(2).to_broadcast([DR, 2 * B, DR]),
                        d.rearrange("p (b j) -> p b j", j=DR)), name)
                    if k == SQUARINGS - 1:
                        used(dve, name)
                        nc.vector.tensor_tensor(FmI[:, :, :], Z[:, B:2 * B, :], idb, ALU.subtract).then_inc(F_done, 1)

            def orthonormal(name):
                kind = name[0]
                d = D(name)
                if kind == "vqt":
                    written(dve, name)
                    nc.vector.tensor_copy(VqT[:, :], d[:, 0:DR])
                    release(nc.vector.tensor_copy(VqTr[:, :], d[0:CR, DR:2 * DR]), name)
                elif kind == "vvt":
                    written(dve, name)
                    nc.vector.tensor_copy(Nn[:, 0, :], d[0:DR, 0:DR])
                    release(nc.vector.tensor_copy(Nn[:, 1, :], d[0:DR, 0:DR]), name)
                    dve.wait_ge(tri_done, 2)
                    nc.vector.tensor_tensor(Tn[:, :], ident[0:DR, 0:DR], Nn[:, 0, :], ALU.subtract).then_inc(N_done, 1)
                elif kind == "nn":
                    written(dve, name)
                    dve.wait_ge(N_done, 1)
                    release(nc.vector.tensor_copy(Nn[:, :, :], d[0:DR, 0:2 * DR].rearrange("p (s j) -> p s j", s=2)),
                            name)
                elif kind == "tn":
                    written(dve, name)
                    release(nc.vector.tensor_tensor(Tn[:, :], Tn[:, :], d[0:DR, 0:DR], ALU.add), name)
                elif kind == "kk":
                    written(dve, name)
                    release(nc.vector.tensor_copy(Kq[:, :], d[0:DR, 0:C]), name)
                elif kind == "uu":
                    written(dve, name)
                    nc.vector.tensor_scalar(Ut[:, DR:C], d[0:DR, DR:C], -1.0, None, ALU.mult)
                    release(nc.vector.tensor_tensor(Ut[:, 0:DR], ident[0:DR, 0:DR], d[0:DR, 0:DR], ALU.subtract), name)
                elif kind == "gm":
                    k = name[1]
                    written(dve, name)
                    release(nc.vector.tensor_copy(Gm[:, 2 * k:2 * k + 2, :],
                                                  d[0:DR, 0:2 * C].rearrange("p (b c) -> p b c", b=2)), name)
                elif kind == "m":
                    b = name[1]
                    written(dve, name)
                    nc.vector.tensor_copy(M[:, b, :], d[:, 0:C])
                    release(nc.vector.tensor_copy(Mr[:, b, :], d[0:CR, C:2 * C]), name)

            def reflectors():
                dve.wait_ge(v_cut, 1)
                link(nc.vector.tensor_tensor(Vq[:, 0:DR], Vq[:, 0:DR], heads[:, :], ALU.add))
                link(nc.vector.tensor_tensor_reduce(out=junk2[:, :], in0=Vq[:, :], in1=Vq[:, :], scale=0.5,
                                                    scalar=1e-37, op0=ALU.mult, op1=ALU.add,
                                                    accum_out=qsc[:, 3:4]))
                nc.vector.tensor_copy(qsc[:, 7:8], qsc[:, 3:4]).then_inc(vn_done, 1)
                dve.wait_ge(vg_done, 1)
                nc.vector.tensor_scalar(Vq[:, :], Vq[:, :], qsc[:, 6:7], None, ALU.mult).then_inc(qr_done, 1)

            def rotate(b):
                name = ("t4", b)
                written(dve, name)
                if b >= 1:
                    written(dve, ("y", b - 1))
                nc.vector.tensor_copy(xT[:, :], D(name)[:, 0:T])
                release(nc.vector.tensor_copy(xTr[:, :], D(name)[0:CR, T:2 * T]), name)
                name = ("y", b)
                written(dve, name)
                release(nc.vector.tensor_tensor(x[:, b, :, :], D(name)[:, 0:NT * C].rearrange("p (n c) -> p n c", n=NT),
                                                x[:, b, :, :], ALU.add), name)

            def rotation(name):
                kind = name[0]
                if kind == "qr":
                    j = name[1]
                    dve.wait_ge(sig_done, j + 1)
                    nc.vector.tensor_tensor_reduce(out=junk2[:, j:C], in0=Pt[:, j:C], in1=vb[:, j:C], scale=1.0,
                                                   scalar=0.0, op0=ALU.mult, op1=ALU.add,
                                                   accum_out=qsc[:, 5:6]).then_inc(dot_done, 1)
                elif name in EXP_JOBS:
                    exponential(name)
                else:
                    orthonormal(name)

            prep(0)
            for h in range(H):
                maxima(0, h)
                for name in V_JOBS[h:h + 1]:
                    skew_vectors(name)
            prep(1)
            for u in range(NU):
                L, b = u // B, u % B
                for g in range(H // 2):
                    if u + 1 < NU:
                        maxima(u + 1, 2 * g)
                    n = H // 2 * u + g
                    if 1 <= n <= DR:
                        update_rows(n - 1)
                    if n == DR:
                        reflectors()
                    if u + 1 < NU:
                        maxima(u + 1, 2 * g + 1)
                    for name in rotation_jobs(u, g):
                        rotation(name)
                    if g in DIVIDE_AT:
                        divide(u, DIVIDE_AT[g])
                divide(u, HG - 1)
                name = ("proj", u)
                written(dve, name)
                release(gated(2 * u, D(name)[:, 0:NT * C].rearrange("p (n c) -> p n c", n=NT),
                              gates[:, L, b, 0, :]), name)
                if u + 2 < NU:
                    prep(u + 2)
                if u == NU - 1:
                    for k in range(B - 1):
                        rotate(k)
                dve.wait_ge(x_new, 2 * u + 1)
                layer_norm(ln_no(2, u), b)
                if L == 1:
                    name = ("gl", u)
                    written(dve, name)
                    if b >= 1:
                        dve.wait_ge(lge_done, b)
                    gl = D(name)[:, 0:NT * NE].rearrange("p (n e) -> p n e", n=NT)
                    release(nc.vector.tensor_copy(lraw[:, :, :], gl), name)
                    used(dve, name)
                    link(nc.vector.tensor_reduce(lgm[:, :], lraw[:, :, :], AX.X, ALU.max))
                    nc.vector.tensor_tensor(lg[:, :, :], lraw[:, :, :],
                                            lgm[:, :].unsqueeze(2).to_broadcast([P, NT, NE]),
                                            ALU.subtract).then_inc(lgm_done, 1)
                    dve.wait_ge(lgm_done, b + 1)
                    link(nc.vector.memset(cmpt[:, :, :, :], 0.0))
                    n_cmp = 0
                    for f in range(NE):
                        for lo, hi, op in ((0, f, ALU.is_gt), (f + 1, NE, ALU.is_ge)):
                            if hi > lo:
                                nc.vector.tensor_tensor(
                                    cmpt[:, :, lo:hi, f], lraw[:, :, f:f + 1].to_broadcast([P, NT, hi - lo]),
                                    lraw[:, :, lo:hi], op).then_inc(dchain, 1)
                                n_cmp += 1
                    count[0] += n_cmp
                    dve.wait_ge(dchain, count[0])
                    link(nc.vector.tensor_reduce(rank[:, :, :], cmpt[:, :, :, :], AX.X, ALU.add))
                    dve.wait_ge(lge_done, b + 1)
                    link(nc.vector.scalar_tensor_tensor(cwt[:, :, :], rank[:, :, :], 1.5, lge[:, :, :],
                                                        ALU.is_lt, ALU.mult))
                    link(nc.vector.tensor_reduce(den[:, :], cwt[:, :, :], AX.X, ALU.add))
                    link(nc.vector.reciprocal(den[:, :], den[:, :]))
                    link(nc.vector.tensor_tensor(cw[:, :, :], cwt[:, :, :],
                                                 den[:, :].unsqueeze(2).to_broadcast([P, NT, NE]), ALU.mult))
                    for e in range(NE):
                        name = ("fc2", u, e)
                        written(dve, name)
                        for k in range(NT):
                            src = D(name)[:, k * C:(k + 1) * C]
                            if e == 0:
                                ins = nc.vector.tensor_scalar(acc[:, k, :], src, cw[:, k, e:e + 1], None, ALU.mult)
                            else:
                                ins = nc.vector.scalar_tensor_tensor(acc[:, k, :], src, cw[:, k, e:e + 1],
                                                                     acc[:, k, :], ALU.mult, ALU.add)
                        release(ins, name)
                        used(dve, name)
                    gated(2 * u + 1, acc[:, :, :], gates[:, L, b, 1, :]).then_inc(mixed, 1)
                else:
                    name = ("fc2", u, 0)
                    written(dve, name)
                    release(gated(2 * u + 1, D(name)[:, 0:NT * C].rearrange("p (n c) -> p n c", n=NT),
                                  gates[:, L, b, 1, :]), name)

            dve.wait_ge(x_new, 2 * NU)
            rotate(B - 1)

        @block.tensor
        def _(pe):
            mm = nc.tensor.matmul
            issued = {"d": 0, "a": 0}

            def d_take(name):
                n = d_no[name]
                assert n == issued["d"], (name, n, issued["d"], d_order[issued["d"]])
                issued["d"] += 1
                if n >= ND:
                    pe.wait_ge(d_free[n % ND], n // ND)
                return D_ring[n % ND]

            def d_give(ins, name):
                return ins.then_inc(d_full[d_no[name] % ND], 1)

            def a_take(name):
                n = a_no[name]
                assert n == issued["a"]
                issued["a"] += 1
                if n >= NA:
                    pe.wait_ge(a_free[n % NA], n // NA)
                return A_ring[n % NA]

            def a_give(ins, name):
                return ins.then_inc(a_full[a_no[name] % NA], 1)

            pe.wait_ge(consts, CONSTS)
            pe.wait_ge(ada_in, 16 * 9)
            pe.wait_ge(silu_done, 2)
            for L in range(NL):
                name = ("ada", L)
                d = d_take(name)
                for s in (0, 1, 3, 4):
                    for lo, rows, col in ((0, P, 0), (P, CR, 6 * B)):
                        o = d[0:rows, col + s * B:col + (s + 1) * B]
                        mm(o, Wada[:, L, s * C + lo:s * C + lo + rows], sT[:, :], start=True, stop=False)
                        last = mm(o, Wadar[:, L, s * C + lo:s * C + lo + rows], sTr[:, :], start=False, stop=True)
                d_give(last, name)
            for L in range(NL):
                for b in range(B):
                    name = ("gate", L, b)
                    d = d_take(name)
                    for k, s in enumerate((2, 5)):
                        o = d[:, k * C:(k + 1) * C]
                        mm(o, sTb[:, b, :], Wada[:, L, s * C:(s + 1) * C], start=True, stop=False)
                        last = mm(o, sTrb[:, b, :], Wadar[:, L, s * C:(s + 1) * C], start=False, stop=True)
                    d_give(last, name)

            def transposed(name, src, ready, value):
                d = d_take(name)
                pe.wait_ge(ready, value)
                for k in range(NT):
                    nc.tensor.transpose(d[:, k * P:(k + 1) * P], src[:, k, 0:P], ident[:, :])
                    last = nc.tensor.transpose(d[0:CR, T + k * P:T + (k + 1) * P], src[:, k, P:C], ident[:, :])
                d_give(last, name)

            def prep(u):
                L, i = u // B, u % 2
                transposed(("t1", u), xh, xh_ready, NT * (LN_ORDER.index((1, u)) + 1))
                if u % B == 0:
                    pe.wait_ge(w_in[L], W_IN[L])
                if u == 2 * B:
                    pe.wait_ge(centred, 2)
                used(pe, ("t1", u))
                c = CH[L]
                for j, (lo, hi) in enumerate(QKJ[L]):
                    name = ("qk", u, j)
                    d = d_take(name)
                    for k in range(lo, hi):
                        o = d[0:c, (k - lo) * T:(k - lo + 1) * T]
                        mm(o, Wqkv[:, L, k * c:(k + 1) * c], hT[:, :], start=True, stop=False)
                        last = mm(o, Wqkvr[:, L, k * c:(k + 1) * c], hTr[:, :], start=False, stop=True)
                    d_give(last, name)
                if L == 2:
                    name = ("var", u)
                    d = d_take(name)
                    for k in range(4):
                        pe.wait_ge(sq_done, 2 * (u - 2 * B) + k // 2 + 1)
                        last = mm(d[32 * k:32 * k + 32, 0:T], pick[:, :], qsq[:, k, :], start=True, stop=True)
                    d_give(last, name)
                    for j, (lo, hi) in enumerate(QKJ[L]):
                        name = ("rs", u, j)
                        d = d_take(name)
                        pe.wait_ge(qrs_done, u - 2 * B + 1)
                        for k in range(lo, hi):
                            last = mm(d[0:c, (k - lo) * T:(k - lo + 1) * T],
                                      spread[:, k, :, :].rearrange("p k r -> p (k r)"), qrs[:, :],
                                      start=True, stop=True)
                        d_give(last, name)
                name = ("v", u)
                d = d_take(name)
                for k in range(NT):
                    o = d[:, k * C:(k + 1) * C]
                    mm(o, hT[:, k * P:(k + 1) * P], Wqkv[:, L, 2 * C:3 * C], start=True, stop=False)
                    last = mm(o, hTr[:, k * P:(k + 1) * P], Wqkvr[:, L, 2 * C:3 * C], start=False, stop=True)
                d_give(last, name)

            def scores(u, h):
                i = u % 2
                if h == 0:
                    pe.wait_ge(stk_in[i], 16 * 2 * SLOTS * (u // 2 + 1))
                name = ("s", u, h)
                d = d_take(name)
                for k in range(NT):
                    last = mm(d[:, k * T:(k + 1) * T], QS[i][0:KS_ROWS, h, k * P:(k + 1) * P],
                              KS[i][0:KS_ROWS, h, :], start=True, stop=True)
                d_give(last, name)

            def maxima(u):
                name = ("nm", u)
                d = d_take(name)
                used(pe, ("s", u, H - 1))
                db = d[:, :].bitcast(BF16)
                for k in range(NT):
                    last = nc.tensor.transpose(db[0:H, k * P:(k + 1) * P], nm[u % 2][:, k, :], identb[:, :])
                d_give(last, name)

            def weights(u, g):
                i = u % 2
                if g == 0:
                    pe.wait_ge(nm_in[i], 16 * (u // 2 + 1))
                name = ("e", u, g)
                a = a_take(name)
                for hh in range(2):
                    for k in range(NT):
                        last = mm(a[:, 2 * hh + k, :], KS[i][:, 2 * g + hh, k * P:(k + 1) * P],
                                  QS[i][:, 2 * g + hh, :], start=True, stop=True)
                a_give(last, name)

            def values(u, q):
                n = HG * u + q
                used(pe, ("e", u, 2 * q + 1))
                if q == 0:
                    used(pe, ("v", u))
                if n >= 1:
                    pe.wait_ge(o_read, n)
                for k in range(NT):
                    for j in range(4):
                        last = mm(O[32 * j:32 * j + HD + 1, :], V[u % 2][:, k, 4 * q + j, :],
                                  PT[:, (2 * n + j // 2) % NPT, 2 * (j % 2) + k, :], start=k == 0, stop=k == NT - 1)
                last.then_inc(pv_step, 1)

            def skew_vectors(name):
                if name == ("wt", 0):
                    pe.wait_ge(l3_in, 32)
                if name[0] == "pt":
                    pe.wait_ge(pt_in, 32)
                if name[0] == "vv":
                    used(pe, ("wt", 7))
                d = d_take(name)
                if name[0] == "wt":
                    q = name[1] // 2
                    lo, rows = ((0, P), (P, CR))[name[1] % 2]
                    for j in range(4):
                        last = nc.tensor.transpose(d[0:rows, 126 * j:126 * j + 126], Wl[:, 4 * q + j, lo:lo + rows],
                                                   ident[0:126, 0:126])
                elif name[0] == "vv":
                    cols = slice(504 * name[1], 504 * name[1] + 504)
                    mm(d[0:B, 0:504], sT[:, :], WT[:, cols], start=True, stop=False)
                    last = mm(d[0:B, 0:504], sTr[:, :], WTr[:, cols], start=False, stop=True)
                else:
                    nc.tensor.transpose(d[0:DR, 0:P], Pn[:, :], ident[:, :])
                    last = nc.tensor.transpose(d[0:DR, P:C], Pnr[:, :], ident[0:CR, 0:CR])
                d_give(last, name)

            def rotation(name):
                kind = name[0]
                if kind == "qr":
                    if name[1] == 0:
                        used(pe, ("pt",))
                    else:
                        pe.wait_ge(qr_done, name[1])
                elif kind == "ut":
                    pe.wait_ge(up_in, 16 * (DR - 1))
                elif kind == "fro":
                    pe.wait_ge(fr_done, 1)
                elif kind == "tay":
                    if name[1] == 0:
                        pe.wait_ge(E_done, 1)
                    else:
                        used(pe, ("tay", name[1] - 1))
                elif kind == "ft":
                    used(pe, ("tay", TAYLOR - 2))
                elif kind == "sq":
                    used(pe, ("sq", name[1] - 1) if name[1] else ("ft",))
                elif kind == "vqt":
                    pe.wait_ge(qr_done, DR + 1)
                elif kind == "vvt":
                    used(pe, ("vqt",))
                elif kind == "nn":
                    if name[1]:
                        used(pe, ("nn", name[1] - 1))
                    else:
                        pe.wait_ge(tri_done, 2)
                elif kind == "tn":
                    used(pe, ("nn", name[1]))
                    if name[1]:
                        used(pe, ("tn", name[1] - 1))
                    else:
                        pe.wait_ge(N_done, 1)
                elif kind == "kk":
                    used(pe, ("tn", 4))
                elif kind == "uu":
                    used(pe, ("kk",))
                elif kind == "gm":
                    used(pe, ("uu",))
                    pe.wait_ge(F_done, 1)
                elif kind == "m":
                    used(pe, ("gm", name[1] // 2))
                d = d_take(name)
                dd = d[0:DR, :]
                if kind == "qr":
                    j = name[1]
                    last = mm(dd[:, j:C], ident[0:DR, j:j + 1].to_broadcast([DR, DR]), Pt[:, j:C],
                              start=True, stop=True)
                elif kind == "ut":
                    for b in range(B):
                        last = nc.tensor.transpose(dd[:, b * DR:(b + 1) * DR], Up[:, b, :], ident[0:DR, 0:DR])
                elif kind == "fro":
                    last = mm(dd[:, 0:B], ones[:, :], fr[:, :], start=True, stop=True)
                elif kind == "tay":
                    for b in range(B):
                        last = mm(dd[:, b * DR:(b + 1) * DR], X[:, b, :], E0[:, b, :], start=True, stop=True)
                elif kind == "ft":
                    for b in range(B):
                        last = nc.tensor.transpose(dd[:, b * DR:(b + 1) * DR], Z[:, b, :], ident[0:DR, 0:DR])
                elif kind == "sq":
                    for b in range(2 * B):
                        last = mm(dd[:, b * DR:(b + 1) * DR], Z[:, (b + B) % (2 * B), :], Z[:, b, :],
                                  start=True, stop=True)
                elif kind == "vqt":
                    nc.tensor.transpose(d[:, 0:DR], Vq[:, 0:P], ident[0:DR, 0:DR])
                    last = nc.tensor.transpose(d[0:CR, DR:2 * DR], Vq[:, P:C], ident[0:DR, 0:DR])
                elif kind == "vvt":
                    mm(dd[:, 0:DR], VqT[:, :], VqT[:, :], start=True, stop=False)
                    last = mm(dd[:, 0:DR], VqTr[:, :], VqTr[:, :], start=False, stop=True)
                elif kind == "nn":
                    mm(dd[:, 0:DR], Nn[:, 1, :], Nn[:, 0, :], start=True, stop=True)
                    last = mm(dd[:, DR:2 * DR], Nn[:, 0, :], Nn[:, 1, :], start=True, stop=True)
                elif kind == "tn":
                    last = mm(dd[:, 0:DR], Nn[:, 1, :], Tn[:, :], start=True, stop=True)
                elif kind == "kk":
                    last = mm(dd[:, 0:C], Tn[:, :], Vq[:, :], start=True, stop=True)
                elif kind == "uu":
                    last = mm(dd[:, 0:C], Vq[:, 0:DR], Kq[:, :], start=True, stop=True)
                elif kind == "gm":
                    for j in range(2):
                        last = mm(dd[:, j * C:(j + 1) * C], FmI[:, 2 * name[1] + j, :], Ut[:, :],
                                  start=True, stop=True)
                elif kind == "m":
                    mm(d[:, 0:C], Ut[:, 0:P], Gm[:, name[1], :], start=True, stop=True)
                    last = mm(d[0:CR, C:2 * C], Ut[:, P:C], Gm[:, name[1], :], start=True, stop=True)
                d_give(last, name)

            def rotate(b):
                transposed(("t4", b), x[:, b, :, :], x_new, 2 * (NU - B + b) + 2)
                name = ("y", b)
                d = d_take(name)
                used(pe, ("t4", b))
                used(pe, ("m", b))
                for k in range(NT):
                    o = d[:, k * C:(k + 1) * C]
                    mm(o, xT[:, k * P:(k + 1) * P], M[:, b, :], start=True, stop=False)
                    last = mm(o, xTr[:, k * P:(k + 1) * P], Mr[:, b, :], start=False, stop=True)
                d_give(last, name)

            prep(0)
            for h in range(H):
                scores(0, h)
                for name in V_JOBS[h:h + 1]:
                    skew_vectors(name)
            maxima(0)
            prep(1)
            for u in range(NU):
                L = u // B
                for g in range(H // 2):
                    weights(u, g)
                    if u + 1 < NU:
                        scores(u + 1, 2 * g)
                        scores(u + 1, 2 * g + 1)
                    for name in rotation_jobs(u, g):
                        rotation(name)
                    if g % 2 == 0 and g >= 2:
                        values(u, g // 2 - 1)
                values(u, HG - 1)
                if u + 1 < NU:
                    maxima(u + 1)
                name = ("proj", u)
                d = d_take(name)
                pe.wait_ge(oT_done, HG * (u + 1))
                for k in range(NT):
                    for q in range(HG):
                        last = mm(d[:, k * C:(k + 1) * C], oT[:, q, k * P:(k + 1) * P], Wp[:, L, q, :],
                                  start=q == 0, stop=q == HG - 1)
                d_give(last, name)
                if u + 2 < NU:
                    prep(u + 2)
                if u == NU - 1:
                    for b in range(B - 1):
                        rotate(b)
                transposed(("t3", u), xh, xh_ready, NT * (LN_ORDER.index((2, u)) + 1))
                used(pe, ("t3", u))
                if L == 1:
                    name = ("gl", u)
                    d = d_take(name)
                    for k in range(NT):
                        o = d[:, k * NE:(k + 1) * NE]
                        mm(o, h2T[:, k * P:(k + 1) * P], Wg[:, :], start=True, stop=False)
                        last = mm(o, h2Tr[0:CR, k * P:(k + 1) * P], Wgr[:, :], start=False, stop=True)
                    d_give(last, name)
                groups = hidden_chunks(L)

                def fc1(e):
                    for k in (2 * e, 2 * e + 1):
                        name = ("g", u, k)
                        a = a_take(name)
                        for j, (e, c, rows) in enumerate(groups[k]):
                            mm(a[0:rows, j, :], W1[L][:, e, c * P:c * P + rows], h2T[:, :], start=True, stop=False)
                            last = mm(a[0:rows, j, :], W1r[L][:, e, c * P:c * P + rows], h2Tr[:, :],
                                      start=False, stop=True)
                        a_give(last, name)

                fc1(0)
                for e in range(EXPERTS[L]):
                    if e + 1 < EXPERTS[L]:
                        fc1(e + 1)
                    at = experts_before(u) + e
                    name = ("fc2", u, e)
                    d = d_take(name)
                    used(pe, ("g", u, 2 * e + 1))
                    for k in range(NT):
                        o = d[:, k * C:(k + 1) * C]
                        for c in range(FC + 1):
                            rows = P if c < FC else FR + 1
                            last = mm(o, G[0:rows, at % 2, c, k * P:(k + 1) * P], W2[L][0:rows, e, c, :],
                                      start=c == 0, stop=c == FC)
                    d_give(last, name)
            rotate(B - 1)


def build(nc, aps, out):
    t = {"x": aps["x"], "cond": aps["cond_1152"]}
    t["ada"] = [aps["L0_cond_W_ada"], aps["L1_cond_w_adaln"], aps["L2_cond_w_mod"]]
    t["b_ada"] = [aps["L0_cond_b_ada"], aps["L1_cond_b_adaln"], aps["L2_cond_b_mod"]]
    t["qkv"] = [aps["L0_cond_W_qkv"], aps["L1_cond_w_qkv"], aps["L2_cond_w_qkv"]]
    t["b_qkv"] = [aps[f"L{L}_cond_b_qkv"] for L in range(3)]
    t["proj"] = [aps["L0_cond_W_proj"], aps["L1_cond_w_proj"], aps["L2_cond_w_proj"]]
    t["b_proj"] = [aps[f"L{L}_cond_b_proj"] for L in range(3)]
    t["w1"] = [[aps["L0_cond_W_fc1"]], [aps["L1_cond_w1"][e] for e in range(4)], [aps["L2_cond_w1"]]]
    t["b1"] = [[aps["L0_cond_b_fc1"]], [aps["L1_cond_b1"][e] for e in range(4)], [aps["L2_cond_b1"]]]
    t["w2"] = [[aps["L0_cond_W_fc2"]], [aps["L1_cond_w2"][e] for e in range(4)], [aps["L2_cond_w2"]]]
    t["b2"] = [[aps["L0_cond_b_fc2"]], [aps["L1_cond_b2"][e] for e in range(4)], [aps["L2_cond_b2"]]]
    t["w_gate"] = aps["L1_cond_w_gate"]
    t["g_q"], t["g_k"] = aps["L2_cond_g_q"], aps["L2_cond_g_k"]
    t["rot_p"], t["rot_w"], t["rot_b"] = aps["L3_cond_P"], aps["L3_cond_W"], aps["L3_cond_b"]
    cond_sequence_kernel(nc, t, out)


def kernel(**inputs):
    import numpy as _np
    import concourse.bacc as _bacc
    from concourse import mybir as _mybir
    from concourse.bass_utils import run_bass_kernel_spmd as _run

    nc = _bacc.Bacc("TRN2", target_bir_lowering=False, num_devices=1)
    arrays, aps = {}, {}
    for name, value in inputs.items():
        a = _np.ascontiguousarray(value)
        arrays[f"in_{name}_dram"] = a
        aps[name] = nc.dram_tensor(f"in_{name}_dram", a.shape, _mybir.dt.from_np(a.dtype), kind="ExternalInput").ap()
    out = nc.dram_tensor("out_0_dram", (4, 256, 144), _mybir.dt.float32, kind="ExternalOutput").ap()
    build(nc, aps, out)
    r = _run(nc, [arrays], core_ids=[0])
    return r.results[0]["out_0_dram"]
```

```python
import concourse.bass as bass
from concourse import mybir
from contextlib import ExitStack


def cond_sequence_kernel(nc, t, out):
    F32 = mybir.dt.float32
    BF16 = mybir.dt.bfloat16
    U32 = mybir.dt.uint32
    ALU = mybir.AluOpType
    ACT = mybir.ActivationFunctionType
    AX = mybir.AxisListType

    B, T, C = 4, 256, 144
    P = 128
    NT = T // P
    CR = C - P
    H, HD = 16, 9
    FF = 4 * C
    FC = FF // P
    FR = FF - FC * P
    NL, NU = 3, 12
    NE = 4
    EXPERTS = [1, NE, 1]
    EPS = 1e-6
    SCALE = float(HD) ** -0.5
    DR = 64
    NSK = DR * (DR - 1) // 2
    SLOTS = 6
    STACKS = 2 * SLOTS
    SR = SLOTS * CR
    CUTS = [(0, None), (0, 0), (1, None), (1, 0), (1, 1), (1, 2), (1, 3), (2, None), (2, 0)]
    CUT_AT = {(0, 2): 2, (0, 4): 3, (1, 2): 4, (1, 5): 5, (2, 2): 6, (2, 5): 7, (3, 2): 8}
    KS_ROWS = SLOTS * HD
    CH = [96, 96, 72]
    NCH = [2 * C // c for c in CH]
    QKJ = [[(0, 2), (2, 3)], [(0, 2), (2, 3)], [(0, 2), (2, 4)]]
    TAYLOR = 10
    SQUARINGS = 16

    def hidden_chunks(L):
        E = EXPERTS[L]
        groups = []
        for e in range(E):
            groups += [[(e, c, P) for c in range(FC)], [(e, FC, FR)]]
        return groups

    def experts_before(u):
        return sum(EXPERTS[k // B] for k in range(u))

    HG = H // 4

    ND, NA = 3, 2
    def scores_at(u, g, i):
        counts = (0, 3, 3, 3, 3, 2, 2, 0) if mlp_end(u) > 3 else (0, 3, 4, 3, 2, 2, 2, 0)
        n, first = counts[g], sum(counts[:g])
        return range(first + n * i // 3, first + n * (i + 1) // 3)

    SPREAD_AT = 2
    VALUES_AT = {2: 0, 4: 1, 6: 2}
    DIVIDE_AT = {3: 0, 5: 1, 7: 2}

    def qk_jobs(u):
        return [("qk", u, 0), ("qk", u, 1)]

    def v_jobs(u):
        return [("v", u)] + ([("var", u)] if u // B == 2 else [])

    def spread_jobs(u):
        return [("rs", u, 0), ("rs", u, 1)] if u // B == 2 else []

    def mlp_at(u, g):
        E = EXPERTS[u // B]
        return range(g - 2, g - 1) if 0 <= g - 2 < E else (), range(g - 3, g - 2) if 0 <= g - 3 < E else ()

    def mlp_end(u):
        return 2 + EXPERTS[(u - 1) // B] if u >= 1 else 0

    def norm_at(u):
        return (3, 5) if mlp_end(u) < 4 else (7, 8)

    NORMALISE_AT = 4

    V_JOBS = [("wt", k) for k in range(8)] + [("vv", k) for k in range(4)] + [("pt",)]
    EXP_JOBS = ([("ut",), ("fro",)] + [("tay", k) for k in range(TAYLOR - 1)] + [("ft",)]
                + [("sq", k) for k in range(SQUARINGS)])
    T_JOBS = ([("vqt",), ("vvt",)] + [(s, k) for k in range(5) for s in ("nn", "tn")] + [("kk",), ("uu",)])
    T_FROM = 12
    U_JOBS = [[("gm", 0), ("gm", 1)], [("m", 0), ("m", 1)], [("m", 2), ("m", 3)]]

    QR_RATE = [(0, 1, 2, 1, 1, 0, 1, 1),
               (0, 1, 1, 2, 1, 1, 1, 1),
               (1, 1, 1, 1, 0, 0, 0, 0)]
    QR_AT = {}
    at = 0
    for u in range(1, 2 * B + 2):
        for g in range(H // 2):
            n = min(QR_RATE[(u > B) + (u > 2 * B)][g], DR - at)
            if n:
                QR_AT[u, g] = list(range(at, at + n))[::-1]
            at += n
    assert at == DR

    def rotation_jobs(u, g):
        if u == 0:
            return V_JOBS[2 * g:2 * g + 1], V_JOBS[2 * g + 1:2 * g + 2]
        steps = [("qr", j) for j in QR_AT.get((u, g), ())]
        if u < 2 * B:
            return steps[1:], steps[:1]
        at = 8 * (u - 2 * B) + g
        basis = T_JOBS[at - T_FROM:at - T_FROM + 1] if at >= T_FROM else []
        if at >= len(EXP_JOBS):
            at -= len(EXP_JOBS)
            return [], U_JOBS[at] if at < len(U_JOBS) else []
        return steps[1:], [EXP_JOBS[at]] + basis + steps[:1]

    def y_jobs(b):
        return [("t4", b), ("y", b)]

    d_order = [("ada", 0), ("rep", 0)]
    for u in range(2):
        d_order += [("t1", u)] + qk_jobs(u) + v_jobs(u)
    d_order += [("ada", 1), ("rep", 1), ("ada", 2), ("rep", 2)] + [("gate", L, b) for L in range(NL) for b in range(B)]
    d_order += [("s", 0, h) for h in range(H)] + [("nm", 0), ("t1", 2)] + qk_jobs(2)
    for u in range(NU + 1):
        if u == NU:
            d_order += [job for b in range(B - 1) for job in y_jobs(b)]
        for g in range(H // 2):
            if g == 0 and u + 2 < NU:
                d_order += v_jobs(u + 2)
            for i in range(3):
                if u + 1 < NU:
                    d_order += [("s", u + 1, h) for h in scores_at(u, g, i)]
                if i == 0 and u >= 1:
                    d_order += [("fc2", u - 1, e) for e in mlp_at(u - 1, g)[1]]
                if i == 0 and u < NU:
                    d_order += rotation_jobs(u, g)[0]
            if g == SPREAD_AT and u + 2 < NU:
                d_order += spread_jobs(u + 2)
            if g == 1 and u >= 1:
                d_order += [("t3", u - 1)] + ([("gl", u - 1)] if (u - 1) // B == 1 else [])
            if u < NU:
                d_order += rotation_jobs(u, g)[1]
            if g == H // 2 - 1 and u + 1 < NU:
                d_order += [("nm", u + 1)]
            if u + 3 < NU and g == norm_at(u)[1]:
                d_order += [("t1", u + 3)]
        if u < NU and norm_at(u)[1] == H // 2:
            d_order += [("proj", u)]
        if u + 3 < NU and norm_at(u)[1] == H // 2:
            d_order += [("t1", u + 3)]
        if u + 3 < NU:
            d_order += qk_jobs(u + 3)
        if u < NU and norm_at(u)[1] < H // 2:
            d_order += [("proj", u)]
    d_order += y_jobs(B - 1)
    LN_ORDER = [(1, 0), (1, 1), (1, 2)]
    for u in range(NU):
        LN_ORDER += ([(2, u - 1)] if u >= 1 else []) + ([(1, u + 3)] if u + 3 < NU else [])
    LN_ORDER += [(2, NU - 1)]
    CONSTS = 20
    W_IN = [16 * (6 + (0, 0, 16)[L]) for L in range(NL)]
    M_IN = [16 * (4 * EXPERTS[L] + (0, 2, 0)[L]) for L in range(NL)]
    d_no = {name: n for n, name in enumerate(d_order)}

    a_order = []
    for u in range(NU + 1):
        for g in range(H // 2):
            if u < NU:
                a_order += [("e", u, g)]
            if u >= 1:
                a_order += [("g", u - 1, k) for e in mlp_at(u - 1, g)[0] for k in (2 * e, 2 * e + 1)]
    a_no = {name: n for n, name in enumerate(a_order)}

    ctx = ExitStack()
    with ctx:
        def sb(name, shape, dt=F32):
            return ctx.enter_context(nc.sbuf_tensor(name, shape, dt))

        def sem(name):
            return ctx.enter_context(nc.semaphore(name))

        x = sb("x", [P, B, NT, C])
        xh = sb("xh", [P, NT, P + SR])
        stats = sb("stats", [P, NT, 6])
        mv = sb("mv", [P, NT, 2])
        ve = sb("ve", [P, NT])
        rstd = sb("rstd", [P, NT])
        mhalf = sb("mhalf", [P, 1])
        phalf = sb("phalf", [P, 1])
        mone = sb("mone", [DR, 1])
        hT = sb("hT", [P, T])
        hF = sb("hF", [SR, T])
        hS = sb("hS", [SR + 3, T], BF16)
        h2T = sb("h2T", [P, T])
        h2F = sb("h2F", [SR, T])
        h2S = sb("h2S", [SR + 3, T], BF16)
        level = sb("level", [SR + 3, 4])
        steps = sb("steps", [SR + 3, 7])
        oT = sb("oT", [P, HG, T])
        ob = sb("ob", [P, T])
        rden = sb("rden", [P, T // 32])
        qt = ob
        parts = sb("parts", [96, 3, 4, T], BF16)
        r1 = sb("r1", [96, 4, T])
        qn = r1[0:72]
        qve = sb("qve", [P, T])
        qrs = sb("qrs", [P, T])
        pick = sb("pick", [72, 32])
        spread = sb("spread", [P, 4, 8, HD])
        QS = [sb(f"QS{i}", [KS_ROWS + 1, H, T], BF16) for i in range(2)]
        KS = [sb(f"KS{i}", [KS_ROWS + 1, H, T], BF16) for i in range(2)]
        V = [sb(f"V{i}", [P, NT, H, HD + 1]) for i in range(3)]
        nm = [sb(f"nm{i}", [P, NT, H], BF16) for i in range(2)]
        nmT = sb("nmT", [H, T], BF16)
        NPT = 4
        PT = sb("PT", [P, NPT, 4, T])
        G = sb("G", [P, 2, FC + 1, T])
        tmp = sb("tmp", [P, NT, C])
        acc = sb("acc", [P, NT, C])
        lraw = sb("lraw", [P, NT, NE])
        lg = sb("lg", [P, NT, NE])
        lgm = sb("lgm", [P, NT])
        lge = sb("lge", [P, NT, NE])
        cmpt = sb("cmpt", [P, NT, NE, NE])
        rank = sb("rank", [P, NT, NE])
        cwt = sb("cwt", [P, NT, NE])
        den = sb("den", [P, NT])
        cw = sb("cw", [P, NT, NE])
        cT = sb("cT", [P, B])
        cTr = sb("cTr", [CR, B])
        sT = sb("sT", [P, B])
        sTr = sb("sTr", [CR + 1, B])
        ee = sb("ee", [P, B])
        eer = sb("eer", [CR, B])
        sTb = PT[:, 0, 0:2, :].rearrange("p k t -> p (k t)").rearrange("p (b q) -> p b q", b=B)
        sTrb = PT[0:CR + 1, 1, 0:2, :].rearrange("p k t -> p (k t)").rearrange("p (b q) -> p b q", b=B)
        mod = sb("mod", [P, NL, 6, B])
        short = sb("short", [CR, 6, B])
        six = sb("six", [CR, SR])
        modr = sb("modr", [SR, NL, 6, B])
        gates = sb("gates", [P, NL, B, 2, C])
        ident = sb("ident", [P, P])
        identb = sb("identb", [P, P], BF16)
        Wada = sb("Wada", [P, NL, 6 * C])
        Wadar = sb("Wadar", [CR + 1, NL, 6 * C])
        Wqkv = sb("Wqkv", [P, NL, 3 * C])
        WqkvS = sb("WqkvS", [SR + 3, NL, 3 * C], BF16)
        gm = sb("gm", [P, 2 * H])
        gmr = sb("gmr", [SR + 3, 2 * H])
        Wp = sb("Wp", [P, NL, HG, C])
        W1 = [sb(f"W1_{L}", [P, EXPERTS[L], FF]) for L in range(NL)]
        W1S = [sb(f"W1S_{L}", [SR + 3, EXPERTS[L], FF], BF16) for L in range(NL)]
        WF = sb("WF", [SR + 3, 2, FF])
        cut1 = sb("cut1", [SR + 3, FF], BF16)
        cut2 = sb("cut2", [SR + 3, FF])
        W2 = [sb(f"W2_{L}", [P, EXPERTS[L], FC + 1, C]) for L in range(NL)]
        Wg = sb("Wg", [P, NE])
        Wgr = sb("Wgr", [CR, NE])
        gq = sb("gq", [72, 2])
        old = Wada[:, :, :].rearrange("p l n -> p (l n)")
        qsq = old[0:72, 0:4 * T].rearrange("p (k t) -> p k t", t=T)
        old_at = [4 * T]

        def reuse(rows, *shape):
            n = 1
            for k in shape:
                n *= k
            part = old[0:rows, old_at[0]:old_at[0] + n]
            old_at[0] += n
            assert old_at[0] <= NL * 6 * C
            return part if len(shape) == 1 else part.rearrange("p (b n) -> p b n", b=shape[0])

        Wl = W1[1][0:126, :, :].rearrange("p e f -> p (e f)").rearrange("p (t c) -> p t c", t=16)
        WT = W2[1][:, :, :, :].rearrange("p e c n -> p (e c n)")[:, 0:NSK]
        WTr = Wadar[:, :, :].rearrange("p l n -> p (l n)")[:, 0:NSK]
        vs = G[0:B, :, :, :].rearrange("p e c t -> p (e c t)")[:, 0:NSK]
        Up = sb("Up", [DR, B, DR])
        Ask = sb("Ask", [DR, B, DR])
        fr = sb("fr", [DR, B])
        frb = sb("frb", [DR, B])
        thr = sb("thr", [DR, SQUARINGS])
        need = sb("need", [DR, B, SQUARINGS])
        needu = sb("needu", [DR, SQUARINGS, 2, B], U32)
        fac = sb("fac", [DR, B, SQUARINGS])
        X = sb("X", [DR, B, DR])
        E0 = sb("E0", [DR, B, DR])
        Asq = E0
        Z = sb("Z", [DR, 2 * B, DR])
        ones = sb("ones", [DR, DR])
        Pt = sb("Pt", [DR, C])
        Pn = sb("Pn", [P, DR])
        Pnr = sb("Pnr", [CR, DR])
        Vq = sb("Vq", [DR, C])
        vb = sb("vb", [DR, C])
        heads = sb("heads", [DR, DR])
        below = sb("below", [DR, DR])
        junk = reuse(DR, C)
        junk2 = reuse(DR, C)
        qsc = sb("qsc", [DR, 10])
        Nn = reuse(DR, 2, DR)
        Tn = reuse(DR, DR)
        VqT = reuse(P, DR)
        VqTr = reuse(CR, DR)
        Kq = reuse(DR, C)
        Ut = reuse(DR, C)
        FmI = sb("FmI", [DR, B, DR])
        Gm = sb("Gm", [DR, B, C])
        M = Wqkv[:, :, :].rearrange("p l n -> p (l n)")[:, 0:B * C].rearrange("p (b c) -> p b c", b=B)
        Mr = WF[0:CR, 0, :].rearrange("p (b c) -> p b c", b=B)
        xT, xTr = hT, hF[0:CR]

        scr = nc.dram_tensor("parts_scratch", (2, 3, 2 * C, T), BF16).ap()
        nmscr = nc.dram_tensor("maxima_scratch", (2, H, T), BF16).ap()
        vscr = nc.dram_tensor("skew_scratch", (B, NSK), F32).ap()

        A_ring = [ctx.enter_context(nc.psum_tensor(f"A{i}", [P, 4, T], F32)) for i in range(NA)]
        D_ring = [ctx.enter_context(nc.psum_tensor(f"D{i}", [P, 512], F32)) for i in range(ND)]
        O = ctx.enter_context(nc.psum_tensor("O", [P, T], F32))

        d_full = [sem(f"d_full{i}") for i in range(ND)]
        d_free = [sem(f"d_free{i}") for i in range(ND)]
        a_full = [sem(f"a_full{i}") for i in range(NA)]
        a_free = [sem(f"a_free{i}") for i in range(NA)]
        consts = sem("consts")
        nm_out = [sem(f"nm_out{i}") for i in range(2)]
        mixed = sem("mixed")
        F_done = sem("F_done")
        var_done = sem("var_done")
        rstd_done = sem("rstd_done")
        qsd_done = sem("qsd_done")
        qrs_done = sem("qrs_done")
        norm_done = sem("norm_done")
        vn_done = sem("vn_done")
        vg_done = sem("vg_done")
        x_in = sem("x_in")
        c_in = sem("c_in")
        w_in = [sem(f"w_in{L}") for L in range(NL)]
        wf_in = [sem(f"wf_in{i}") for i in range(2)]
        w_cut = sem("w_cut")
        hs_done = sem("hs_done")
        h2s_done = sem("h2s_done")
        m_in = [sem(f"m_in{L}") for L in range(NL)]
        ada_in = sem("ada_in")
        l3_in = sem("l3_in")
        pt_in = sem("pt_in")
        silu_done = sem("silu_done")
        six_done = sem("six_done")
        centred = sem("centred")
        xh_ready = sem("xh_ready")
        p1_done = sem("p1_done")
        p2_done = sem("p2_done")
        r1_done = sem("r1_done")
        p3_done = sem("p3_done")
        sq_done = sem("sq_done")
        parts_out = [sem(f"parts_out{i}") for i in range(2)]
        stk_in = [sem(f"stk_in{i}") for i in range(2)]
        nm_in = [sem(f"nm_in{i}") for i in range(2)]
        o_read = sem("o_read")
        oT_done = sem("oT_done")
        wp_zero = sem("wp_zero")
        x_new = sem("x_new")
        lgm_done = sem("lgm_done")
        lge_done = sem("lge_done")
        dchain = sem("dchain")
        achain = sem("achain")
        pchain = sem("pchain")
        tri_done = sem("tri_done")
        pv_step = sem("pv_step")
        v_out = sem("v_out")
        up_zero = sem("up_zero")
        thr_set = sem("thr_set")
        up_in = sem("up_in")
        X_done = sem("X_done")
        fr_done = sem("fr_done")
        E_done = sem("E_done")
        sig_done = sem("sig_done")
        dot_done = sem("dot_done")
        v_cut = sem("v_cut")
        qr_done = sem("qr_done")
        N_done = sem("N_done")
        y_out = sem("y_out")

        def slot(name):
            if name in a_no:
                return a_no[name] % NA, a_no[name] // NA, a_full, a_free
            return d_no[name] % ND, d_no[name] // ND, d_full, d_free

        def D(name):
            return D_ring[d_no[name] % ND]

        def A(name):
            return A_ring[a_no[name] % NA]

        def written(eng, name):
            i, turn, full, _ = slot(name)
            eng.wait_ge(full[i], turn + 1)

        def used(eng, name):
            i, turn, _, free = slot(name)
            eng.wait_ge(free[i], turn + 1)

        def release(ins, name):
            i, _, _, free = slot(name)
            return ins.then_inc(free[i], 1)

        def fc2_job(n):
            for u in range(NU):
                if n < EXPERTS[u // B]:
                    return ("fc2", u, n)
                n -= EXPERTS[u // B]

        def remainder(eng, u, j):
            if u // B == 2:
                eng.wait_ge(r1_done, 2 * (u - 2 * B) + j + 1)
            else:
                used(eng, ("qk", u, j))

        def norm_job(n):
            kind, u = LN_ORDER[n]
            return ("t1" if kind == 1 else "t3", u)

        block = ctx.enter_context(nc.Block())

        @block.sync
        def _(sp):
            sp.dma_start(cT[:, :], t["cond"][:, 0:P].rearrange("b c -> c b"), allow_slow_non_contiguous=True).then_inc(c_in, 16)
            sp.dma_start(cTr[:, :], t["cond"][:, P:C].rearrange("b c -> c b"), allow_slow_non_contiguous=True).then_inc(c_in, 16)
            for b in range(B):
                sp.dma_start(x[:, b, :, :], t["x"][b].rearrange("(n p) c -> p n c", p=P)).then_inc(x_in, 16)
            for L in range(NL):
                sp.dma_start(Wada[:, L, :], t["ada"][L][0:P, :]).then_inc(ada_in, 16)
                sp.dma_start(Wadar[0:CR, L, :], t["ada"][L][P:C, :]).then_inc(ada_in, 16)
                sp.dma_start(Wadar[CR:CR + 1, L, :], t["b_ada"][L].unsqueeze(0)).then_inc(ada_in, 16)

            def load(into, dst, src):
                sp.dma_start(dst, src).then_inc(into, 16)

            def load_attention(L):
                load(w_in[L], Wqkv[:, L, :], t["qkv"][L][0:P, :])
                if L == 0:
                    sp.wait_ge(wp_zero, 1)
                for j in range(4):
                    load(w_in[L], Wp[32 * j:32 * j + HD, L, :, :],
                         t["proj"][L].rearrange("(q j r) n -> j r q n", q=HG, j=4)[j])
                load(w_in[L], Wp[HD:HD + 1, L, 0, :], t["b_proj"][L].unsqueeze(0))
                if L == 2:
                    for s, g in enumerate(("g_q", "g_k")):
                        for k in range(8):
                            load(w_in[L], gq[HD * k:HD * k + HD, s:s + 1], t[g].unsqueeze(1))

            def load_mlp(L):
                if L == 1:
                    load(m_in[L], Wg[:, :], t["w_gate"][0:P, :])
                    load(m_in[L], Wgr[:, :], t["w_gate"][P:C, :])
                for e in range(EXPERTS[L]):
                    load(m_in[L], W1[L][:, e, :], t["w1"][L][e][0:P, :])
                    load(m_in[L], W2[L][:, e, 0:FC, :], t["w2"][L][e][0:FC * P, :].rearrange("(c p) n -> p c n", p=P))
                    load(m_in[L], W2[L][0:FR, e, FC, :], t["w2"][L][e][FC * P:FF, :])
                    load(m_in[L], W2[L][FR:FR + 1, e, FC, :], t["b2"][L][e].unsqueeze(0))

            def load_short(c):
                L, e = CUTS[c]
                w, bias, n = (t["qkv"][L], t["b_qkv"][L], 3 * C) if e is None else (t["w1"][L][e], t["b1"][L][e], FF)
                if c >= 2:
                    sp.wait_ge(w_cut, c - 1)
                load(wf_in[c % 2], WF[0:SR, c % 2, 0:n], w[P:C, :].unsqueeze(0).to_broadcast([SLOTS, CR, n]))
                load(wf_in[c % 2], WF[SR:SR + 3, c % 2, 0:n], bias.unsqueeze(0).to_broadcast([3, n]))

            load_short(0)
            load_short(1)
            load_attention(0)
            load_mlp(0)
            sp.dma_start(Wl, t["rot_w"].rearrange("(p t) c -> p t c", t=16)).then_inc(l3_in, 16)
            sp.dma_start(Pn[:, :], t["rot_p"][0:P, :]).then_inc(pt_in, 16)
            sp.dma_start(Pnr[:, :], t["rot_p"][P:C, :]).then_inc(pt_in, 16)

            def store_parts(u):
                L, i = u // B, u % 2
                sp.wait_ge(p1_done, 2 * u + 2)
                sp.wait_ge(p2_done, 2 * u + 2)
                sp.wait_ge(p3_done, 2 * u + 2)
                if u >= 2:
                    sp.wait_ge(stk_in[i], 16 * STACKS * (u // 2))
                for p in range(3):
                    sp.dma_start(scr[i, p].rearrange("(k r) t -> r k t", r=CH[L]),
                                 parts[0:CH[L], p, 0:NCH[L], :]).then_inc(parts_out[i], 16)

            def stack_parts(u):
                i = u % 2
                sp.wait_ge(parts_out[i], 16 * 3 * (u // 2 + 1))
                if u >= 2:
                    written(sp, ("e", u - 2, H // 2 - 1))
                for s, dst in enumerate((QS[i], KS[i])):
                    src = scr[i, :, s * C:(s + 1) * C, :].rearrange("p (h r) t -> p r h t", r=HD)
                    for slot in range(SLOTS):
                        part = ((0, 0, 0, 1, 1, 2), (0, 1, 2, 0, 1, 0))[s][slot]
                        sp.dma_start(dst[HD * slot:HD * slot + HD, :, :], src[part]).then_inc(stk_in[i], 16)

            def store_maxima(u):
                used(sp, ("nm", u))
                sp.dma_start(nmscr[u % 2], nmT[:, :]).then_inc(nm_out[u % 2], 16)

            def load_maxima(u):
                i = u % 2
                if u >= 2:
                    written(sp, ("e", u - 2, H // 2 - 1))
                sp.wait_ge(nm_out[i], 16 * (u // 2 + 1))
                sp.dma_start(QS[i][KS_ROWS:KS_ROWS + 1, :, :], nmscr[i].unsqueeze(0)).then_inc(nm_in[i], 16)

            sp.wait_ge(consts, CONSTS)
            store_parts(0)
            stack_parts(0)
            store_parts(1)
            stack_parts(1)
            store_maxima(0)
            load_maxima(0)
            store_parts(2)
            written(sp, ("gate", NL - 1, B - 1))
            sp.dma_start(WTr[CR:CR + 1, :], t["rot_b"].unsqueeze(0)).then_inc(l3_in, 16)
            load_attention(1)
            load_attention(2)
            load_short(2)
            load_short(3)

            def skew_row(r):
                first = r * (2 * DR - 1 - r) // 2
                sp.dma_start(Up[r:r + 1, :, r + 1:DR], vscr[:, first:first + DR - 1 - r].unsqueeze(0),
                             allow_slow_non_contiguous=True).then_inc(up_in, 16)

            for u in range(NU):
                if u == 1:
                    sp.wait_ge(v_out, 16)
                    sp.wait_ge(up_zero, 1)
                if u >= 1:
                    for r in range(9 * u - 9, min(9 * u, DR - 1)):
                        skew_row(r)
                for c in {1: (4, 5), 2: (6, 7), 3: (8,)}.get(u, ()):
                    load_short(c)
                if u + 1 < NU:
                    store_maxima(u + 1)
                if u + 2 < NU:
                    stack_parts(u + 2)
                if u + 1 < NU:
                    load_maxima(u + 1)
                if u == 0:
                    used(sp, ("vv", 3))
                    sp.dma_start(vscr, vs[:, :]).then_inc(v_out, 16)
                    load_mlp(1)
                    load_mlp(2)
                if u + 3 < NU:
                    store_parts(u + 3)
            for b in range(B):
                used(sp, ("y", b))
                sp.dma_start(out[b].rearrange("(n p) c -> p n c", p=P), x[:, b, :, :]).then_inc(y_out, 16)
            sp.wait_ge(y_out, 16 * B)

        @block.gpsimd
        def _(pool):
            count = [0]

            def link(ins):
                count[0] += 1
                ins.then_inc(pchain, 1)
                pool.wait_ge(pchain, count[0])

            nc.gpsimd.memset(Wp[:, :, :, :], 0.0).then_inc(wp_zero, 1)

            link(nc.gpsimd.memset(ident[:, :], 0.0))
            link(nc.gpsimd.affine_select(out=ident[:, :], in_=ident[:, :], compare_op=ALU.not_equal, fill=1.0,
                                         base=0, pattern=[[-1, P]], channel_multiplier=1))
            nc.gpsimd.tensor_copy(identb[:, :], ident[:, :]).then_inc(consts, 1)
            link(nc.gpsimd.memset(pick[:, :], 1.0 / HD))
            link(nc.gpsimd.affine_select(out=pick[:, :], in_=pick[:, :], compare_op=ALU.is_ge, fill=0.0,
                                         base=0, pattern=[[-HD, 32]], channel_multiplier=1))
            nc.gpsimd.affine_select(out=pick[:, :], in_=pick[:, :], compare_op=ALU.is_ge, fill=0.0,
                                    base=HD - 1, pattern=[[HD, 32]], channel_multiplier=-1).then_inc(consts, 1)
            link(nc.gpsimd.memset(spread[:, :, :, :], 0.0))
            link(nc.gpsimd.affine_select(out=spread[:, :, :, :], in_=spread[:, :, :, :], compare_op=ALU.not_equal,
                                         fill=1.0, base=0, pattern=[[-32, 4], [-1, 8], [0, HD]],
                                         channel_multiplier=1))
            nc.gpsimd.memset(mhalf[:, :], -0.5).then_inc(consts, 1)
            nc.gpsimd.memset(phalf[:, :], 0.5).then_inc(consts, 1)
            nc.gpsimd.memset(mone[:, :], -1.0).then_inc(consts, 1)
            link(nc.gpsimd.memset(steps[:, :], -1.0))
            for k, first in enumerate((16, 32, 48, 64, 80, 97, 98)):
                link(nc.gpsimd.affine_select(out=steps[:, k:k + 1], in_=steps[:, k:k + 1], compare_op=ALU.is_ge,
                                             fill=0.0, base=-first, pattern=[[0, 1]], channel_multiplier=1))
            st = [steps[:, k:k + 1] for k in range(7)]
            w2, w3 = level[:, 0:1], level[:, 1:2]
            link(nc.gpsimd.tensor_tensor(w2, st[0], st[2], ALU.subtract))
            link(nc.gpsimd.tensor_tensor(w2, w2, st[3], ALU.add))
            link(nc.gpsimd.tensor_tensor(w2, w2, st[4], ALU.subtract))
            nc.gpsimd.tensor_tensor(w2, w2, st[5], ALU.add).then_inc(consts, 1)
            link(nc.gpsimd.tensor_tensor(w3, st[1], st[2], ALU.subtract))
            nc.gpsimd.tensor_tensor(w3, w3, st[6], ALU.add).then_inc(consts, 1)
            nc.gpsimd.tensor_copy(level[:, 2:3], st[2]).then_inc(consts, 1)
            nc.gpsimd.tensor_copy(level[:, 3:4], st[4]).then_inc(consts, 1)
            for i in range(3):
                nc.gpsimd.memset(V[i][:, :, :, :], 1.0).then_inc(consts, 1)
            nc.gpsimd.memset(ones[:, :], 1.0).then_inc(consts, 1)
            nc.gpsimd.memset(Up[:, :, :], 0.0).then_inc(up_zero, 1)
            for k in range(SQUARINGS):
                nc.gpsimd.memset(thr[:, k:k + 1], 2.0 * 4.0 ** k).then_inc(thr_set, 1)
            link(nc.gpsimd.memset(below[:, :], -1.0))
            link(nc.gpsimd.affine_select(out=below[:, :], in_=below[:, :], compare_op=ALU.is_gt, fill=0.0, base=0,
                                         pattern=[[-1, DR]], channel_multiplier=1))

            def deviation(n):
                pool.wait_ge(var_done, n + 1)
                if n >= 1:
                    pool.wait_ge(xh_ready, NT * n)
                nc.gpsimd.tensor_tensor(rstd[:, :], ve[:, :], mhalf[:, :].to_broadcast([P, NT]),
                                        ALU.pow).then_inc(rstd_done, 1)

            def third_parts(u):
                L = u // B
                for j, (a, b) in enumerate(QKJ[L]):
                    pool.wait_ge(p2_done, 2 * u + j + 1)
                    remainder(pool, u, j)
                    nc.gpsimd.tensor_tensor(parts[0:CH[L], 2, a:b, :], r1[0:CH[L], a:b, :],
                                            parts[0:CH[L], 1, a:b, :], ALU.subtract).then_inc(p3_done, 1)

            def residual(n):
                u, b = n // 2, (n // 2) % B
                if u // B == 1:
                    pool.wait_ge(mixed, b + 1)
                else:
                    used(pool, ("fc2", u, 0))
                nc.gpsimd.tensor_tensor(x[:, b, :, :], x[:, b, :, :], tmp[:, :, :], ALU.add).then_inc(x_new, 1)

            def rotation(name):
                if name[0] == "qr":
                    j = name[1]
                    norm, sa, g, sg, dot, w = (qsc[:, k:k + 1] for k in range(1, 7))
                    alpha, head = vb[:, j:j + 1], heads[:, j:j + 1]
                    pool.wait_ge(sig_done, j + 1)
                    if j >= 1:
                        pool.wait_ge(qr_done, j)
                    link(nc.gpsimd.tensor_tensor(norm, qsc[:, 0:1], phalf[0:DR, :], ALU.pow))
                    pool.wait_ge(dot_done, 2 * j + 2)
                    link(nc.gpsimd.tensor_tensor(sa, sg, norm, ALU.mult))
                    link(nc.gpsimd.tensor_tensor(head, alpha, sa, ALU.add))
                    link(nc.gpsimd.tensor_scalar(g, sa, head, 1e-37, ALU.mult, ALU.max))
                    link(nc.gpsimd.tensor_tensor(g, g, mone[:, :], ALU.pow))
                    link(nc.gpsimd.tensor_scalar(w, Pt[:, j:j + 1], sa, dot, ALU.mult, ALU.add))
                    nc.gpsimd.tensor_scalar(w, w, g, below[:, j:j + 1], ALU.mult, ALU.mult).then_inc(norm_done, 1)
                elif name == ("vqt",):
                    pool.wait_ge(qr_done, DR)
                    link(nc.gpsimd.affine_select(out=Vq[:, :], in_=Pt[:, :], compare_op=ALU.is_gt, fill=0.0, base=0,
                                                 pattern=[[1, C]], channel_multiplier=-1))
                    nc.gpsimd.affine_select(out=heads[:, :], in_=heads[:, :], compare_op=ALU.is_equal, fill=0.0, base=0,
                                            pattern=[[1, DR]], channel_multiplier=-1).then_inc(v_cut, 1)
                    pool.wait_ge(vn_done, 1)
                    nc.gpsimd.tensor_tensor(qsc[:, 6:7], qsc[:, 7:8], mhalf[0:DR, :], ALU.pow).then_inc(vg_done, 1)
                elif name == ("vvt",):
                    for s, sign in ((0, 1), (1, -1)):
                        used(pool, ("vvt",))
                        nc.gpsimd.affine_select(out=Nn[:, s, :], in_=Nn[:, s, :], compare_op=ALU.is_gt, fill=0.0,
                                                base=0, pattern=[[sign, DR]],
                                                channel_multiplier=-sign).then_inc(tri_done, 1)

            deviation(0)
            third_parts(0)
            deviation(1)
            third_parts(1)
            deviation(2)
            third_parts(2)
            for u in range(NU + 1):
                if u >= 1:
                    deviation(LN_ORDER.index((2, u - 1)))
                for g in range(H // 2):
                    if u < NU:
                        for name in rotation_jobs(u, g)[0]:
                            rotation(name)
                    if g == SPREAD_AT and 2 * B <= u + 2 < NU:
                        third_parts(u + 2)
                    if u >= 1 and g == mlp_end(u):
                        residual(2 * u - 1)
                    if u < NU:
                        for name in rotation_jobs(u, g)[1]:
                            rotation(name)
                    if u + 3 < NU and g == norm_at(u)[0]:
                        deviation(LN_ORDER.index((1, u + 3)))
                if u + 3 < 2 * B:
                    third_parts(u + 3)

        @block.scalar
        def _(act):
            act.wait_ge(c_in, 32)
            nc.scalar.activation(ee[:, :], cT[:, :], ACT.Exp, scale=-1.0).then_inc(achain, 1)
            nc.scalar.activation(eer[:, :], cTr[:, :], ACT.Exp, scale=-1.0).then_inc(achain, 1)

            def modulate(u):
                L, b = u // B, u % B
                written(act, ("t1", u))
                if u >= 1:
                    written(act, ("v", u - 1))
                nc.scalar.activation(hT[:, :], D(("t1", u))[:, 0:T], ACT.Identity,
                                     scale=mod[:, L, 1, b:b + 1], bias=mod[:, L, 0, b:b + 1])
                release(nc.scalar.activation(hF[:, :], D(("t1", u))[0:SR, T:2 * T], ACT.Identity,
                                               scale=modr[:, L, 1, b:b + 1], bias=modr[:, L, 0, b:b + 1]),
                          ("t1", u))

            def qk_of(u):
                L, c = u // B, CH[u // B]
                if L < 2:
                    if u >= 1:
                        act.wait_ge(parts_out[(u - 1) % 2], 16 * 3 * ((u - 1) // 2 + 1))
                    for j, (lo, hi) in enumerate(QKJ[L]):
                        name = ("qk", u, j)
                        written(act, name)
                        nc.scalar.copy(parts[0:c, 0, lo:hi, :],
                                       D(name)[0:c, 0:(hi - lo) * T].rearrange("p (k t) -> p k t", t=T)).then_inc(p1_done, 1)
                else:
                    for j, (lo, hi) in enumerate(QKJ[L]):
                        name = ("qk", u, j)
                        written(act, name)
                        if u > 2 * B:
                            written(act, ("var", u - 1))
                        src = D(name)[0:c, :].rearrange("p (k t) -> p k t", t=T)
                        nc.scalar.activation(qsq[:, lo:hi, :], src, ACT.Square).then_inc(sq_done, 1)
                        act.wait_ge(p3_done, 2 * u)
                        release(nc.scalar.activation(qn[:, lo:hi, :], src, ACT.Copy, scale=gq[:, j:j + 1]), name)

            def v_of(u):
                L = u // B
                name = ("v", u)
                written(act, name)
                if u >= 3:
                    act.wait_ge(pv_step, HG * (u - 2))
                release(nc.scalar.copy(V[u % 3][:, :, :, 0:HD],
                                         D(name)[:, 0:NT * C].rearrange("p (n h r) -> p n h r", n=NT, h=H)),
                          name)
                if L == 2:
                    used(act, ("var", u))
                    if u > 2 * B:
                        written(act, ("rs", u - 1, 1))
                    nc.scalar.activation(qrs[:, :], qve[:, :], ACT.Sqrt).then_inc(qsd_done, 1)

            def first_parts(u):
                L, c = u // B, CH[u // B]
                act.wait_ge(parts_out[(u - 1) % 2], 16 * 3 * ((u - 1) // 2 + 1))
                for j, (lo, hi) in enumerate(QKJ[L]):
                    used(act, ("rs", u, j))
                    nc.scalar.copy(parts[0:c, 0, lo:hi, :], qn[:, lo:hi, :]).then_inc(p1_done, 1)

            def maxima(u):
                name = ("nm", u)
                written(act, name)
                if u >= 1:
                    act.wait_ge(nm_out[(u - 1) % 2], 16 * ((u - 1) // 2 + 1))
                release(nc.scalar.copy(nmT[:, :], D(name)[:, :].bitcast(BF16)[0:H, 0:T]), name)

            def hidden(u, e):
                L = u // B
                for k in (2 * e, 2 * e + 1):
                    group = hidden_chunks(L)[k]
                    name = ("g", u, k)
                    e0, c0, rows = group[0]
                    n = len(group)
                    at = experts_before(u) + e0
                    written(act, name)
                    if at == 0 and k == 0:
                        act.wait_ge(v_out, 16)
                    if at >= 2 and c0 == 0:
                        written(act, fc2_job(at - 2))
                    release(nc.scalar.activation(G[0:rows, at % 2, c0:c0 + n, :], A(name)[0:rows, 0:n, :],
                                                 ACT.Gelu_apprx_tanh), name)

            def modulate_mlp(u):
                L, b = u // B, u % B
                name = ("t3", u)
                written(act, name)
                if u >= 1:
                    written(act, ("g", u - 1, 2 * EXPERTS[(u - 1) // B] - 1))
                nc.scalar.activation(h2T[:, :], D(name)[:, 0:T], ACT.Identity,
                                     scale=mod[:, L, 4, b:b + 1], bias=mod[:, L, 3, b:b + 1])
                release(nc.scalar.activation(h2F[:, :], D(name)[0:SR, T:2 * T], ACT.Identity,
                                               scale=modr[:, L, 4, b:b + 1], bias=modr[:, L, 3, b:b + 1]),
                          name)
                if L == 1:
                    act.wait_ge(lgm_done, b + 1)
                    nc.scalar.activation(lge[:, :, :], lg[:, :, :], ACT.Exp).then_inc(lge_done, 1)

            used(act, ("rep", 0))
            act.wait_ge(consts, CONSTS)
            for u in range(2):
                modulate(u)
                qk_of(u)
                v_of(u)
            used(act, ("rep", NL - 1))
            maxima(0)
            modulate(2)
            qk_of(2)
            written(act, ("gate", NL - 1, B - 1))
            for u in range(NU + 1):
                for g in range(H // 2):
                    if u < NU:
                        name = ("e", u, g)
                        n = 8 * u + g
                        written(act, name)
                        if n >= NPT:
                            act.wait_ge(pv_step, (n - NPT) // 2 + 1)
                        release(nc.scalar.activation(PT[:, n % NPT, :, :], A(name)[:, :, :], ACT.Exp, scale=SCALE),
                                name)
                    if g == 0 and u + 2 < NU:
                        v_of(u + 2)
                    if g == SPREAD_AT and 2 * B <= u + 2 < NU:
                        first_parts(u + 2)
                    if g == 1 and u >= 1:
                        modulate_mlp(u - 1)
                    if u >= 1:
                        for e in mlp_at(u - 1, g)[0]:
                            hidden(u - 1, e)
                    if g == H // 2 - 1 and u + 1 < NU:
                        maxima(u + 1)
                    if u + 3 < NU and g == norm_at(u)[1]:
                        modulate(u + 3)
                if u + 3 < NU and norm_at(u)[1] == H // 2:
                    modulate(u + 3)
                if u + 3 < NU:
                    qk_of(u + 3)

        @block.vector
        def _(dve):
            count = [0]

            def link(ins):
                count[0] += 1
                ins.then_inc(dchain, 1)
                dve.wait_ge(dchain, count[0])

            for i in range(2):
                nc.vector.memset(KS[i][32:KS_ROWS + 1, :, :].bitcast(U32), 0x3F803F80).then_inc(consts, 1)
            nc.vector.memset(G[FR:FR + 1, :, FC, :], 1.0).then_inc(consts, 1)
            for tile in (hS, h2S):
                nc.vector.memset(tile[:, :], 1.0).then_inc(consts, 1)
            nc.vector.memset(O[:, :], 1.0).then_inc(consts, 1)
            nc.vector.memset(short[:, :, :], 0.0).then_inc(consts, 1)
            link(nc.vector.memset(sTr[:, :], 1.0))
            dve.wait_ge(achain, 2)
            link(nc.vector.tensor_scalar(ee[:, :], ee[:, :], 1.0, None, ALU.add))
            link(nc.vector.tensor_scalar(eer[:, :], eer[:, :], 1.0, None, ALU.add))
            link(nc.vector.reciprocal(ee[:, :], ee[:, :]))
            link(nc.vector.reciprocal(eer[:, :], eer[:, :]))
            link(nc.vector.tensor_tensor(sT[:, :], cT[:, :], ee[:, :], ALU.mult))
            link(nc.vector.tensor_tensor(sTr[0:CR, :], cTr[:, :], eer[:, :], ALU.mult))
            nc.vector.tensor_copy(sTb[:, :, :], sT[:, :].unsqueeze(2).to_broadcast([P, B, P])).then_inc(silu_done, 1)
            nc.vector.tensor_copy(sTrb[:, :, :],
                                  sTr[:, :].unsqueeze(2).to_broadcast([CR + 1, B, P])).then_inc(silu_done, 1)
            dve.wait_ge(consts, CONSTS)
            nc.vector.tensor_copy(six[:, :].rearrange("p (s r) -> p s r", r=CR),
                                  ident[0:CR, 0:CR].unsqueeze(1).to_broadcast([CR, SLOTS, CR])).then_inc(six_done, 1)

            def modulation(L):
                name = ("ada", L)
                written(dve, name)
                src = D(name)[:, 0:6 * B].rearrange("p (s b) -> p s b", b=B)
                srcr = D(name)[0:CR, 6 * B:12 * B].rearrange("p (s b) -> p s b", b=B)
                nc.vector.tensor_copy(mod[:, L, 0:4:3, :], src[:, 0:4:3, :])
                nc.vector.tensor_copy(short[:, 0:4:3, :], srcr[:, 0:4:3, :])
                nc.vector.tensor_scalar(mod[:, L, 1:5:3, :], src[:, 1:5:3, :], 1.0, None, ALU.add)
                release(nc.vector.tensor_scalar(short[:, 1:5:3, :], srcr[:, 1:5:3, :], 1.0, None, ALU.add),
                          name)
                name = ("rep", L)
                written(dve, name)
                release(nc.vector.tensor_copy(modr[:, L, :, :],
                                              D(name)[0:SR, 0:6 * B].rearrange("p (s b) -> p s b", b=B)), name)

            def centre(w, m):
                wv = w.rearrange("p (h r) -> p h r", r=HD)
                link(nc.vector.tensor_reduce(m[:, :], wv, AX.X, ALU.add))
                link(nc.vector.tensor_scalar(m[:, :], m[:, :], 1.0 / HD, None, ALU.mult))
                nc.vector.tensor_tensor(wv, wv, m[:, :].unsqueeze(2).to_broadcast([w.shape[0], 2 * H, HD]),
                                        ALU.subtract).then_inc(centred, 1)

            def cut(dst, src, second, third):
                rows, n = src.shape
                a, r = cut1[0:rows, 0:n], cut2[0:rows, 0:n]
                link(nc.vector.tensor_copy(a, src))
                link(nc.vector.scalar_tensor_tensor(r, a, second, src, ALU.mult, ALU.add))
                link(nc.vector.tensor_copy(a, r))
                return nc.vector.scalar_tensor_tensor(dst, a, third, r, ALU.mult, ALU.add)

            def cut_weights(c):
                L, e = CUTS[c]
                dve.wait_ge(wf_in[c % 2], 16 * 2 * (c // 2 + 1))
                n = 3 * C if e is None else FF
                if c == CUTS.index((2, None)):
                    centre(WF[:, c % 2, 0:2 * C], gmr)
                    dve.wait_ge(centred, 1)
                dst = WqkvS[:, L, :] if e is None else W1S[L][:, e, :]
                cut(dst, WF[:, c % 2, 0:n], level[:, 0:1], level[:, 1:2]).then_inc(w_cut, 1)
                dve.wait_ge(w_cut, c + 1)

            def cut_input(u):
                used(dve, ("t1", u))
                if u >= 1:
                    written(dve, ("v", u - 1))
                cut(hS[0:SR, :], hF[:, :], level[0:SR, 2:3], level[0:SR, 3:4]).then_inc(hs_done, 1)
                dve.wait_ge(hs_done, u + 1)

            def cut_mlp_input(u):
                used(dve, ("t3", u))
                if u >= 1:
                    written(dve, ("g", u - 1, 2 * EXPERTS[(u - 1) // B] - 1))
                cut(h2S[0:SR, :], h2F[:, :], level[0:SR, 2:3], level[0:SR, 3:4]).then_inc(h2s_done, 1)
                dve.wait_ge(h2s_done, u + 1)

            def moments(b):
                for k in range(NT):
                    nc.vector.bn_stats(stats[:, k, :], x[:, b, k, :]).then_inc(dchain, 1)
                count[0] += NT
                dve.wait_ge(dchain, count[0])
                for k in range(NT):
                    nc.vector.bn_aggr(mv[:, k, :], stats[:, k, :]).then_inc(dchain, 1)
                count[0] += NT
                dve.wait_ge(dchain, count[0])
                nc.vector.tensor_scalar(ve[:, :], mv[:, :, 1], EPS, None, ALU.add).then_inc(var_done, 1)

            def normalise(n, b):
                dve.wait_ge(rstd_done, n + 1)
                if n >= 1:
                    written(dve, norm_job(n - 1))
                for k in range(NT):
                    nc.vector.tensor_scalar(xh[:, k, 0:C], x[:, b, k, :], mv[:, k, 0:1], rstd[:, k:k + 1],
                                            ALU.subtract, ALU.mult)
                    nc.vector.tensor_scalar(xh[:, k, C:P + SR].rearrange("p (s r) -> p s r", r=CR),
                                            x[:, b, k, P:C].unsqueeze(1).to_broadcast([P, SLOTS - 1, CR]),
                                            mv[:, k, 0:1], rstd[:, k:k + 1],
                                            ALU.subtract, ALU.mult).then_inc(xh_ready, 1)

            def ln_no(kind, u):
                return LN_ORDER.index((kind, u))

            def norm_1(u):
                if u < B:
                    dve.wait_ge(x_in, 16 * B)
                else:
                    dve.wait_ge(x_new, 2 * (u - B) + 2)
                moments(u % B)

            def variances(u):
                name = ("var", u)
                written(dve, name)
                if u > 2 * B:
                    dve.wait_ge(qrs_done, u - 2 * B)
                release(nc.vector.tensor_scalar(qve[:, :], D(name)[:, 0:T], EPS, None, ALU.add), name)

            def inverse_deviations(u):
                dve.wait_ge(qsd_done, u - 2 * B + 1)
                link(nc.vector.reciprocal(qrs[:, :], qrs[:, :]))
                link(nc.vector.tensor_tensor(qt[:, :], qrs[:, :], qrs[:, :], ALU.mult))
                link(nc.vector.scalar_tensor_tensor(qt[:, :], qt[:, :], -0.5, qve[:, :], ALU.mult, ALU.mult))
                nc.vector.scalar_tensor_tensor(qrs[:, :], qt[:, :], 1.5, qrs[:, :], ALU.add,
                                               ALU.mult).then_inc(qrs_done, 1)

            def second_parts(u):
                L, c = u // B, CH[u // B]
                if L == 2:
                    for j, (lo, hi) in enumerate(QKJ[L]):
                        name = ("rs", u, j)
                        written(dve, name)
                        used(dve, ("qk", u, j))
                        release(nc.vector.tensor_tensor(
                            qn[:, lo:hi, :], qn[:, lo:hi, :], D(name)[0:c, :].rearrange("p (k t) -> p k t", t=T),
                            ALU.mult), name)
                for j, (lo, hi) in enumerate(QKJ[L]):
                    dve.wait_ge(p1_done, 2 * u + j + 1)
                    if u >= 1:
                        dve.wait_ge(p3_done, 2 * u)
                    if L < 2:
                        name = ("qk", u, j)
                        ins = nc.vector.tensor_tensor(
                            r1[0:c, lo:hi, :], D(name)[0:c, 0:(hi - lo) * T].rearrange("p (k t) -> p k t", t=T),
                            parts[0:c, 0, lo:hi, :], ALU.subtract)
                        release(ins, name)
                    else:
                        used(dve, ("rs", u, j))
                        nc.vector.tensor_tensor(r1[0:c, lo:hi, :], qn[0:c, lo:hi, :], parts[0:c, 0, lo:hi, :],
                                                ALU.subtract).then_inc(r1_done, 1)
                    remainder(dve, u, j)
                    if u >= 1:
                        dve.wait_ge(parts_out[(u - 1) % 2], 16 * 3 * ((u - 1) // 2 + 1))
                    nc.vector.tensor_copy(parts[0:c, 1, lo:hi, :], r1[0:c, lo:hi, :]).then_inc(p2_done, 1)

            def maxima(u, h):
                name = ("s", u, h)
                written(dve, name)
                if u >= 2 and h == 0:
                    written(dve, ("nm", u - 2))
                release(nc.vector.tensor_reduce(nm[u % 2][:, :, h], D(name)[:, :].rearrange("p (n k) -> p n k", n=NT),
                                                  AX.X, ALU.max, negate=True), name)

            def residual(u):
                name = ("proj", u)
                written(dve, name)
                b = u % B
                release(gated(2 * u, D(name)[:, 0:NT * C].rearrange("p (n c) -> p n c", n=NT),
                              gates[:, u // B, b, 0, :]), name)
                used(dve, name)
                nc.vector.tensor_tensor(x[:, b, :, :], x[:, b, :, :], tmp[:, :, :], ALU.add).then_inc(x_new, 1)

            def gated(n, src, gate):
                if n >= 1:
                    dve.wait_ge(x_new, n)
                return nc.vector.tensor_tensor(tmp[:, :, :], src,
                                               gate.unsqueeze(1).to_broadcast([P, NT, C]), ALU.mult)

            def divide(u, q):
                n = HG * u + q
                dve.wait_ge(pv_step, n + 1)
                nc.vector.transpose(ob[:, :], O[:, :]).then_inc(o_read, 1)
                dve.wait_ge(o_read, n + 1)
                blocks = ob[:, :].rearrange("p (k r) -> p k r", r=32)
                link(nc.vector.reciprocal(rden[:, :], blocks[:, :, HD]))
                link(nc.vector.tensor_tensor(blocks, blocks, rden[:, :].unsqueeze(2).to_broadcast([P, T // 32, 32]),
                                             ALU.mult))
                if u >= 1:
                    written(dve, ("proj", u - 1))
                nc.vector.transpose(oT[:, q, :], ob[:, :]).then_inc(oT_done, 1)
                dve.wait_ge(oT_done, n + 1)

            WTv = WT[:, :].rearrange("c (p t) -> c t p", t=16)
            WTrv = WTr[0:CR, :].rearrange("c (p t) -> c t p", t=16)
            idb = ident[0:DR, 0:DR].unsqueeze(1).to_broadcast([DR, B, DR])

            def skew_vectors(name):
                written(dve, name)
                if name[0] == "wt":
                    q = name[1] // 2
                    dst, rows = ((WTv, P), (WTrv, CR))[name[1] % 2]
                    ins = nc.vector.tensor_copy(dst[:, 4 * q:4 * q + 4, :],
                                                D(name)[0:rows, 0:504].rearrange("c (t p) -> c t p", t=4))
                elif name[0] == "vv":
                    q = name[1]
                    ins = nc.vector.tensor_copy(vs[:, 504 * q:504 * q + 504], D(name)[0:B, 0:504])
                else:
                    ins = nc.vector.tensor_copy(Pt[:, :], D(name)[0:DR, 0:C])
                release(ins, name)

            def update_rows(j):
                w = qsc[:, 6:7]
                dve.wait_ge(norm_done, j + 1)
                nc.vector.scalar_tensor_tensor(Pt[:, j + 1:C], vb[:, j + 1:C], w, Pt[:, j + 1:C], ALU.mult,
                                               ALU.add).then_inc(qr_done, 1)

            def exponential(name):
                kind = name[0]
                d = D(name)[0:DR, :]
                if kind == "ut":
                    written(dve, name)
                    release(nc.vector.tensor_tensor(Ask[:, :, :], Up[:, :, :],
                                                    d[:, 0:256].rearrange("p (b j) -> p b j", b=B), ALU.subtract),
                            name)
                    used(dve, name)
                    link(nc.vector.tensor_tensor(Asq[:, :, :], Ask[:, :, :], Ask[:, :, :], ALU.mult))
                    nc.vector.tensor_reduce(fr[:, :], Asq[:, :, :], AX.X, ALU.add).then_inc(fr_done, 1)
                elif kind == "fro":
                    written(dve, name)
                    release(nc.vector.tensor_copy(frb[:, :], d[:, 0:B]), name)
                    used(dve, name)
                    dve.wait_ge(thr_set, SQUARINGS)
                    link(nc.vector.tensor_tensor(need[:, :, :],
                                                 frb[:, :].unsqueeze(2).to_broadcast([DR, B, SQUARINGS]),
                                                 thr[:, :].unsqueeze(1).to_broadcast([DR, B, SQUARINGS]), ALU.is_gt))
                    for s in range(2):
                        link(nc.vector.tensor_copy(needu[:, :, s, :], need[:, :, :].rearrange("p b k -> p k b")))
                    link(nc.vector.tensor_scalar(fac[:, :, :], need[:, :, :], -0.5, 1.0, ALU.mult, ALU.add))
                    n = SQUARINGS // 2
                    while n >= 1:
                        link(nc.vector.tensor_tensor(fac[:, :, 0:n], fac[:, :, 0:n], fac[:, :, n:2 * n], ALU.mult))
                        n //= 2
                    nc.vector.tensor_tensor(X[:, :, :], Ask[:, :, :], fac[:, :, 0:1].to_broadcast([DR, B, DR]),
                                            ALU.mult).then_inc(X_done, 1)
                    dve.wait_ge(X_done, 1)
                    nc.vector.scalar_tensor_tensor(E0[:, :, :], X[:, :, :], 1.0 / TAYLOR, idb, ALU.mult,
                                                   ALU.add).then_inc(E_done, 1)
                elif kind == "tay":
                    k = name[1]
                    dst = Z[:, 0:B, :] if k == TAYLOR - 2 else E0[:, :, :]
                    written(dve, name)
                    release(nc.vector.scalar_tensor_tensor(
                        dst, d[:, 0:B * DR].rearrange("p (b j) -> p b j", b=B), -1.0 / (TAYLOR - 1 - k), idb,
                        ALU.mult, ALU.add), name)
                elif kind == "ft":
                    written(dve, name)
                    release(nc.vector.tensor_copy(Z[:, B:2 * B, :], d[:, 0:B * DR].rearrange("p (b j) -> p b j", b=B)),
                            name)
                elif kind == "sq":
                    k = name[1]
                    written(dve, name)
                    release(nc.vector.copy_predicated(
                        Z[:, :, :],
                        needu[:, k, :, :].rearrange("p s b -> p (s b)").unsqueeze(2).to_broadcast([DR, 2 * B, DR]),
                        d.rearrange("p (b j) -> p b j", j=DR)), name)
                    if k == SQUARINGS - 1:
                        used(dve, name)
                        nc.vector.tensor_tensor(FmI[:, :, :], Z[:, B:2 * B, :], idb, ALU.subtract).then_inc(F_done, 1)

            def orthonormal(name):
                kind = name[0]
                d = D(name)
                if kind == "vqt":
                    reflectors()
                    written(dve, name)
                    nc.vector.tensor_copy(VqT[:, :], d[:, 0:DR])
                    release(nc.vector.tensor_copy(VqTr[:, :], d[0:CR, DR:2 * DR]), name)
                elif kind == "vvt":
                    written(dve, name)
                    nc.vector.tensor_copy(Nn[:, 0, :], d[0:DR, 0:DR])
                    release(nc.vector.tensor_copy(Nn[:, 1, :], d[0:DR, 0:DR]), name)
                    dve.wait_ge(tri_done, 2)
                    nc.vector.tensor_tensor(Tn[:, :], ident[0:DR, 0:DR], Nn[:, 0, :], ALU.subtract).then_inc(N_done, 1)
                elif kind == "nn":
                    written(dve, name)
                    dve.wait_ge(N_done, 1)
                    release(nc.vector.tensor_copy(Nn[:, :, :], d[0:DR, 0:2 * DR].rearrange("p (s j) -> p s j", s=2)),
                            name)
                elif kind == "tn":
                    written(dve, name)
                    release(nc.vector.tensor_tensor(Tn[:, :], Tn[:, :], d[0:DR, 0:DR], ALU.add), name)
                elif kind == "kk":
                    written(dve, name)
                    release(nc.vector.tensor_copy(Kq[:, :], d[0:DR, 0:C]), name)
                elif kind == "uu":
                    written(dve, name)
                    nc.vector.tensor_scalar(Ut[:, DR:C], d[0:DR, DR:C], -1.0, None, ALU.mult)
                    release(nc.vector.tensor_tensor(Ut[:, 0:DR], ident[0:DR, 0:DR], d[0:DR, 0:DR], ALU.subtract), name)
                elif kind == "gm":
                    k = name[1]
                    written(dve, name)
                    release(nc.vector.tensor_copy(Gm[:, 2 * k:2 * k + 2, :],
                                                  d[0:DR, 0:2 * C].rearrange("p (b c) -> p b c", b=2)), name)
                elif kind == "m":
                    b = name[1]
                    written(dve, name)
                    nc.vector.tensor_copy(M[:, b, :], d[:, 0:C])
                    release(nc.vector.tensor_copy(Mr[:, b, :], d[0:CR, C:2 * C]), name)

            def reflectors():
                dve.wait_ge(v_cut, 1)
                link(nc.vector.tensor_tensor(Vq[:, 0:DR], Vq[:, 0:DR], heads[:, :], ALU.add))
                link(nc.vector.tensor_tensor_reduce(out=junk2[:, :], in0=Vq[:, :], in1=Vq[:, :], scale=0.5,
                                                    scalar=1e-37, op0=ALU.mult, op1=ALU.add,
                                                    accum_out=qsc[:, 3:4]))
                nc.vector.tensor_copy(qsc[:, 7:8], qsc[:, 3:4]).then_inc(vn_done, 1)
                dve.wait_ge(vg_done, 1)
                nc.vector.tensor_scalar(Vq[:, :], Vq[:, :], qsc[:, 6:7], None, ALU.mult).then_inc(qr_done, 1)

            def rotate(b):
                name = ("t4", b)
                written(dve, name)
                if b >= 1:
                    written(dve, ("y", b - 1))
                nc.vector.tensor_copy(xT[:, :], D(name)[:, 0:T])
                release(nc.vector.tensor_copy(xTr[:, :], D(name)[0:CR, T:2 * T]), name)
                name = ("y", b)
                written(dve, name)
                release(nc.vector.tensor_tensor(x[:, b, :, :], D(name)[:, 0:NT * C].rearrange("p (n c) -> p n c", n=NT),
                                                x[:, b, :, :], ALU.add), name)

            def rotation(name):
                kind = name[0]
                if kind == "qr":
                    j = name[1]
                    written(dve, name)
                    release(nc.vector.tensor_copy(vb[:, j:C], D(name)[0:DR, j:C]), name)
                    used(dve, name)
                    nc.vector.tensor_tensor_reduce(out=junk[:, j:C], in0=vb[:, j:C], in1=vb[:, j:C], scale=4.0,
                                                   scalar=0.0, op0=ALU.mult, op1=ALU.add,
                                                   accum_out=qsc[:, 0:1]).then_inc(sig_done, 1)
                    nc.vector.tensor_scalar(qsc[:, 4:5], vb[:, j:j + 1], 0.0, 0.5, ALU.is_ge,
                                            ALU.subtract).then_inc(dot_done, 1)
                    nc.vector.tensor_tensor_reduce(out=junk2[:, j:C], in0=Pt[:, j:C], in1=vb[:, j:C], scale=1.0,
                                                   scalar=0.0, op0=ALU.mult, op1=ALU.add,
                                                   accum_out=qsc[:, 5:6]).then_inc(dot_done, 1)
                elif name in EXP_JOBS:
                    exponential(name)
                else:
                    orthonormal(name)

            def mlp_gates(u):
                L, b = u // B, u % B
                name = ("gl", u)
                written(dve, name)
                if b >= 1:
                    dve.wait_ge(lge_done, b)
                gl = D(name)[:, 0:NT * NE].rearrange("p (n e) -> p n e", n=NT)
                release(nc.vector.tensor_copy(lraw[:, :, :], gl), name)
                used(dve, name)
                link(nc.vector.tensor_reduce(lgm[:, :], lraw[:, :, :], AX.X, ALU.max))
                nc.vector.tensor_tensor(lg[:, :, :], lraw[:, :, :],
                                        lgm[:, :].unsqueeze(2).to_broadcast([P, NT, NE]),
                                        ALU.subtract).then_inc(lgm_done, 1)
                dve.wait_ge(lgm_done, b + 1)
                link(nc.vector.memset(cmpt[:, :, :, :], 0.0))
                n_cmp = 0
                for f in range(NE):
                    for lo, hi, op in ((0, f, ALU.is_gt), (f + 1, NE, ALU.is_ge)):
                        if hi > lo:
                            nc.vector.tensor_tensor(
                                cmpt[:, :, lo:hi, f], lraw[:, :, f:f + 1].to_broadcast([P, NT, hi - lo]),
                                lraw[:, :, lo:hi], op).then_inc(dchain, 1)
                            n_cmp += 1
                count[0] += n_cmp
                dve.wait_ge(dchain, count[0])
                link(nc.vector.tensor_reduce(rank[:, :, :], cmpt[:, :, :, :], AX.X, ALU.add))
                dve.wait_ge(lge_done, b + 1)
                link(nc.vector.scalar_tensor_tensor(cwt[:, :, :], rank[:, :, :], 1.5, lge[:, :, :],
                                                    ALU.is_lt, ALU.mult))
                link(nc.vector.tensor_reduce(den[:, :], cwt[:, :, :], AX.X, ALU.add))
                link(nc.vector.reciprocal(den[:, :], den[:, :]))
                link(nc.vector.tensor_tensor(cw[:, :, :], cwt[:, :, :],
                                             den[:, :].unsqueeze(2).to_broadcast([P, NT, NE]), ALU.mult))

            def mixture(u, e):
                L, b = u // B, u % B
                name = ("fc2", u, e)
                written(dve, name)
                if L == 1:
                    for k in range(NT):
                        src = D(name)[:, k * C:(k + 1) * C]
                        if e == 0:
                            ins = nc.vector.tensor_scalar(acc[:, k, :], src, cw[:, k, e:e + 1], None, ALU.mult)
                        else:
                            ins = nc.vector.scalar_tensor_tensor(acc[:, k, :], src, cw[:, k, e:e + 1],
                                                                 acc[:, k, :], ALU.mult, ALU.add)
                    release(ins, name)
                    used(dve, name)
                    if e == NE - 1:
                        gated(2 * u + 1, acc[:, :, :], gates[:, L, b, 1, :]).then_inc(mixed, 1)
                else:
                    release(gated(2 * u + 1, D(name)[:, 0:NT * C].rearrange("p (n c) -> p n c", n=NT),
                                  gates[:, L, b, 1, :]), name)

            for u in range(2):
                norm_1(u)
                normalise(ln_no(1, u), u % B)
                cut_weights(u)
                if u == 0:
                    modulation(0)
                cut_input(u)
                second_parts(u)
            for L in (1, 2):
                modulation(L)
            for L in range(NL):
                for b in range(B):
                    name = ("gate", L, b)
                    written(dve, name)
                    release(nc.vector.tensor_copy(gates[:, L, b, :, :],
                                                    D(name)[:, 0:2 * C].rearrange("p (s c) -> p s c", s=2)),
                              name)
            for h in range(H):
                maxima(0, h)
            norm_1(2)
            normalise(ln_no(1, 2), 2 % B)
            cut_input(2)
            second_parts(2)
            row = None
            for u in range(NU + 1):
                if u == NU:
                    for b in range(B - 1):
                        rotate(b)
                if u >= 1:
                    dve.wait_ge(x_new, 2 * u - 1)
                    moments((u - 1) % B)
                    normalise(ln_no(2, u - 1), (u - 1) % B)
                if 2 * B <= u + 2 < NU:
                    variances(u + 2)
                for g in range(H // 2):
                    if g == 2 and u >= 1 and (u - 1) // B != 1:
                        cut_mlp_input(u - 1)
                    if g == H // 2 - 1 and u + 3 < NU and norm_at(u)[1] < g:
                        cut_input(u + 3)
                    for i in range(3):
                        if u + 1 < NU:
                            for h in scores_at(u, g, i):
                                maxima(u + 1, h)
                        if g == 1 and i == 1 and 2 * B <= u + 2 < NU:
                            inverse_deviations(u + 2)
                        if i == 0 and u + 3 < NU and norm_at(u)[1] < H // 2 and g == NORMALISE_AT:
                            normalise(ln_no(1, u + 3), (u + 3) % B)
                        if row is not None and (i == 2 or i == 0 and u < NU and rotation_jobs(u, g)[0]):
                            update_rows(row)
                            row = None
                        if i == 0 and u < NU:
                            for name in rotation_jobs(u, g)[0]:
                                if name in V_JOBS:
                                    skew_vectors(name)
                                else:
                                    rotation(name)
                                if name[0] == "qr":
                                    row = name[1]
                        if i == 1 and u >= 1:
                            for e in mlp_at(u - 1, g)[1]:
                                mixture(u - 1, e)
                    if row is not None:
                        update_rows(row)
                        row = None
                    if g == SPREAD_AT and 2 * B <= u + 2 < NU:
                        second_parts(u + 2)
                    if (u, g) in CUT_AT:
                        cut_weights(CUT_AT[u, g])
                    if g == 2 and u == B:
                        dve.wait_ge(w_in[2], W_IN[2])
                        centre(Wqkv[:, 2, 0:2 * C], gm)
                    if g == 1 and u >= 1 and (u - 1) // B == 1:
                        cut_mlp_input(u - 1)
                        mlp_gates(u - 1)
                    if g in DIVIDE_AT and u < NU:
                        divide(u, DIVIDE_AT[g])
                    if u < NU:
                        for name in rotation_jobs(u, g)[1]:
                            if name in V_JOBS:
                                skew_vectors(name)
                            else:
                                rotation(name)
                            if name[0] == "qr":
                                row = name[1]
                    if u + 3 < NU and g == norm_at(u)[0]:
                        norm_1(u + 3)
                if u < NU:
                    divide(u, HG - 1)
                if u + 3 < NU and norm_at(u)[1] == H // 2:
                    normalise(ln_no(1, u + 3), (u + 3) % B)
                if u < NU and norm_at(u)[1] == H // 2:
                    residual(u)
                if u + 3 < NU and norm_at(u)[1] == H // 2:
                    cut_input(u + 3)
                if u + 3 < 2 * B:
                    second_parts(u + 3)
                if u < NU and norm_at(u)[1] < H // 2:
                    residual(u)
            dve.wait_ge(x_new, 2 * NU)
            rotate(B - 1)

        @block.tensor
        def _(pe):
            mm = nc.tensor.matmul
            issued = {"d": 0, "a": 0}

            def d_take(name):
                n = d_no[name]
                assert n == issued["d"], (name, n, issued["d"], d_order[issued["d"]])
                issued["d"] += 1
                if n >= ND:
                    pe.wait_ge(d_free[n % ND], n // ND)
                return D_ring[n % ND]

            def d_give(ins, name):
                return ins.then_inc(d_full[d_no[name] % ND], 1)

            def a_take(name):
                n = a_no[name]
                assert n == issued["a"]
                issued["a"] += 1
                if n >= NA:
                    pe.wait_ge(a_free[n % NA], n // NA)
                return A_ring[n % NA]

            def a_give(ins, name):
                return ins.then_inc(a_full[a_no[name] % NA], 1)

            pe.wait_ge(ada_in, 16 * 9)
            pe.wait_ge(silu_done, 2)

            def modulation(L):
                name = ("ada", L)
                d = d_take(name)
                for s in (0, 1, 3, 4):
                    for lo, rows, col in ((0, P, 0), (P, CR, 6 * B)):
                        o = d[0:rows, col + s * B:col + (s + 1) * B]
                        mm(o, Wada[:, L, s * C + lo:s * C + lo + rows], sT[:, :], start=True, stop=False)
                        last = mm(o, Wadar[:, L, s * C + lo:s * C + lo + rows], sTr[:, :], start=False, stop=True)
                d_give(last, name)

                name = ("rep", L)
                d = d_take(name)
                if L == 0:
                    pe.wait_ge(consts, CONSTS)
                    pe.wait_ge(six_done, 1)
                used(pe, ("ada", L))
                d_give(mm(d[0:SR, 0:6 * B], six[:, :], short[:, :, :].rearrange("p s b -> p (s b)"),
                          start=True, stop=True), name)

            def gate_rows(L, b):
                name = ("gate", L, b)
                d = d_take(name)
                for k, s in enumerate((2, 5)):
                    o = d[:, k * C:(k + 1) * C]
                    mm(o, sTb[:, b, :], Wada[:, L, s * C:(s + 1) * C], start=True, stop=False)
                    last = mm(o, sTrb[:, b, :], Wadar[:, L, s * C:(s + 1) * C], start=False, stop=True)
                d_give(last, name)

            def transposed(name, src, ready, value):
                d = d_take(name)
                pe.wait_ge(ready, value)
                more = src.shape[2] - P
                for k in range(NT):
                    nc.tensor.transpose(d[:, k * P:(k + 1) * P], src[:, k, 0:P], ident[:, :])
                    last = nc.tensor.transpose(d[0:more, T + k * P:T + (k + 1) * P], src[:, k, P:P + more],
                                               ident[:, :])
                d_give(last, name)

            def input_transposed(u):
                transposed(("t1", u), xh, xh_ready, NT * (LN_ORDER.index((1, u)) + 1))

            def qk_of(u):
                L = u // B
                if u % B == 0:
                    pe.wait_ge(w_in[L], W_IN[L])
                if u == 2 * B:
                    pe.wait_ge(centred, 2)
                used(pe, ("t1", u))
                c = CH[L]
                for j, (lo, hi) in enumerate(QKJ[L]):
                    name = ("qk", u, j)
                    d = d_take(name)
                    for k in range(lo, hi):
                        mm(d[0:c, (k - lo) * T:(k - lo + 1) * T], Wqkv[:, L, k * c:(k + 1) * c], hT[:, :],
                           start=True, stop=False)
                        if j == 0 and k == lo:
                            pe.wait_ge(hs_done, u + 1)
                            pe.wait_ge(w_cut, CUTS.index((L, None)) + 1)
                        last = mm(d[0:c, (k - lo) * T:(k - lo + 1) * T], WqkvS[:, L, k * c:(k + 1) * c], hS[:, :],
                                  start=False, stop=True)
                    d_give(last, name)

            def v_of(u):
                L = u // B
                name = ("v", u)
                d = d_take(name)
                for k in range(NT):
                    o = d[:, k * C:(k + 1) * C]
                    mm(o, hT[:, k * P:(k + 1) * P], Wqkv[:, L, 2 * C:3 * C], start=True, stop=False)
                    last = mm(o, hS[:, k * P:(k + 1) * P], WqkvS[:, L, 2 * C:3 * C], start=False, stop=True)
                d_give(last, name)
                if L == 2:
                    name = ("var", u)
                    d = d_take(name)
                    for k in range(4):
                        pe.wait_ge(sq_done, 2 * (u - 2 * B) + k // 2 + 1)
                        last = mm(d[32 * k:32 * k + 32, 0:T], pick[:, :], qsq[:, k, :], start=True, stop=True)
                    d_give(last, name)

            def deviations(u):
                for j, (lo, hi) in enumerate(QKJ[u // B]):
                    name = ("rs", u, j)
                    d = d_take(name)
                    pe.wait_ge(qrs_done, u - 2 * B + 1)
                    for k in range(lo, hi):
                        last = mm(d[0:CH[2], (k - lo) * T:(k - lo + 1) * T],
                                  spread[:, k, :, :].rearrange("p k r -> p (k r)"), qrs[:, :],
                                  start=True, stop=True)
                    d_give(last, name)

            def scores(u, h):
                i = u % 2
                if h == 0:
                    pe.wait_ge(stk_in[i], 16 * STACKS * (u // 2 + 1))
                name = ("s", u, h)
                d = d_take(name)
                for k in range(NT):
                    last = mm(d[:, k * T:(k + 1) * T], QS[i][0:KS_ROWS, h, k * P:(k + 1) * P],
                              KS[i][0:KS_ROWS, h, :], start=True, stop=True)
                d_give(last, name)

            def maxima(u):
                name = ("nm", u)
                d = d_take(name)
                used(pe, ("s", u, H - 1))
                db = d[:, :].bitcast(BF16)
                for k in range(NT):
                    last = nc.tensor.transpose(db[0:H, k * P:(k + 1) * P], nm[u % 2][:, k, :], identb[:, :])
                d_give(last, name)

            def weights(u, g):
                i = u % 2
                if g == 0:
                    pe.wait_ge(nm_in[i], 16 * (u // 2 + 1))
                name = ("e", u, g)
                a = a_take(name)
                for hh in range(2):
                    for k in range(NT):
                        last = mm(a[:, 2 * hh + k, :], KS[i][:, 2 * g + hh, k * P:(k + 1) * P],
                                  QS[i][:, 2 * g + hh, :], start=True, stop=True)
                a_give(last, name)

            def values(u, q):
                n = HG * u + q
                used(pe, ("e", u, 2 * q + 1))
                if q == 0:
                    used(pe, ("v", u))
                if n >= 1:
                    pe.wait_ge(o_read, n)
                for k in range(NT):
                    for j in range(4):
                        last = mm(O[32 * j:32 * j + HD + 1, :], V[u % 3][:, k, 4 * q + j, :],
                                  PT[:, (2 * n + j // 2) % NPT, 2 * (j % 2) + k, :], start=k == 0, stop=k == NT - 1)
                last.then_inc(pv_step, 1)

            def skew_vectors(name):
                if name == ("wt", 0):
                    pe.wait_ge(l3_in, 32)
                if name[0] == "pt":
                    pe.wait_ge(pt_in, 32)
                if name[0] == "vv":
                    used(pe, ("wt", 7))
                d = d_take(name)
                if name[0] == "wt":
                    q = name[1] // 2
                    lo, rows = ((0, P), (P, CR))[name[1] % 2]
                    for j in range(4):
                        last = nc.tensor.transpose(d[0:rows, 126 * j:126 * j + 126], Wl[:, 4 * q + j, lo:lo + rows],
                                                   ident[0:126, 0:126])
                elif name[0] == "vv":
                    cols = slice(504 * name[1], 504 * name[1] + 504)
                    mm(d[0:B, 0:504], sT[:, :], WT[:, cols], start=True, stop=False)
                    last = mm(d[0:B, 0:504], sTr[:, :], WTr[:, cols], start=False, stop=True)
                else:
                    nc.tensor.transpose(d[0:DR, 0:P], Pn[:, :], ident[:, :])
                    last = nc.tensor.transpose(d[0:DR, P:C], Pnr[:, :], ident[0:CR, 0:CR])
                d_give(last, name)

            def rotation(name):
                kind = name[0]
                if name in V_JOBS:
                    skew_vectors(name)
                    return
                if kind == "qr":
                    if name[1] == 0:
                        used(pe, ("pt",))
                    else:
                        pe.wait_ge(qr_done, name[1])
                elif kind == "ut":
                    pe.wait_ge(up_in, 16 * (DR - 1))
                elif kind == "fro":
                    pe.wait_ge(fr_done, 1)
                elif kind == "tay":
                    if name[1] == 0:
                        pe.wait_ge(E_done, 1)
                    else:
                        used(pe, ("tay", name[1] - 1))
                elif kind == "ft":
                    used(pe, ("tay", TAYLOR - 2))
                elif kind == "sq":
                    used(pe, ("sq", name[1] - 1) if name[1] else ("ft",))
                elif kind == "vqt":
                    pe.wait_ge(qr_done, DR + 1)
                elif kind == "vvt":
                    used(pe, ("vqt",))
                elif kind == "nn":
                    if name[1]:
                        used(pe, ("nn", name[1] - 1))
                    else:
                        pe.wait_ge(tri_done, 2)
                elif kind == "tn":
                    used(pe, ("nn", name[1]))
                    if name[1]:
                        used(pe, ("tn", name[1] - 1))
                    else:
                        pe.wait_ge(N_done, 1)
                elif kind == "kk":
                    used(pe, ("tn", 4))
                elif kind == "uu":
                    used(pe, ("kk",))
                elif kind == "gm":
                    used(pe, ("uu",))
                    pe.wait_ge(F_done, 1)
                elif kind == "m":
                    used(pe, ("gm", name[1] // 2))
                d = d_take(name)
                dd = d[0:DR, :]
                if kind == "qr":
                    j = name[1]
                    last = mm(dd[:, j:C], ident[0:DR, j:j + 1].to_broadcast([DR, DR]), Pt[:, j:C],
                              start=True, stop=True)
                elif kind == "ut":
                    for b in range(B):
                        last = nc.tensor.transpose(dd[:, b * DR:(b + 1) * DR], Up[:, b, :], ident[0:DR, 0:DR])
                elif kind == "fro":
                    last = mm(dd[:, 0:B], ones[:, :], fr[:, :], start=True, stop=True)
                elif kind == "tay":
                    for b in range(B):
                        last = mm(dd[:, b * DR:(b + 1) * DR], X[:, b, :], E0[:, b, :], start=True, stop=True)
                elif kind == "ft":
                    for b in range(B):
                        last = nc.tensor.transpose(dd[:, b * DR:(b + 1) * DR], Z[:, b, :], ident[0:DR, 0:DR])
                elif kind == "sq":
                    for b in range(2 * B):
                        last = mm(dd[:, b * DR:(b + 1) * DR], Z[:, (b + B) % (2 * B), :], Z[:, b, :],
                                  start=True, stop=True)
                elif kind == "vqt":
                    nc.tensor.transpose(d[:, 0:DR], Vq[:, 0:P], ident[0:DR, 0:DR])
                    last = nc.tensor.transpose(d[0:CR, DR:2 * DR], Vq[:, P:C], ident[0:DR, 0:DR])
                elif kind == "vvt":
                    mm(dd[:, 0:DR], VqT[:, :], VqT[:, :], start=True, stop=False)
                    last = mm(dd[:, 0:DR], VqTr[:, :], VqTr[:, :], start=False, stop=True)
                elif kind == "nn":
                    mm(dd[:, 0:DR], Nn[:, 1, :], Nn[:, 0, :], start=True, stop=True)
                    last = mm(dd[:, DR:2 * DR], Nn[:, 0, :], Nn[:, 1, :], start=True, stop=True)
                elif kind == "tn":
                    last = mm(dd[:, 0:DR], Nn[:, 1, :], Tn[:, :], start=True, stop=True)
                elif kind == "kk":
                    last = mm(dd[:, 0:C], Tn[:, :], Vq[:, :], start=True, stop=True)
                elif kind == "uu":
                    last = mm(dd[:, 0:C], Vq[:, 0:DR], Kq[:, :], start=True, stop=True)
                elif kind == "gm":
                    for j in range(2):
                        last = mm(dd[:, j * C:(j + 1) * C], FmI[:, 2 * name[1] + j, :], Ut[:, :],
                                  start=True, stop=True)
                elif kind == "m":
                    mm(d[:, 0:C], Ut[:, 0:P], Gm[:, name[1], :], start=True, stop=True)
                    last = mm(d[0:CR, C:2 * C], Ut[:, P:C], Gm[:, name[1], :], start=True, stop=True)
                d_give(last, name)

            def rotate(b):
                transposed(("t4", b), x[:, b, :, :], x_new, 2 * (NU - B + b) + 2)
                name = ("y", b)
                d = d_take(name)
                used(pe, ("t4", b))
                used(pe, ("m", b))
                for k in range(NT):
                    o = d[:, k * C:(k + 1) * C]
                    mm(o, xT[:, k * P:(k + 1) * P], M[:, b, :], start=True, stop=False)
                    last = mm(o, xTr[:, k * P:(k + 1) * P], Mr[:, b, :], start=False, stop=True)
                d_give(last, name)

            def mlp_input(u):
                L = u // B
                transposed(("t3", u), xh, xh_ready, NT * (LN_ORDER.index((2, u)) + 1))
                if L == 1:
                    used(pe, ("t3", u))
                    pe.wait_ge(m_in[L], M_IN[L])
                    name = ("gl", u)
                    d = d_take(name)
                    for k in range(NT):
                        o = d[:, k * NE:(k + 1) * NE]
                        mm(o, h2T[:, k * P:(k + 1) * P], Wg[:, :], start=True, stop=False)
                        last = mm(o, h2F[0:CR, k * P:(k + 1) * P], Wgr[:, :], start=False, stop=True)
                    d_give(last, name)

            def fc1(u, e, part):
                L = u // B
                lo, hi = ((0, 2), (2, 4), (4, 5))[part]
                name = ("g", u, 2 * e + part // 2)
                if part != 1:
                    a_take(name)
                if part == 0:
                    used(pe, ("t3", u))
                    if u % B == 0:
                        pe.wait_ge(m_in[L], M_IN[L])
                for c in range(lo, hi):
                    rows = P if c < FC else FR
                    o = A(name)[0:rows, c % FC, :]
                    mm(o, W1[L][:, e, c * P:c * P + rows], h2T[:, :], start=True, stop=False)
                    if c == 0 and e == 0:
                        pe.wait_ge(h2s_done, u + 1)
                        if u % B == 0:
                            pe.wait_ge(w_cut, CUTS.index((L, EXPERTS[L] - 1)) + 1)
                    last = mm(o, W1S[L][:, e, c * P:c * P + rows], h2S[:, :], start=False, stop=True)
                if part >= 1:
                    a_give(last, name)

            def fc2(u, e, k):
                L = u // B
                at = experts_before(u) + e
                name = ("fc2", u, e)
                if k == 0:
                    d_take(name)
                    used(pe, ("g", u, 2 * e + 1))
                o = D(name)[:, k * C:(k + 1) * C]
                for c in range(FC + 1):
                    rows = P if c < FC else FR + 1
                    last = mm(o, G[0:rows, at % 2, c, k * P:(k + 1) * P], W2[L][0:rows, e, c, :],
                              start=c == 0, stop=c == FC)
                if k == NT - 1:
                    d_give(last, name)

            def projection(u):
                name = ("proj", u)
                d = d_take(name)
                pe.wait_ge(oT_done, HG * (u + 1))
                for k in range(NT):
                    for q in range(HG):
                        last = mm(d[:, k * C:(k + 1) * C], oT[:, q, k * P:(k + 1) * P], Wp[:, u // B, q, :],
                                  start=q == 0, stop=q == HG - 1)
                d_give(last, name)

            modulation(0)
            for u in range(2):
                input_transposed(u)
                qk_of(u)
                v_of(u)
            for L in (1, 2):
                modulation(L)
            for L in range(NL):
                for b in range(B):
                    gate_rows(L, b)
            for h in range(H):
                scores(0, h)
            maxima(0)
            input_transposed(2)
            qk_of(2)
            for u in range(NU + 1):
                if u == NU:
                    for b in range(B - 1):
                        rotate(b)
                for g in range(H // 2):
                    if u < NU:
                        weights(u, g)
                    if g == 0 and u + 2 < NU:
                        v_of(u + 2)
                    for i in range(3):
                        if u + 1 < NU:
                            for h in scores_at(u, g, i):
                                scores(u + 1, h)
                        if u >= 1:
                            for e in mlp_at(u - 1, g)[0]:
                                fc1(u - 1, e, i)
                            if i < NT:
                                for e in mlp_at(u - 1, g)[1]:
                                    fc2(u - 1, e, i)
                        if i == 0 and u < NU:
                            for name in rotation_jobs(u, g)[0]:
                                rotation(name)
                    if g == SPREAD_AT and 2 * B <= u + 2 < NU:
                        deviations(u + 2)
                    if g == 1 and u >= 1:
                        mlp_input(u - 1)
                    if g in VALUES_AT and u < NU:
                        values(u, VALUES_AT[g])
                    if u < NU:
                        for name in rotation_jobs(u, g)[1]:
                            rotation(name)
                    if g == H // 2 - 1 and u + 1 < NU:
                        maxima(u + 1)
                    if u + 3 < NU and g == norm_at(u)[1]:
                        input_transposed(u + 3)
                if u < NU:
                    values(u, HG - 1)
                if u < NU and norm_at(u)[1] == H // 2:
                    projection(u)
                if u + 3 < NU and norm_at(u)[1] == H // 2:
                    input_transposed(u + 3)
                if u + 3 < NU:
                    qk_of(u + 3)
                if u < NU and norm_at(u)[1] < H // 2:
                    projection(u)
            rotate(B - 1)


def build(nc, aps, out):
    t = {"x": aps["x"], "cond": aps["cond_1152"]}
    t["ada"] = [aps["L0_cond_W_ada"], aps["L1_cond_w_adaln"], aps["L2_cond_w_mod"]]
    t["b_ada"] = [aps["L0_cond_b_ada"], aps["L1_cond_b_adaln"], aps["L2_cond_b_mod"]]
    t["qkv"] = [aps["L0_cond_W_qkv"], aps["L1_cond_w_qkv"], aps["L2_cond_w_qkv"]]
    t["b_qkv"] = [aps[f"L{L}_cond_b_qkv"] for L in range(3)]
    t["proj"] = [aps["L0_cond_W_proj"], aps["L1_cond_w_proj"], aps["L2_cond_w_proj"]]
    t["b_proj"] = [aps[f"L{L}_cond_b_proj"] for L in range(3)]
    t["w1"] = [[aps["L0_cond_W_fc1"]], [aps["L1_cond_w1"][e] for e in range(4)], [aps["L2_cond_w1"]]]
    t["b1"] = [[aps["L0_cond_b_fc1"]], [aps["L1_cond_b1"][e] for e in range(4)], [aps["L2_cond_b1"]]]
    t["w2"] = [[aps["L0_cond_W_fc2"]], [aps["L1_cond_w2"][e] for e in range(4)], [aps["L2_cond_w2"]]]
    t["b2"] = [[aps["L0_cond_b_fc2"]], [aps["L1_cond_b2"][e] for e in range(4)], [aps["L2_cond_b2"]]]
    t["w_gate"] = aps["L1_cond_w_gate"]
    t["g_q"], t["g_k"] = aps["L2_cond_g_q"], aps["L2_cond_g_k"]
    t["rot_p"], t["rot_w"], t["rot_b"] = aps["L3_cond_P"], aps["L3_cond_W"], aps["L3_cond_b"]
    cond_sequence_kernel(nc, t, out)


def kernel(**inputs):
    import numpy as _np
    import concourse.bacc as _bacc
    from concourse import mybir as _mybir
    from concourse.bass_utils import run_bass_kernel_spmd as _run

    nc = _bacc.Bacc("TRN2", target_bir_lowering=False, num_devices=1)
    arrays, aps = {}, {}
    for name, value in inputs.items():
        a = _np.ascontiguousarray(value)
        arrays[f"in_{name}_dram"] = a
        aps[name] = nc.dram_tensor(f"in_{name}_dram", a.shape, _mybir.dt.from_np(a.dtype), kind="ExternalInput").ap()
    out = nc.dram_tensor("out_0_dram", (4, 256, 144), _mybir.dt.float32, kind="ExternalOutput").ap()
    build(nc, aps, out)
    r = _run(nc, [arrays], core_ids=[0])
    return r.results[0]["out_0_dram"]
```
